# Optimizing a Trainium2 kernel written in Bass

```python
import numpy as np
import jax
import jax.numpy as jnp

def _softmax(x, axis=-1):
    return jax.nn.softmax(x, axis=axis)

def _gelu(x):
    return jax.nn.gelu(x, approximate=True)

def _silu(x):
    return jax.nn.silu(x)

def _sigmoid(x):
    return jax.nn.sigmoid(x)

def _layernorm(x, axis=-1, eps=1e-05):
    m = jnp.mean(x, axis=axis, keepdims=True)
    v = jnp.var(x, axis=axis, keepdims=True)
    return (x - m) / jnp.sqrt(v + eps)

def _scatter_add(tgt, idx, src, axis=0):
    return tgt.at[idx].add(src)

def _segment_sum(src, seg, n):
    return jax.ops.segment_sum(src, seg, n)
kernel_name = 'mk_seq_postln_d2_jaxref_r8_a54be9'

def setup_inputs(seed: int=0):
    np.random.seed(seed)
    _w = jnp.asarray

    def _L0_attn_setup():
        import jax, jax.numpy as jnp
        import numpy as np
        HIDDEN = 512
        HEAD_DIM = 128
        N_Q_HEADS = 32
        N_KV_HEADS = 8
        SLIDING_WINDOW = 128
        ROPE_THETA = 10000.0
        BATCH, SEQ = (1, 256)

        def _rope(t, pos):
            d = t.shape[-1]
            half = d // 2
            inv_freq = ROPE_THETA ** (-jnp.arange(half, dtype=jnp.float32) / half)
            ang = pos[:, None].astype(jnp.float32) * inv_freq[None, :]
            cos = jnp.cos(ang)[None, :, None, :]
            sin = jnp.sin(ang)[None, :, None, :]
            t1, t2 = (t[..., :half], t[..., half:])
            return jnp.concatenate([t1 * cos - t2 * sin, t1 * sin + t2 * cos], axis=-1)
        key = jax.random.key(seed)
        ks = jax.random.split(key, 5)
        w_scale = HIDDEN ** (-0.5)
        return {'x': jax.random.normal(ks[0], (BATCH, SEQ, HIDDEN), jnp.float32), 'wq': jax.random.normal(ks[1], (HIDDEN, N_Q_HEADS * HEAD_DIM), jnp.float32) * w_scale, 'wk': jax.random.normal(ks[2], (HIDDEN, N_KV_HEADS * HEAD_DIM), jnp.float32) * w_scale, 'wv': jax.random.normal(ks[3], (HIDDEN, N_KV_HEADS * HEAD_DIM), jnp.float32) * w_scale, 'wo': jax.random.normal(ks[4], (N_Q_HEADS * HEAD_DIM, HIDDEN), jnp.float32) * w_scale}
    _L0_attn_in = _L0_attn_setup()

    def _L0_ffn_setup():
        import jax, jax.numpy as jnp
        import numpy as np
        D = 512
        F = 1376
        B, S = (4, 256)
        key = jax.random.key(seed)
        k_x, k_g, k_u, k_d = jax.random.split(key, 4)
        scale = 0.02
        return {'x': jax.random.normal(k_x, (B, S, D), dtype=jnp.float32), 'W_gate': jax.random.normal(k_g, (F, D), dtype=jnp.float32) * scale, 'W_up': jax.random.normal(k_u, (F, D), dtype=jnp.float32) * scale, 'W_down': jax.random.normal(k_d, (D, F), dtype=jnp.float32) * scale}
    _L0_ffn_in = _L0_ffn_setup()

    def _L1_attn_setup():
        import jax, jax.numpy as jnp
        import numpy as np
        import math
        B, T, D_IN, D_OUT = (2, 256, 512, 512)
        N_HEADS, N_KV = (32, 8)
        HEAD_DIM = D_OUT // N_HEADS
        GROUP_SIZE = N_HEADS // N_KV
        ROPE_BASE = 500000.0
        CTX = 256

        def _rope_tables(head_dim, base, seq_len):
            inv_freq = 1.0 / base ** (jnp.arange(0, head_dim, 2, dtype=jnp.float32) / head_dim)
            t = jnp.arange(seq_len, dtype=jnp.float32)
            freqs = jnp.einsum('i,j->ij', t, inv_freq)
            return (jnp.cos(freqs), jnp.sin(freqs))

        def _apply_rope(x, cos, sin):
            x1, x2 = jnp.split(x, 2, axis=-1)
            c = cos[None, None]
            s = sin[None, None]
            return jnp.concatenate([x1 * c - x2 * s, x1 * s + x2 * c], axis=-1)
        key = jax.random.key(seed)
        ks = jax.random.split(key, 5)
        scale = 0.02
        return {'x': jax.random.normal(ks[0], (B, T, D_IN), dtype=jnp.float32), 'Wq': jax.random.normal(ks[1], (D_IN, D_OUT), dtype=jnp.float32) * scale, 'Wk': jax.random.normal(ks[2], (D_IN, N_KV * HEAD_DIM), dtype=jnp.float32) * scale, 'Wv': jax.random.normal(ks[3], (D_IN, N_KV * HEAD_DIM), dtype=jnp.float32) * scale, 'Wo': jax.random.normal(ks[4], (D_OUT, D_OUT), dtype=jnp.float32) * scale}
    _L1_attn_in = _L1_attn_setup()

    def _L1_ffn_setup():
        import jax, jax.numpy as jnp
        import numpy as np
        B, S, IN, OUT = (4, 256, 512, 512)
        E, K, R = (8, 2, 16)
        CAP_FACTOR = 3.0
        ALPHA = 1.0 / R
        LN_EPS = 1e-05
        key = jax.random.key(seed)
        ks = jax.random.split(key, 6)
        return {'x': jax.random.normal(ks[0], (B, S, IN), dtype=jnp.float32), 'weight': jax.random.normal(ks[1], (OUT, IN), dtype=jnp.float32) * 0.02, 'lora_A': jax.random.normal(ks[2], (E, IN, R), dtype=jnp.float32) / np.sqrt(R), 'lora_B': jax.random.normal(ks[3], (E, R, OUT), dtype=jnp.float32) * 0.02, 'gw1': jax.random.normal(ks[4], (4 * E, IN), dtype=jnp.float32) * 0.02, 'gb1': jnp.zeros((4 * E,), dtype=jnp.float32), 'ln_gamma': jnp.ones((4 * E,), dtype=jnp.float32), 'ln_beta': jnp.zeros((4 * E,), dtype=jnp.float32), 'gw2': jax.random.normal(ks[5], (E, 4 * E), dtype=jnp.float32) * 0.02, 'gb2': jnp.zeros((E,), dtype=jnp.float32)}
    _L1_ffn_in = _L1_ffn_setup()
    _d = {'L0_attn_x': _L0_attn_in['x'], 'L0_attn_wq': _L0_attn_in['wq'], 'L0_attn_wk': _L0_attn_in['wk'], 'L0_attn_wv': _L0_attn_in['wv'], 'L0_attn_wo': _L0_attn_in['wo'], 'L0_ffn_W_gate': _L0_ffn_in['W_gate'], 'L0_ffn_W_up': _L0_ffn_in['W_up'], 'L0_ffn_W_down': _L0_ffn_in['W_down'], 'L1_attn_Wq': _L1_attn_in['Wq'], 'L1_attn_Wk': _L1_attn_in['Wk'], 'L1_attn_Wv': _L1_attn_in['Wv'], 'L1_attn_Wo': _L1_attn_in['Wo'], 'L1_ffn_weight': _L1_ffn_in['weight'], 'L1_ffn_lora_A': _L1_ffn_in['lora_A'], 'L1_ffn_lora_B': _L1_ffn_in['lora_B'], 'L1_ffn_gw1': _L1_ffn_in['gw1'], 'L1_ffn_gb1': _L1_ffn_in['gb1'], 'L1_ffn_ln_gamma': _L1_ffn_in['ln_gamma'], 'L1_ffn_ln_beta': _L1_ffn_in['ln_beta'], 'L1_ffn_gw2': _L1_ffn_in['gw2'], 'L1_ffn_gb2': _L1_ffn_in['gb2']}
    _x0 = _d['L0_attn_x']
    _d['L0_attn_x'] = jax.random.normal(jax.random.fold_in(jax.random.key(seed), 1), (2, 512, 512), dtype=_x0.dtype)
    del _x0
    return _d

def reference(L0_attn_x, L0_attn_wq, L0_attn_wk, L0_attn_wv, L0_attn_wo, L0_ffn_W_gate, L0_ffn_W_up, L0_ffn_W_down, L1_attn_Wq, L1_attn_Wk, L1_attn_Wv, L1_attn_Wo, L1_ffn_weight, L1_ffn_lora_A, L1_ffn_lora_B, L1_ffn_gw1, L1_ffn_gb1, L1_ffn_ln_gamma, L1_ffn_ln_beta, L1_ffn_gw2, L1_ffn_gb2):

    def _L0_attn_ref(x, wq, wk, wv, wo):
        import jax, jax.numpy as jnp
        import numpy as np
        HIDDEN = 512
        HEAD_DIM = 128
        N_Q_HEADS = 32
        N_KV_HEADS = 8
        SLIDING_WINDOW = 128
        ROPE_THETA = 10000.0
        BATCH, SEQ = (1, 256)

        def _rope(t, pos):
            d = t.shape[-1]
            half = d // 2
            inv_freq = ROPE_THETA ** (-jnp.arange(half, dtype=jnp.float32) / half)
            ang = pos[:, None].astype(jnp.float32) * inv_freq[None, :]
            cos = jnp.cos(ang)[None, :, None, :]
            sin = jnp.sin(ang)[None, :, None, :]
            t1, t2 = (t[..., :half], t[..., half:])
            return jnp.concatenate([t1 * cos - t2 * sin, t1 * sin + t2 * cos], axis=-1)
        B, S, _ = x.shape
        G = N_Q_HEADS // N_KV_HEADS
        sm_scale = HEAD_DIM ** (-0.5)
        q = (x @ wq).reshape(B, S, N_Q_HEADS, HEAD_DIM)
        k = (x @ wk).reshape(B, S, N_KV_HEADS, HEAD_DIM)
        v = (x @ wv).reshape(B, S, N_KV_HEADS, HEAD_DIM)
        pos = jnp.arange(S)
        q = _rope(q, pos)
        k = _rope(k, pos)
        qg = q.reshape(B, S, N_KV_HEADS, G, HEAD_DIM)
        scores = jnp.einsum('bqhgd,bshd->bhgqs', qg, k) * sm_scale
        i = pos[:, None]
        j = pos[None, :]
        allowed = (j <= i) & (j > i - SLIDING_WINDOW)
        neg = jnp.finfo(scores.dtype).min
        scores = jnp.where(allowed[None, None, None], scores, neg)
        attn = jax.nn.softmax(scores, axis=-1)
        out = jnp.einsum('bhgqs,bshd->bqhgd', attn, v).reshape(B, S, N_Q_HEADS * HEAD_DIM)
        return out @ wo

    def _L0_ffn_ref(x, W_gate, W_up, W_down):
        import jax, jax.numpy as jnp
        import numpy as np
        D = 512
        F = 1376
        B, S = (4, 256)
        out_shape = x.shape[:-1] + (W_down.shape[0],)
        xt = x.reshape(-1, x.shape[-1])
        up = xt @ W_up.T
        gate = jax.nn.silu(xt @ W_gate.T)
        y = gate * up @ W_down.T
        return y.reshape(out_shape)

    def _L1_attn_ref(x, Wq, Wk, Wv, Wo):
        import jax, jax.numpy as jnp
        import numpy as np
        import math
        B, T, D_IN, D_OUT = (2, 256, 512, 512)
        N_HEADS, N_KV = (32, 8)
        HEAD_DIM = D_OUT // N_HEADS
        GROUP_SIZE = N_HEADS // N_KV
        ROPE_BASE = 500000.0
        CTX = 256

        def _rope_tables(head_dim, base, seq_len):
            inv_freq = 1.0 / base ** (jnp.arange(0, head_dim, 2, dtype=jnp.float32) / head_dim)
            t = jnp.arange(seq_len, dtype=jnp.float32)
            freqs = jnp.einsum('i,j->ij', t, inv_freq)
            return (jnp.cos(freqs), jnp.sin(freqs))

        def _apply_rope(x, cos, sin):
            x1, x2 = jnp.split(x, 2, axis=-1)
            c = cos[None, None]
            s = sin[None, None]
            return jnp.concatenate([x1 * c - x2 * s, x1 * s + x2 * c], axis=-1)
        b, t, _ = x.shape
        cos, sin = _rope_tables(HEAD_DIM, ROPE_BASE, t)
        q = (x @ Wq).reshape(b, t, N_HEADS, HEAD_DIM).transpose(0, 2, 1, 3)
        k = (x @ Wk).reshape(b, t, N_KV, HEAD_DIM).transpose(0, 2, 1, 3)
        v = (x @ Wv).reshape(b, t, N_KV, HEAD_DIM).transpose(0, 2, 1, 3)
        q = _apply_rope(q, cos, sin)
        k = _apply_rope(k, cos, sin)
        k_h = jnp.repeat(k, GROUP_SIZE, axis=1)
        v_h = jnp.repeat(v, GROUP_SIZE, axis=1)
        scores = jnp.einsum('bhqd,bhkd->bhqk', q, k_h) / math.sqrt(HEAD_DIM)
        causal = jnp.triu(jnp.ones((t, t), dtype=bool), k=1)
        scores = jnp.where(causal[None, None], jnp.finfo(scores.dtype).min, scores)
        attn = jax.nn.softmax(scores, axis=-1)
        ctx = jnp.einsum('bhqk,bhkd->bhqd', attn, v_h)
        ctx = ctx.transpose(0, 2, 1, 3).reshape(b, t, D_OUT)
        return ctx @ Wo

    def _L1_ffn_ref(x, weight, lora_A, lora_B, gw1, gb1, ln_gamma, ln_beta, gw2, gb2):
        import jax, jax.numpy as jnp
        import numpy as np
        B, S, IN, OUT = (4, 256, 512, 512)
        E, K, R = (8, 2, 16)
        CAP_FACTOR = 3.0
        ALPHA = 1.0 / R
        LN_EPS = 1e-05
        orig_shape = x.shape
        xf = x.reshape(-1, orig_shape[-1])
        N = xf.shape[0]
        capacity = int(CAP_FACTOR * N / E)
        h = xf @ gw1.T + gb1
        mu = jnp.mean(h, axis=-1, keepdims=True)
        var = jnp.mean((h - mu) ** 2, axis=-1, keepdims=True)
        h = (h - mu) * jax.lax.rsqrt(var + LN_EPS) * ln_gamma + ln_beta
        h = jax.nn.relu(h)
        gates = h @ gw2.T + gb2
        top_v, top_i = jax.lax.top_k(gates, K)
        top_g = jax.nn.softmax(top_v, axis=-1)
        onehot = (top_i[..., None] == jnp.arange(E)).astype(xf.dtype)
        counts = onehot.sum(axis=0)
        allowed = (counts <= capacity).astype(xf.dtype)
        w = jnp.einsum('nke,nk,ke->ne', onehot, top_g, allowed)
        main = xf @ weight.T
        tmp = jnp.einsum('ni,eir->enr', xf, lora_A)
        tmp = tmp * w.T[:, :, None]
        lora = jnp.einsum('enr,ero->no', tmp, lora_B) * ALPHA
        out = main + lora
        return out.reshape(*orig_shape[:-1], weight.shape[0])
    x = L0_attn_x
    x = _layernorm(x + _L0_attn_ref(x, L0_attn_wq, L0_attn_wk, L0_attn_wv, L0_attn_wo), axis=-1)
    x = _layernorm(x + _L0_ffn_ref(x, L0_ffn_W_gate, L0_ffn_W_up, L0_ffn_W_down), axis=-1)
    x = _layernorm(x + _L1_attn_ref(x, L1_attn_Wq, L1_attn_Wk, L1_attn_Wv, L1_attn_Wo), axis=-1)
    x = _layernorm(x + _L1_ffn_ref(x, L1_ffn_weight, L1_ffn_lora_A, L1_ffn_lora_B, L1_ffn_gw1, L1_ffn_gb1, L1_ffn_ln_gamma, L1_ffn_ln_beta, L1_ffn_gw2, L1_ffn_gb2), axis=-1)
    return x

_drawn_inputs = setup_inputs


def setup_inputs(seed=0):
    import zlib

    import numpy as np

    out = dict(_drawn_inputs(seed))
    spreads = {'L1_ffn_gb1': (0.0, 0.8),
     'L1_ffn_ln_gamma': (1.0, 0.6),
     'L1_ffn_ln_beta': (0.0, 0.8),
     'L1_ffn_gb2': (0.0, 0.507)}
    factors = {'L1_attn_Wq': 8.0,
     'L1_attn_Wk': 8.0,
     'L1_ffn_lora_A': 4.883,
     'L1_ffn_lora_B': 4.904,
     'L1_ffn_gw1': 5.648,
     'L1_ffn_gw2': 5.335}
    for name, (base, spread) in spreads.items():
        noise = np.random.default_rng([zlib.crc32(name.encode()), seed]).standard_normal(out[name].shape)
        drawn = base * np.exp(spread * noise) if base else spread * noise
        out[name] = jnp.asarray(drawn.astype(out[name].dtype))
    for name, factor in factors.items():
        out[name] = (out[name] * factor).astype(out[name].dtype)
    return out
```

```python
from contextlib import ExitStack

import numpy as np

import concourse.bass as bass
from concourse import mybir
from concourse.alu_op_type import AluOpType as ALU

F32 = mybir.dt.float32
F32R = mybir.dt.float32r
ACT = mybir.ActivationFunctionType

P = 128
BATCH, SEQ, D = 2, 512, 512
TOK = BATCH * SEQ
TILES = TOK // P
SEQ_TILES = SEQ // P
KC = D // P
EPS = 1e-5
MASKED = -1e30
LOWEST = -3e38

HEADS0, KV0, HD0 = 32, 8, 128
GROUP0 = HEADS0 // KV0
SCALE0 = HD0 ** -0.5
PAIRS = KV0 // 2
WEIGHT_ORDER = [
    (1, "k", 1, 0), (1, "q", 1, 0), (2, "q", 1, 1), (2, "q", 1, 2), (3, "q", 1, 3),
    (3, "o", 1, 0), (4, "o", 1, 1), (4, "o", 1, 2), (5, "o", 1, 3),
    (6, "v", 0, 0), (7, "v", 1, 0), (9, "k", 0, 0), (9, "q", 0, 0), (10, "q", 0, 1), (10, "q", 0, 2),
    (11, "q", 0, 3), (12, "o", 0, 0), (13, "o", 0, 1), (14, "o", 0, 2), (15, "o", 0, 3),
]
PER_PAIR = len(WEIGHT_ORDER)
FIRST_OF_NEXT = 9
HEAD_START = PER_PAIR - FIRST_OF_NEXT
WEIGHT_AT = {w[1:]: n for n, w in enumerate(WEIGHT_ORDER)}
SLOTS = 16
PIECES = {0: ["k", 0], 1: [1, 2], 2: [3], 3: []}


def weights_done(pair, kind, g, h=0):
    n = WEIGHT_AT[(kind, g, h)]
    if n >= FIRST_OF_NEXT:
        return pair * PER_PAIR + n - FIRST_OF_NEXT + 1
    return pair * PER_PAIR + HEAD_START + n + 1


def piece_index(unit, piece):
    return 5 * unit + (0 if piece == "k" else piece + 1)


def key_tiles(qt):
    return (0, 1) if qt == 0 else (qt - 1, 2)


def blocks_before(s):
    return (s // 4) * 7 + (0, 1, 3, 5)[s % 4]


def three(pe, out, terms, done):
    steps = [(a, b) for a_hi, a_lo, b_hi, b_lo in terms for a, b in ((a_hi, b_hi), (a_hi, b_lo), (a_lo, b_hi))]
    for n, (a, b) in enumerate(steps):
        mm = pe.matmul(out, a, b, start=(n == 0), stop=(n == len(steps) - 1))
    mm.then_inc(done, 1)


def attention0(nc, t, x_T, weight_stream, x_rows, cos_T, sin_T, masks, ident_in, psum):
    ctx = ExitStack()
    with ctx:
        def sb(name, shape, dt=F32):
            return ctx.enter_context(nc.sbuf_tensor(name, shape, dt))

        sem = lambda name: ctx.enter_context(nc.semaphore(name))

        xT_hi = sb("xT_hi", [P, KC, TOK], F32R)
        xT_lo = sb("xT_lo", [P, KC, TOK], F32R)
        wq_hi, wq_lo = (sb(f"wq_{n}", [P, GROUP0, KC, P], F32R) for n in ("hi", "lo"))
        wk_hi, wk_lo = (sb(f"wk_{n}", [P, KC, P], F32R) for n in ("hi", "lo"))
        wv_hi, wv_lo = (sb(f"wv_{n}", [P, KC, 2, P], F32R) for n in ("hi", "lo"))
        wo_hi, wo_lo = (sb(f"wo_{n}", [P, 2, GROUP0, D], F32R) for n in ("hi", "lo"))
        staged = sb("staged", [P, 2, 512])
        qT_hi, qT_lo = (sb(f"qT_{n}", [P, 2, GROUP0, SEQ], F32R) for n in ("hi", "lo"))
        kT_hi, kT_lo = (sb(f"kT_{n}", [P, 2, SEQ], F32R) for n in ("hi", "lo"))
        v_hi, v_lo = (sb(f"v_{n}", [P, TILES, 2 * P], F32R) for n in ("hi", "lo"))
        probs = sb("probs", [P, 2, GROUP0, 2 * P])
        pT_hi, pT_lo = (sb(f"pT_{n}", [P, 2, GROUP0 * P], F32R) for n in ("hi", "lo"))
        oT_hi, oT_lo = (sb(f"oT_{n}", [P, 2, GROUP0 * P], F32R) for n in ("hi", "lo"))
        cos = sb("cos", [P, SEQ])
        sin = sb("sin", [P, SEQ])
        mask = sb("mask", [P, 3 * P])
        turned = sb("turned", [P, 2, SEQ])
        by_cos = sb("by_cos", [P, 2, SEQ])
        row_max = sb("row_max", [P, 2, GROUP0])
        neg_max = sb("neg_max", [P, 2, GROUP0])
        row_sum = sb("row_sum", [P, 2, GROUP0])
        inv_sum = sb("inv_sum", [P, 2, GROUP0])
        gate = sb("gate", [P, 2])
        rows, ident = t["rows"], t["ident"]

        ps_s, ps_a, ps_t = psum[0:2], psum[2:4], psum[4:6]
        ps_o, ps_y = psum[6], psum[7]

        constants_in = sem("constants_in")
        xT_in = [sem(f"xT_in{k}") for k in range(KC)]
        weight_in = [sem("weight_in0"), sem("weight_in1")]
        xT_hi_done, xT_lo_done = sem("xT_hi_done"), sem("xT_lo_done")
        weight_hi_done, weight_lo_done = sem("weight_hi_done"), sem("weight_lo_done")
        projected = sem("projected")
        turned_done, sin_done, cos_done = sem("turned_done"), sem("sin_done"), sem("cos_done")
        roped, rope_hi, rope_lo = sem("roped"), sem("rope_hi"), sem("rope_lo")
        v_ready, v_hi_done, v_lo_done = sem("v_ready"), sem("v_hi_done"), sem("v_lo_done")
        scored, masked, max_done = sem("scored"), sem("masked"), sem("max_done")
        exp_done, inv_done, probs_done = sem("exp_done"), sem("inv_done"), sem("probs_done")
        pT_ready, pT_hi_done, pT_lo_done = sem("pT_ready"), sem("pT_hi_done"), sem("pT_lo_done")
        o_ready, o_hi_done, o_lo_done = sem("o_ready"), sem("o_hi_done"), sem("o_lo_done")
        y_ready, y_added = sem("y_ready"), sem("y_added")

        def weight_dest(n, hi):
            _, kind, g, h = WEIGHT_ORDER[n]
            if kind == "q":
                return (wq_hi if hi else wq_lo)[:, h, :, :]
            if kind == "k":
                return (wk_hi if hi else wk_lo)[:, :, :]
            if kind == "v":
                return (wv_hi if hi else wv_lo)[:, :, g, :]
            return (wo_hi if hi else wo_lo)[:, g, h, :]

        def staged_as(n, slot):
            v = staged[:, slot, :]
            return v if WEIGHT_ORDER[n][1] == "o" else v.rearrange("p (k c) -> p k c", k=KC)

        block = ctx.enter_context(nc.Block())

        @block.sync
        def _(sp):
            for k in range(KC):
                sp.dma_start(t["x_stage"][:, k, :],
                             x_T[k * P:(k + 1) * P, :]).then_inc(xT_in[k], 16)
            for n in range(HEAD_START):
                if n >= 2:
                    sp.wait_ge(weight_lo_done, n - 1)
                sp.dma_start(staged[:, n % 2, :], weight_stream[n]).then_inc(weight_in[n % 2], 16)
            sp.dma_start(cos[:, :], cos_T).then_inc(constants_in, 16)
            sp.dma_start(sin[:, :], sin_T).then_inc(constants_in, 16)
            sp.dma_start(mask[:, :], masks).then_inc(constants_in, 16)
            sp.dma_start(ident[:, :], ident_in).then_inc(constants_in, 16)
            sp.wait_ge(xT_lo_done, 2 * KC)
            sp.dma_start(rows[:, :, :], x_rows.rearrange("(t p) d -> p t d", p=P)).then_inc(constants_in, 16)
            with sp.Fori(0, PAIRS) as i:
                for n in range(PER_PAIR):
                    sp.wait_ge(weight_lo_done, i * PER_PAIR + HEAD_START + n - 1)
                    sp.dma_start(staged[:, (HEAD_START + n) % 2, :],
                                 weight_stream[bass.ds(i * PER_PAIR + HEAD_START + n, 1), :, :].rearrange(
                                     "a p c -> p (a c)")).then_inc(weight_in[(HEAD_START + n) % 2], 16)

        def loads(i, n):
            m = HEAD_START + n
            return i * (PER_PAIR // 2) * 16 + (m // 2 + 1) * 16, m % 2

        @block.scalar
        def _(act):
            for k in range(KC):
                act.wait_ge(xT_in[k], 16)
                for half in range(BATCH):
                    cols = slice(half * SEQ, (half + 1) * SEQ)
                    act.activation(xT_hi[:, k, cols], t["x_stage"][:, k, cols], ACT.Copy).then_inc(xT_hi_done, 1)
            for m in range(HEAD_START):
                act.wait_ge(weight_in[m % 2], (m // 2 + 1) * 16)
                n = m + FIRST_OF_NEXT
                act.activation(weight_dest(n, True), staged_as(n, m % 2), ACT.Copy).then_inc(weight_hi_done, 1)

            def turn(i, a):
                act.wait_ge(projected, 20 * i + a + 1)
                if a >= 2:
                    act.wait_ge(rope_lo, 20 * i + a - 1)
                half = HD0 // 2
                act.activation(turned[0:half, a % 2, :], ps_a[a % 2][half:P, :], ACT.Copy).then_inc(turned_done, 1)
                act.activation(turned[half:P, a % 2, :], ps_a[a % 2][0:half, :], ACT.Copy).then_inc(turned_done, 1)

            def rope_high(i, a):
                u, piece = a // 5, a % 5
                dest = kT_hi[:, u % 2, :] if piece == 0 else qT_hi[:, u % 2, piece - 1, :]
                act.wait_ge(roped, 20 * i + a + 1)
                act.activation(dest, turned[:, a % 2, :], ACT.Copy).then_inc(rope_hi, 1)

            with act.Fori(0, PAIRS) as i:
                for a in range(5):
                    if a >= 1:
                        rope_high(i, a - 1)
                    turn(i, a)
                rope_high(i, 4)
                for tile in range(TILES):
                    act.wait_ge(v_ready, TILES * i + tile + 1)
                    act.activation(v_hi[:, tile, :], ps_t[tile % 2][:, 0:2 * P], ACT.Copy).then_inc(v_hi_done, 1)
                for s in range(SLOTS + 1):
                    u, qt = divmod(s, 4)
                    if s >= 1:
                        for kb in range(key_tiles((s - 1) % 4)[1]):
                            act.wait_ge(pT_ready, 28 * i + blocks_before(s - 1) + kb + 1)
                            act.activation(pT_hi[:, kb, :], ps_t[kb][:, :], ACT.Copy).then_inc(pT_hi_done, 1)
                    if s < SLOTS:
                        act.wait_ge(max_done, 16 * i + s + 1)
                        for h in range(GROUP0):
                            act.activation(probs[:, s % 2, h, :], probs[:, s % 2, h, :], ACT.Exp,
                                           bias=neg_max[:, s % 2, h:h + 1], scale=SCALE0,
                                           accum_out=row_sum[:, s % 2, h:h + 1]).then_inc(exp_done, 1)
                    if 1 <= s < 13:
                        before = (s - 1) // 4
                        for piece in PIECES[(s - 1) % 4]:
                            rope_high(i, piece_index(before + 1, piece))
                    if s < 12:
                        for piece in PIECES[qt]:
                            turn(i, piece_index(u + 1, piece))
                    if s >= 1:
                        act.wait_ge(o_ready, 16 * i + s)
                        act.activation(oT_hi[:, (s - 1) % 2, :], ps_o[:, :], ACT.Copy).then_inc(o_hi_done, 1)
                    for n, (slot, kind, g, h) in enumerate(WEIGHT_ORDER):
                        if slot != s:
                            continue
                        if kind == "v":
                            act.wait_ge(v_ready, TILES * (i + 1))
                        elif kind == "o" and g == 0:
                            act.wait_ge(y_ready, 16 * i + 8)
                        elif kind == "o":
                            pass
                        else:
                            last = piece_index(1 if g == 1 else 3, "k" if kind == "k" else h)
                            act.wait_ge(projected, 20 * i + last + 1)
                        count, stage = loads(i, n)
                        act.wait_ge(weight_in[stage], count)
                        act.activation(weight_dest(n, True), staged_as(n, stage), ACT.Copy).then_inc(weight_hi_done, 1)

        @block.gpsimd
        def _(pool):
            for m in range(HEAD_START):
                n = m + FIRST_OF_NEXT
                pool.wait_ge(weight_hi_done, m + 1)
                pool.tensor_tensor(weight_dest(n, False), staged_as(n, m % 2), weight_dest(n, True).bitcast(F32),
                                   ALU.subtract).then_inc(weight_lo_done, 1)
            pool.wait_ge(constants_in, 80)

            def rotate(i, a):
                pool.wait_ge(turned_done, 2 * (20 * i + a + 1))
                pool.tensor_tensor(turned[:, a % 2, :], turned[:, a % 2, :], sin[:, :], ALU.mult).then_inc(sin_done, 1)
                pool.wait_ge(sin_done, 20 * i + a + 1)
                pool.wait_ge(cos_done, 20 * i + a + 1)
                pool.tensor_tensor(turned[:, a % 2, :], turned[:, a % 2, :], by_cos[:, a % 2, :],
                                   ALU.add).then_inc(roped, 1)

            with pool.Fori(0, PAIRS) as i:
                for a in range(5):
                    rotate(i, a)
                for s in range(SLOTS):
                    if s < 12:
                        for piece in PIECES[s % 4]:
                            rotate(i, piece_index(s // 4 + 1, piece))
                    for n, (slot, *_rest) in enumerate(WEIGHT_ORDER):
                        if slot == s:
                            count, stage = loads(i, n)
                            pool.wait_ge(weight_hi_done, i * PER_PAIR + HEAD_START + n + 1)
                            pool.tensor_tensor(weight_dest(n, False), staged_as(n, stage),
                                               weight_dest(n, True).bitcast(F32),
                                               ALU.subtract).then_inc(weight_lo_done, 1)

        @block.vector
        def _(dve):
            for k in range(KC):
                for half in range(BATCH):
                    cols = slice(half * SEQ, (half + 1) * SEQ)
                    dve.wait_ge(xT_hi_done, 2 * k + half + 1)
                    dve.tensor_tensor(xT_lo[:, k, cols], t["x_stage"][:, k, cols],
                                      xT_hi[:, k, cols].bitcast(F32), ALU.subtract).then_inc(xT_lo_done, 1)
            dve.wait_ge(constants_in, 80)

            def times_cos(i, a):
                dve.wait_ge(turned_done, 2 * (20 * i + a + 1))
                if a >= 2:
                    dve.wait_ge(roped, 20 * i + a - 1)
                dve.tensor_tensor(by_cos[:, a % 2, :], ps_a[a % 2][:, :], cos[:, :], ALU.mult).then_inc(cos_done, 1)

            def rope_low(i, a):
                u, piece = a // 5, a % 5
                hi = kT_hi[:, u % 2, :] if piece == 0 else qT_hi[:, u % 2, piece - 1, :]
                lo = kT_lo[:, u % 2, :] if piece == 0 else qT_lo[:, u % 2, piece - 1, :]
                dve.wait_ge(rope_hi, 20 * i + a + 1)
                dve.tensor_tensor(lo, turned[:, a % 2, :], hi.bitcast(F32), ALU.subtract).then_inc(rope_lo, 1)

            with dve.Fori(0, PAIRS) as i:
                for a in range(5):
                    if a >= 1:
                        rope_low(i, a - 1)
                    times_cos(i, a)
                rope_low(i, 4)
                for tile in range(TILES):
                    dve.wait_ge(v_hi_done, TILES * i + tile + 1)
                    dve.tensor_tensor(v_lo[:, tile, :], ps_t[tile % 2][:, 0:2 * P],
                                      v_hi[:, tile, :].bitcast(F32), ALU.subtract).then_inc(v_lo_done, 1)
                for s in range(SLOTS + 2):
                    u, qt = divmod(s, 4)
                    if s < SLOTS:
                        seen = mask[:, P:3 * P] if qt == 0 else mask[:, 0:2 * P]
                        for h in range(GROUP0):
                            if h % 2 == 0:
                                dve.wait_ge(scored, 2 * (16 * i + s) + h // 2 + 1)
                                dve.memset(gate[:, h // 2:h // 2 + 1], 0.0)
                            dve.tensor_tensor_reduce(
                                probs[:, s % 2, h, :], ps_s[h // 2][:, (h % 2) * 2 * P:(h % 2 + 1) * 2 * P], seen,
                                1.0, LOWEST, ALU.add, ALU.max, row_max[:, s % 2, h:h + 1]).then_inc(masked, 1)
                        dve.wait_ge(masked, 4 * (16 * i + s + 1))
                        dve.tensor_scalar(neg_max[:, s % 2, :], row_max[:, s % 2, :], -SCALE0, None,
                                          ALU.mult).then_inc(max_done, 1)
                    if 1 <= s <= SLOTS:
                        for kb in range(key_tiles((s - 1) % 4)[1]):
                            dve.wait_ge(pT_hi_done, 28 * i + blocks_before(s - 1) + kb + 1)
                            dve.tensor_tensor(pT_lo[:, kb, :], ps_t[kb][:, :], pT_hi[:, kb, :].bitcast(F32),
                                              ALU.subtract).then_inc(pT_lo_done, 1)
                    if s < SLOTS:
                        dve.wait_ge(exp_done, 4 * (16 * i + s + 1))
                        dve.reciprocal(inv_sum[:, s % 2, :], row_sum[:, s % 2, :]).then_inc(inv_done, 1)
                        dve.wait_ge(inv_done, 16 * i + s + 1)
                        for h in range(GROUP0):
                            dve.tensor_scalar(probs[:, s % 2, h, :], probs[:, s % 2, h, :],
                                              inv_sum[:, s % 2, h:h + 1], None, ALU.mult).then_inc(probs_done, 1)
                    if 1 <= s < 13:
                        before = (s - 1) // 4
                        for piece in PIECES[(s - 1) % 4]:
                            rope_low(i, piece_index(before + 1, piece))
                    if s < 12:
                        for piece in PIECES[qt]:
                            times_cos(i, piece_index(u + 1, piece))
                    if 1 <= s <= SLOTS:
                        dve.wait_ge(o_hi_done, 16 * i + s)
                        dve.tensor_tensor(oT_lo[:, (s - 1) % 2, :], ps_o[:, :],
                                          oT_hi[:, (s - 1) % 2, :].bitcast(F32), ALU.subtract).then_inc(o_lo_done, 1)
                    if s >= 2:
                        b, tile = ((s - 2) // 4) % 2, (s - 2) % 4
                        row = rows[:, b * SEQ_TILES + tile, :]
                        dve.wait_ge(y_ready, 16 * i + s - 1)
                        dve.tensor_tensor(row, ps_y[:, :], row, ALU.add).then_inc(y_added, 1)

        @block.tensor
        def _(pe):
            def project(i, u, piece):
                a = piece_index(u, piece)
                g, b = divmod(u, 2)
                cols = slice(b * SEQ, (b + 1) * SEQ)
                pe.wait_ge(weight_lo_done, weights_done(i, "k" if piece == "k" else "q", g, 0 if piece == "k" else piece))
                if a >= 2:
                    pe.wait_ge(cos_done, 20 * i + a - 1)
                w = (wk_hi, wk_lo) if piece == "k" else (wq_hi[:, piece, :, :], wq_lo[:, piece, :, :])
                three(pe, ps_a[a % 2][:, :], [(w[0][:, k, :], w[1][:, k, :], xT_hi[:, k, cols], xT_lo[:, k, cols])
                                          for k in range(KC)], projected)

            def values(i, tile):
                if tile == 0:
                    pe.wait_ge(weight_lo_done, weights_done(i, "v", 1))
                if tile >= 2:
                    pe.wait_ge(v_lo_done, TILES * i + tile - 1)
                at = slice(tile * P, (tile + 1) * P)
                three(pe, ps_t[tile % 2][:, 0:2 * P],
                      [(xT_hi[:, k, at], xT_lo[:, k, at], wv_hi[:, k, :, :].rearrange("p g c -> p (g c)"),
                        wv_lo[:, k, :, :].rearrange("p g c -> p (g c)")) for k in range(KC)], v_ready)

            def scores(i, s):
                u, qt = divmod(s, 4)
                first, _ = key_tiles(qt)
                keys = slice(first * P, (first + 2) * P)
                at = slice(qt * P, (qt + 1) * P)
                for pair in range(2):
                    if s >= 1:
                        pe.wait_ge(masked, 4 * (16 * i + s - 1) + 2 * pair + 2)
                    for h in (2 * pair, 2 * pair + 1):
                        if qt == 0:
                            pe.wait_ge(rope_lo, 20 * i + piece_index(u, h) + 1)
                        steps = [(qT_hi, kT_hi), (qT_hi, kT_lo), (qT_lo, kT_hi)]
                        for n, (q, k) in enumerate(steps):
                            mm = pe.matmul(ps_s[pair][:, (h % 2) * 2 * P:(h % 2 + 1) * 2 * P], q[:, u % 2, h, at],
                                           k[:, u % 2, keys], start=(n == 0), stop=(n == 2))
                    mm.then_inc(scored, 1)

            def turn_probs(i, s):
                pe.wait_ge(probs_done, 4 * (16 * i + s + 1))
                if s == 0:
                    pe.wait_ge(v_lo_done, TILES * (i + 1))
                for kb in range(key_tiles(s % 4)[1]):
                    for h in range(GROUP0):
                        mm = pe.transpose(ps_t[kb][:, h * P:(h + 1) * P], probs[:, s % 2, h, kb * P:(kb + 1) * P],
                                          ident[:, :])
                    mm.then_inc(pT_ready, 1)

            def apply_probs(i, s):
                u, qt = divmod(s, 4)
                g, b = divmod(u, 2)
                first, count = key_tiles(qt)
                if s >= 1:
                    pe.wait_ge(o_lo_done, 16 * i + s)
                terms = []
                for kb in range(count):
                    tile = b * SEQ_TILES + first + kb
                    at = slice(g * P, (g + 1) * P)
                    terms.append((kb, v_hi[:, tile, at], v_lo[:, tile, at], pT_hi[:, kb, :], pT_lo[:, kb, :]))
                pe.wait_ge(pT_lo_done, 28 * i + blocks_before(s) + count)
                three(pe, ps_o[:, :], [x[1:] for x in terms], o_ready)

            def project_out(i, s):
                g = s // 8
                pe.wait_ge(weight_lo_done, weights_done(i, "o", g, GROUP0 - 1))
                pe.wait_ge(o_lo_done, 16 * i + s + 1)
                if s >= 1:
                    pe.wait_ge(y_added, 16 * i + s)
                three(pe, ps_y[:, :], [(oT_hi[:, s % 2, h * P:(h + 1) * P], oT_lo[:, s % 2, h * P:(h + 1) * P],
                                    wo_hi[:, g, h, :], wo_lo[:, g, h, :]) for h in range(GROUP0)], y_ready)

            pe.wait_ge(xT_lo_done, 2 * KC)
            pe.wait_ge(constants_in, 80)
            with pe.Fori(0, PAIRS) as i:
                for piece in ("k", 0, 1, 2, 3):
                    project(i, 0, piece)
                for tile in range(TILES):
                    values(i, tile)
                for s in range(SLOTS + 2):
                    u, qt = divmod(s, 4)
                    if s < SLOTS:
                        scores(i, s)
                    if 1 <= s <= SLOTS:
                        turn_probs(i, s - 1)
                    if s < 12:
                        for piece in PIECES[qt]:
                            project(i, u + 1, piece)
                    if 1 <= s <= SLOTS:
                        apply_probs(i, s - 1)
                    if s >= 2:
                        project_out(i, s - 2)


def layout0(inputs):
    x = inputs["L0_attn_x"].reshape(TOK, D)
    wq = inputs["L0_attn_wq"].reshape(KC, P, KV0, GROUP0, HD0)
    wk = inputs["L0_attn_wk"].reshape(KC, P, KV0, HD0)
    wv = inputs["L0_attn_wv"].reshape(KC, P, KV0, HD0)
    wo = inputs["L0_attn_wo"].reshape(KV0, GROUP0, P, D)
    blocks = []
    def add(pair, n):
        _, kind, g, h = WEIGHT_ORDER[n]
        kv = 2 * pair + g
        if kind == "o":
            blocks.append(wo[kv, h])
        else:
            w = {"q": wq[:, :, kv, h, :] if kind == "q" else None, "k": wk[:, :, kv], "v": wv[:, :, kv]}[kind]
            blocks.append(w.transpose(1, 0, 2).reshape(P, 512))
    for n in range(FIRST_OF_NEXT, PER_PAIR):
        add(0, n)
    for pair in range(PAIRS):
        for n in range(PER_PAIR):
            add(pair if n < FIRST_OF_NEXT else (pair + 1) % PAIRS, n)
    return {"x_T": np.ascontiguousarray(x.T), "x_rows": x, "weights0": np.stack(blocks)}


def tables0():
    half = HD0 // 2
    inv = 10000.0 ** (-np.arange(half, dtype=np.float32) / half)
    ang = (np.arange(SEQ, dtype=np.float32)[:, None] * inv[None, :].astype(np.float32)).T
    cos = np.concatenate([np.cos(ang), np.cos(ang)]).astype(np.float32)
    sin = np.concatenate([-np.sin(ang), np.sin(ang)]).astype(np.float32)
    q, k = np.arange(P)[:, None], np.arange(P)[None, :]
    mask = np.concatenate([np.where(k > q, 0, MASKED), np.where(k <= q, 0, MASKED), np.full((P, P), MASKED)], 1)
    return {"cos0": cos, "sin0": sin, "mask0": mask.astype(np.float32), "ident": np.eye(P, dtype=np.float32)}

F0 = 1376
F_TILES = -(-F0 // P)


class Norm:

    def __init__(self, ctx, nc, name, rows, ident, banks, xT_hi, xT_lo, xT=None):
        sb = lambda n, shape: ctx.enter_context(nc.sbuf_tensor(f"{name}_{n}", shape, F32))
        sem = lambda n: ctx.enter_context(nc.semaphore(f"{name}_{n}"))
        self.rows, self.ident, self.banks = rows, ident, banks
        self.xT_hi, self.xT_lo, self.xT = xT_hi, xT_lo, xT
        self.stats = sb("stats", [P, TILES, 6])
        self.mean_var = sb("mean_var", [P, TILES, 2])
        self.deviation = sb("deviation", [P, TILES])
        self.inv_deviation = sb("inv_deviation", [P, TILES])
        self.eps = sb("eps", [P, 1])
        self.eps_set, self.stats_done, self.var_done = sem("eps_set"), sem("stats_done"), sem("var_done")
        self.sqrt_done, self.inv_done, self.normed = sem("sqrt_done"), sem("inv_done"), sem("normed")
        self.turned, self.hi_done, self.lo_done = sem("turned"), sem("hi_done"), sem("lo_done")

    def on_vector(self, dve, transposed=True):
        dve.memset(self.eps[:, :], EPS).then_inc(self.eps_set, 1)
        for t in range(TILES):
            dve.bn_stats(self.stats[:, t, :], self.rows[:, t, :]).then_inc(self.stats_done, 1)
        for t in range(TILES):
            dve.wait_ge(self.stats_done, t + 1)
            dve.bn_aggr(self.mean_var[:, t, :], self.stats[:, t, :]).then_inc(self.var_done, 1)
        dve.wait_ge(self.sqrt_done, 1)
        dve.reciprocal(self.inv_deviation[:, :], self.deviation[:, :]).then_inc(self.inv_done, 1)
        dve.wait_ge(self.inv_done, 1)
        for t in range(TILES):
            dve.tensor_scalar(self.rows[:, t, :], self.rows[:, t, :], self.mean_var[:, t, 0:1],
                              self.inv_deviation[:, t:t + 1], ALU.subtract, ALU.mult).then_inc(self.normed, 1)
        if transposed:
            for t in range(TILES):
                at = slice(t * P, (t + 1) * P)
                dve.wait_ge(self.hi_done, t + 1)
                dve.tensor_tensor(self.xT_lo[:, :, at], self.bank(t), self.xT_hi[:, :, at].bitcast(F32),
                                  ALU.subtract).then_inc(self.lo_done, 1)

    def bank(self, t):
        return self.banks[t % 2][:, :].rearrange("p (k c) -> p k c", k=KC)

    def on_scalar(self, act, transposed=True):
        act.wait_ge(self.eps_set, 1)
        act.wait_ge(self.var_done, TILES)
        act.activation(self.deviation[:, :], self.mean_var[:, :, 1], ACT.Sqrt,
                       bias=self.eps[:, 0:1]).then_inc(self.sqrt_done, 1)
        if transposed:
            for t in range(TILES):
                act.wait_ge(self.turned, t + 1)
                act.activation(self.xT_hi[:, :, t * P:(t + 1) * P], self.bank(t), ACT.Copy).then_inc(self.hi_done, 1)

    def on_tensor(self, pe):
        for t in range(TILES):
            pe.wait_ge(self.normed, t + 1)
            if t >= 2:
                pe.wait_ge(self.lo_done, t - 1)
            for k in range(KC):
                mm = pe.transpose(self.banks[t % 2][:, k * P:(k + 1) * P], self.rows[:, t, k * P:(k + 1) * P],
                                  self.ident[:, :])
            mm.then_inc(self.turned, 1)


def feed_forward0(nc, t, weight_stream, psum):
    ctx = ExitStack()
    with ctx:
        def sb(name, shape, dt=F32):
            return ctx.enter_context(nc.sbuf_tensor(name, shape, dt))

        sem = lambda name: ctx.enter_context(nc.semaphore(name))
        rows = t["rows"]
        xT_hi, xT_lo = (sb(f"f0_xT_{n}", [P, KC, TOK], F32R) for n in ("hi", "lo"))
        hT_hi, hT_lo = (sb(f"f0_hT_{n}", [P, F_TILES, TOK], F32R) for n in ("hi", "lo"))
        wg_hi, wg_lo, wu_hi, wu_lo = (sb(f"f0_w{n}", [P, KC, P], F32R) for n in ("g_hi", "g_lo", "u_hi", "u_lo"))
        wd_hi, wd_lo = (sb(f"f0_wd_{n}", [P, F_TILES, D], F32R) for n in ("hi", "lo"))
        staged = sb("f0_staged", [P, 3, 512])
        gated = sb("f0_gated", [P, BATCH, SEQ])
        hidden = sb("f0_hidden", [P, BATCH, SEQ])
        ps_g, ps_u, ps_y = psum[0:2], psum[2:4], psum[4:6]

        norm = Norm(ctx, nc, "n0", rows, t["ident"], psum[6:8], xT_hi, xT_lo)
        weight_in = {k: sem(f"f0_in_{k}") for k in "gud"}
        w_hi_done = {k: sem(f"f0_hi_{k}") for k in "gud"}
        w_lo_done = {k: sem(f"f0_lo_{k}") for k in "gud"}
        gate_ready, up_ready = sem("f0_gate_ready"), sem("f0_up_ready")
        gated_done, hidden_done = sem("f0_gated_done"), sem("f0_hidden_done")
        h_hi_done, h_lo_done = sem("f0_h_hi_done"), sem("f0_h_lo_done")
        y_ready, y_added = sem("f0_y_ready"), sem("f0_y_added")

        def dest(kind, f, hi):
            if kind == "d":
                return (wd_hi if hi else wd_lo)[:, bass.ds(f, 1), :].rearrange("p a c -> p (a c)")
            pair = {"g": (wg_hi, wg_lo), "u": (wu_hi, wu_lo)}[kind]
            return pair[0 if hi else 1][:, :, :].rearrange("p k c -> p (k c)")

        block = ctx.enter_context(nc.Block())

        @block.sync
        def _(sp):
            def load(f, kind):
                n = "gud".index(kind)
                sp.dma_start(staged[:, n, :], weight_stream[bass.ds(3 * f + n, 1), :, :].rearrange(
                    "a p c -> p (a c)")).then_inc(weight_in[kind], 16)

            for kind in "gud":
                load(0, kind)
            with sp.Fori(1, F_TILES) as f:
                for kind in "gud":
                    sp.wait_ge(w_lo_done[kind], f)
                    load(f, kind)

        @block.scalar
        def _(act):
            def split(kind, f):
                act.wait_ge(weight_in[kind], 16 * (f + 1))
                act.activation(dest(kind, f, True), staged[:, "gud".index(kind), :],
                               ACT.Copy).then_inc(w_hi_done[kind], 1)

            def gates(f):
                for b in range(BATCH):
                    act.wait_ge(gate_ready, 2 * f + b + 1)
                    act.activation(gated[:, b, :], ps_g[b][:, :], ACT.Silu).then_inc(gated_done, 1)

            def high(f):
                for b in range(BATCH):
                    act.wait_ge(hidden_done, 2 * f + b + 1)
                    act.activation(hT_hi[:, bass.ds(f, 1), b * SEQ:(b + 1) * SEQ].rearrange("p a c -> p (a c)"),
                                   hidden[:, b, :], ACT.Copy).then_inc(h_hi_done, 1)

            split("g", 0)
            split("u", 0)
            norm.on_scalar(act)
            with act.Fori(0, F_TILES - 1) as f:
                gates(f)
                split("g", f + 1)
                split("d", f)
                high(f)
                act.wait_ge(up_ready, 2 * f + 2)
                split("u", f + 1)
            gates(F_TILES - 1)
            split("d", F_TILES - 1)
            high(F_TILES - 1)

        @block.gpsimd
        def _(pool):
            def rest(kind, f):
                pool.wait_ge(w_hi_done[kind], f + 1)
                pool.tensor_tensor(dest(kind, f, False), staged[:, "gud".index(kind), :],
                                   dest(kind, f, True).bitcast(F32), ALU.subtract).then_inc(w_lo_done[kind], 1)

            rest("g", 0)
            rest("u", 0)
            with pool.Fori(0, F_TILES - 1) as f:
                rest("g", f + 1)
                rest("d", f)
                rest("u", f + 1)
            rest("d", F_TILES - 1)

        @block.vector
        def _(dve):
            norm.on_vector(dve)
            with dve.Fori(0, F_TILES) as f:
                for b in range(BATCH):
                    dve.wait_ge(up_ready, 2 * f + b + 1)
                    dve.wait_ge(gated_done, 2 * f + b + 1)
                    dve.tensor_tensor(hidden[:, b, :], ps_u[b][:, :], gated[:, b, :], ALU.mult).then_inc(hidden_done, 1)
                for b in range(BATCH):
                    at = lambda x: x[:, bass.ds(f, 1), b * SEQ:(b + 1) * SEQ].rearrange("p a c -> p (a c)")
                    dve.wait_ge(h_hi_done, 2 * f + b + 1)
                    dve.tensor_tensor(at(hT_lo), hidden[:, b, :], at(hT_hi).bitcast(F32),
                                      ALU.subtract).then_inc(h_lo_done, 1)
                dve.wait_ge(h_lo_done, 2 * f + 2)
            for tile in range(TILES):
                dve.wait_ge(y_ready, tile + 1)
                dve.tensor_tensor(rows[:, tile, :], ps_y[tile % 2][:, :], rows[:, tile, :],
                                  ALU.add).then_inc(y_added, 1)

        @block.tensor
        def _(pe):
            norm.on_tensor(pe)
            pe.wait_ge(norm.lo_done, TILES)
            with pe.Fori(0, F_TILES) as f:
                pe.wait_ge(w_lo_done["g"], f + 1)
                for b in range(BATCH):
                    three(pe, ps_g[b][:, :], [(wg_hi[:, k, :], wg_lo[:, k, :], xT_hi[:, k, b * SEQ:(b + 1) * SEQ],
                                               xT_lo[:, k, b * SEQ:(b + 1) * SEQ]) for k in range(KC)], gate_ready)
                pe.wait_ge(w_lo_done["u"], f + 1)
                for b in range(BATCH):
                    three(pe, ps_u[b][:, :], [(wu_hi[:, k, :], wu_lo[:, k, :], xT_hi[:, k, b * SEQ:(b + 1) * SEQ],
                                               xT_lo[:, k, b * SEQ:(b + 1) * SEQ]) for k in range(KC)], up_ready)
            pe.wait_ge(w_lo_done["d"], F_TILES)
            pe.wait_ge(h_lo_done, 2 * F_TILES)
            for tile in range(TILES):
                if tile >= 2:
                    pe.wait_ge(y_added, tile - 1)
                at = slice(tile * P, (tile + 1) * P)
                three(pe, ps_y[tile % 2][:, :], [(hT_hi[:, f, at], hT_lo[:, f, at], wd_hi[:, f, :], wd_lo[:, f, :])
                                                 for f in range(F_TILES)], y_ready)


def layout_ffn0(inputs):
    pad = F_TILES * P - F0
    blocks = []
    up, gate = (np.pad(inputs[n], ((0, pad), (0, 0))).T.reshape(KC, P, F_TILES, P).transpose(2, 1, 0, 3)
                for n in ("L0_ffn_W_up", "L0_ffn_W_gate"))
    down = np.pad(inputs["L0_ffn_W_down"], ((0, 0), (0, pad))).T.reshape(F_TILES, P, D)
    for f in range(F_TILES):
        blocks += [gate[f].reshape(P, 512), up[f].reshape(P, 512), down[f]]
    return {"weights_f0": np.stack(blocks)}

HEADS1, KV1 = 32, 8
HD1 = D // HEADS1
GROUP1 = HEADS1 // KV1
SCALE1 = HD1 ** -0.5
GQ = GROUP1 * HD1
PARTS = 4
STACK = PARTS * HD1
SLOTS1 = 8
QT_OF = [3, 2, 1, 0] * BATCH
EVEN_BLOCKS = [2, 2, 1, 1] * BATCH
ODD_BLOCKS = [2, 1, 1, 0] * BATCH


def odd_bank_order():
    order = []
    for s in range(SLOTS1 + 1):
        if s >= 1:
            order += [("p", s - 1, kb) for kb in range(1, QT_OF[s - 1] + 1, 2)]
        if s < 4:
            order.append(("s", 1, s))
        if s > 4:
            order.append(("s", 0, s - 5))
    return order


ODD_ORDER = odd_bank_order()
ODD_AT = {x: n for n, x in enumerate(ODD_ORDER)}
EVEN_ORDER = [(s, kb) for s in range(SLOTS1) for kb in range(0, QT_OF[s] + 1, 2)]
EVEN_AT = {x: n for n, x in enumerate(EVEN_ORDER)}
ODD_N, EVEN_N = len(ODD_ORDER), len(EVEN_ORDER)


def attention1(nc, t, w_qkv, w_o, cos_in, sin_in, mask_in, psum):
    ctx = ExitStack()
    with ctx:
        def sb(name, shape, dt=F32):
            return ctx.enter_context(nc.sbuf_tensor("a1_" + name, shape, dt))

        sem = lambda name: ctx.enter_context(nc.semaphore("a1_" + name))
        rows, ident = t["rows"], t["ident"]
        KVW = 2 * KV1 * HD1
        xT_hi, xT_lo = (sb(f"xT_{n}", [P, KC, TOK], F32R) for n in ("hi", "lo"))
        w_hi, w_lo = (sb(f"w_{n}", [P, KC, D + KVW], F32R) for n in ("hi", "lo"))
        wo_hi, wo_lo = (sb(f"wo_{n}", [P, KC, D], F32R) for n in ("hi", "lo"))
        staged = sb("staged", [P, 2, D + KVW])
        q_tok = sb("q_tok", [P, TILES, (KV1 + 1) * GQ])
        k_tok = sb("k_tok", [P, TILES, (KV1 + 1) * HD1])
        v_tok = sb("v_tok", [P, TILES, (KV1 + 1) * HD1])
        q_parts = sb("q_parts", [P, TILES, GROUP1, PARTS, HD1], F32R)
        k_parts = sb("k_parts", [P, TILES, STACK + STACK + STACK], F32R)
        q_stack = sb("q_stack", [P, 2, TOK], F32R)
        k_stack = sb("k_stack", [P, 2, TOK], F32R)
        v_now = sb("v_now", [P, TILES, P])
        probs = sb("probs", [P, 2, GROUP1, SEQ])
        pT = sb("pT", [P, SEQ_TILES, GROUP1 * P])
        oT_now = sb("oT_now", [P, GROUP1 * P])
        o_tok = sb("o_tok", [P, TILES, D])
        cos = sb("cos", [P, SEQ_TILES, HD1])
        sin = sb("sin", [P, SEQ_TILES, HD1])
        mask = sb("mask", [P, 5 * P])
        ident_r = sb("ident_r", [P, P], F32R)
        by_cos = sb("by_cos", [P, D + KV1 * HD1])
        by_sin = sb("by_sin", [P, D + KV1 * HD1])
        row_max = sb("row_max", [P, 2, GROUP1])
        neg_max = sb("neg_max", [P, 2, GROUP1])
        row_sum = sb("row_sum", [P, 4, GROUP1])
        inv_sum = sb("inv_sum", [P, 2, GROUP1])
        gate = sb("gate", [P, GROUP1])

        norm = Norm(ctx, nc, "n1", rows, ident, psum[4:6], xT_hi, xT_lo)
        ps_q, ps_kv = psum[0:2], psum[2:4]
        ps_s, ps_even, ps_odd, ps_o, ps_oT = psum[0:4], psum[4], psum[5], psum[6], psum[7]

        constants_in = sem("constants_in")
        weight_in = [sem("weight_in0"), sem("weight_in1")]
        w_hi_done, w_lo_done, ident_done, pads_set = sem("w_hi_done"), sem("w_lo_done"), sem("ident_done"), sem("pads_set")
        qkv_ready, cos_done, sin_done, v_done = sem("qkv_ready"), sem("cos_done"), sem("sin_done"), sem("v_done")
        tok_done = sem("tok_done")
        part_hi, part_lo, part_copied, v_now_done = sem("part_hi"), sem("part_lo"), sem("part_copied"), sem("v_now_done")
        scored, masked, max_done, exp_done = sem("scored"), sem("masked"), sem("max_done"), sem("exp_done")
        even_ready, even_read, odd_ready, odd_read = sem("even_ready"), sem("even_read"), sem("odd_ready"), sem("odd_read")
        o_ready, o_read, oT_ready, inv_done, o_done = sem("o_ready"), sem("o_read"), sem("oT_ready"), sem("inv_done"), sem("o_done")
        out_turned, out_hi, out_lo = sem("out_turned"), sem("out_hi"), sem("out_lo")
        y_ready, y_added = sem("y_ready"), sem("y_added")

        heads = lambda ap, n: ap.rearrange("p (h d) -> p h d", d=HD1)
        half = HD1 // 2
        block = ctx.enter_context(nc.Block())

        @block.sync
        def _(sp):
            for k in range(KC):
                if k >= 2:
                    sp.wait_ge(w_lo_done, k - 1)
                sp.dma_start(staged[:, k % 2, :], w_qkv[k]).then_inc(weight_in[k % 2], 16)
            sp.dma_start(cos[:, :, :], cos_in).then_inc(constants_in, 16)
            sp.dma_start(sin[:, :, :], sin_in).then_inc(constants_in, 16)
            sp.dma_start(mask[:, :], mask_in).then_inc(constants_in, 16)
            for k in range(KC, 2 * KC):
                sp.wait_ge(w_lo_done, k - 1)
                sp.dma_start(staged[:, k % 2, 0:D], w_o[k - KC]).then_inc(weight_in[k % 2], 16)

        def weight_block(k):
            hi, lo = (w_hi, w_lo) if k < KC else (wo_hi, wo_lo)
            width = D + KVW if k < KC else D
            return hi[:, k % KC, :], lo[:, k % KC, :], staged[:, k % 2, 0:width]

        def q_part(n):
            return q_parts[:, :, :, n, :]

        def k_part(n):
            return k_parts[:, :, STACK + n * HD1:STACK + (n + 1) * HD1]

        def q_of(g):
            return q_tok[:, :, bass.ds(g * GQ, GQ)].rearrange("p t (h d) -> p t h d", d=HD1)

        def k_of(g):
            return k_tok[:, :, bass.ds(g * HD1, HD1)]

        @block.scalar
        def _(act):
            norm.on_scalar(act, transposed=False)
            for k in range(KC):
                act.wait_ge(weight_in[k % 2], 16 * (k // 2 + 1))
                hi, _, raw = weight_block(k)
                act.activation(hi, raw, ACT.Copy).then_inc(w_hi_done, 1)
            for tile in range(TILES):
                act.wait_ge(norm.turned, tile + 1)
                act.activation(xT_hi[:, :, tile * P:(tile + 1) * P], norm.bank(tile), ACT.Copy).then_inc(norm.hi_done, 1)
            act.activation(ident_r[:, :], ident[:, :], ACT.Copy).then_inc(ident_done, 1)
            for tile in range(TILES):
                act.wait_ge(sin_done, 4 * (tile + 1))
                act.activation(v_tok[:, tile, 0:KV1 * HD1], ps_kv[tile % 2][:, KV1 * HD1:KVW], ACT.Copy).then_inc(v_done, 1)
            for k in range(KC, 2 * KC):
                act.wait_ge(weight_in[k % 2], 16 * (k // 2 + 1))
                hi, _, raw = weight_block(k)
                act.activation(hi, raw, ACT.Copy).then_inc(w_hi_done, 1)

            def high_parts(g):
                for n in (0, 1):
                    act.activation(q_part(n), q_of(g), ACT.Copy).then_inc(part_hi, 1)
                for n in (0, 2):
                    act.activation(k_part(n), k_of(g), ACT.Copy).then_inc(part_hi, 1)

            act.wait_ge(tok_done, 2 * TILES)
            act.wait_ge(pads_set, 6)

            def values(g, b):
                at = slice(b * SEQ_TILES, (b + 1) * SEQ_TILES)
                act.activation(v_now[:, at, 0:HD1], v_tok[:, at, bass.ds(g * HD1, HD1)], ACT.Copy).then_inc(v_now_done, 1)

            high_parts(0)
            values(0, 0)
            with act.Fori(0, KV1) as g:
                for s in range(SLOTS1 + 1):
                    if s >= 1:
                        for kb in range(0, QT_OF[s - 1] + 1, 2):
                            act.wait_ge(even_ready, EVEN_N * g + EVEN_AT[(s - 1, kb)] + 1)
                            act.activation(pT[:, kb, :], ps_even[:, :], ACT.Copy).then_inc(even_read, 1)
                    if s < SLOTS1:
                        n = max(QT_OF[s] + 1, 2) * P
                        act.wait_ge(max_done, SLOTS1 * g + s + 1)
                        for h in range(GROUP1):
                            act.activation(probs[:, s % 2, h, 0:n], probs[:, s % 2, h, 0:n], ACT.Exp,
                                           bias=neg_max[:, s % 2, h:h + 1], scale=SCALE1,
                                           accum_out=row_sum[:, s % 4, h:h + 1]).then_inc(exp_done, 1)
                    if s >= 1:
                        act.wait_ge(o_ready, SLOTS1 * g + s)
                        act.activation(oT_now[:, :], ps_o[:, :], ACT.Copy).then_inc(o_read, 1)
                    if s == 0:
                        values(g, 1)
                    if s == 4:
                        values(g + 1, 0)
                        act.wait_ge(odd_ready, ODD_N * g + 4 + ODD_AT[("s", 1, 3)] + 1)
                        high_parts(g + 1)
            for tile in range(TILES):
                act.wait_ge(out_turned, tile + 1)
                act.activation(xT_hi[:, :, tile * P:(tile + 1) * P], norm.bank(tile), ACT.Copy).then_inc(out_hi, 1)

        @block.gpsimd
        def _(pool):
            pool.memset(q_tok[:, :, KV1 * GQ:], 0.0).then_inc(pads_set, 1)
            pool.memset(k_tok[:, :, KV1 * HD1:], 0.0).then_inc(pads_set, 1)
            pool.memset(v_tok[:, :, KV1 * HD1:], 0.0).then_inc(pads_set, 1)
            pool.memset(v_now[:, :, :], 0.0).then_inc(pads_set, 1)
            pool.memset(k_parts[:, :, 0:STACK].bitcast(F32), 0.0).then_inc(pads_set, 1)
            pool.memset(k_parts[:, :, 2 * STACK:].bitcast(F32), 0.0).then_inc(pads_set, 1)

            def weights(ks):
                for k in ks:
                    hi, lo, raw = weight_block(k)
                    pool.wait_ge(w_hi_done, k + 1)
                    pool.tensor_tensor(lo, raw, hi.bitcast(F32), ALU.subtract).then_inc(w_lo_done, 1)

            weights(range(KC))
            for tile in range(TILES):
                pool.wait_ge(sin_done, 4 * (tile + 1))
                pool.tensor_tensor(q_tok[:, tile, 0:D], by_cos[:, 0:D], by_sin[:, 0:D], ALU.add).then_inc(tok_done, 1)
                pool.tensor_tensor(k_tok[:, tile, 0:KV1 * HD1], by_cos[:, D:], by_sin[:, D:], ALU.add).then_inc(tok_done, 1)
            weights(range(KC, 2 * KC))

            def low_again(g):
                pool.wait_ge(part_hi, 4 * (g + 1))
                pool.tensor_tensor(q_part(3), q_of(g), q_part(0).bitcast(F32), ALU.subtract).then_inc(part_copied, 1)
                pool.tensor_tensor(k_part(3), k_of(g), k_part(0).bitcast(F32), ALU.subtract).then_inc(part_copied, 1)

            pool.wait_ge(tok_done, 2 * TILES)
            low_again(0)
            with pool.Fori(0, KV1) as g:
                low_again(g + 1)

        @block.vector
        def _(dve):
            norm.on_vector(dve)
            dve.wait_ge(constants_in, 48)
            for tile in range(TILES):
                q_in = ps_q[tile % 2][:, 0:D].rearrange("p (h d) -> p h d", d=HD1)
                k_in = ps_kv[tile % 2][:, 0:KV1 * HD1].rearrange("p (h d) -> p h d", d=HD1)
                c, s_ = cos[:, tile % SEQ_TILES, :], sin[:, tile % SEQ_TILES, :]
                dve.wait_ge(qkv_ready, 2 * (tile + 1))
                if tile >= 1:
                    dve.wait_ge(tok_done, 2 * tile)
                for source, n, at in ((q_in, HEADS1, 0), (k_in, KV1, D)):
                    out = by_cos[:, at:at + n * HD1].rearrange("p (h d) -> p h d", d=HD1)
                    dve.tensor_tensor(out, source, c.rearrange("p (a d) -> p a d", a=1).broadcast_to([P, n, HD1]),
                                      ALU.mult).then_inc(cos_done, 1)
                    out = by_sin[:, at:at + n * HD1].rearrange("p (h d) -> p h d", d=HD1)
                    for to, of in ((slice(0, half), slice(half, HD1)), (slice(half, HD1), slice(0, half))):
                        dve.tensor_tensor(out[:, :, to], source[:, :, of],
                                          s_[:, to].rearrange("p (a d) -> p a d", a=1).broadcast_to([P, n, half]),
                                          ALU.mult).then_inc(sin_done, 1)

            def low_parts(g):
                dve.wait_ge(part_hi, 4 * (g + 1))
                dve.tensor_tensor(q_part(2), q_of(g), q_part(0).bitcast(F32), ALU.subtract).then_inc(part_lo, 1)
                dve.tensor_tensor(k_part(1), k_of(g), k_part(0).bitcast(F32), ALU.subtract).then_inc(part_lo, 1)

            def read_stack(g, b, n):
                base = ODD_N * g + 4 + ODD_AT[("s", b, n)]
                to = (q_stack if n < 2 else k_stack)[:, n % 2, b * SEQ:(b + 1) * SEQ]
                dve.wait_ge(odd_ready, base + 1)
                dve.tensor_copy(to, ps_odd[:, :]).then_inc(odd_read, 1)

            low_parts(0)
            for n in range(4):
                dve.wait_ge(odd_ready, n + 1)
                dve.tensor_copy((q_stack if n < 2 else k_stack)[:, n % 2, 0:SEQ], ps_odd[:, :]).then_inc(odd_read, 1)

            def finish(g, s):
                b, qt = s // 4, QT_OF[s]
                dve.wait_ge(exp_done, GROUP1 * (SLOTS1 * g + s + 1))
                dve.reciprocal(inv_sum[:, s % 2, :], row_sum[:, s % 4, :]).then_inc(inv_done, 1)
                dve.wait_ge(inv_done, SLOTS1 * g + s + 1)
                dve.wait_ge(oT_ready, SLOTS1 * g + s + 1)
                dve.tensor_tensor(
                    o_tok[:, b * SEQ_TILES + qt, bass.ds(g * GQ, GQ)].rearrange("p (h d) -> p h d", d=HD1),
                    ps_oT[:, :].rearrange("p (h d) -> p h d", d=P)[:, :, 0:HD1],
                    inv_sum[:, s % 2, :].rearrange("p (h a) -> p h a", a=1).broadcast_to([P, GROUP1, HD1]),
                    ALU.mult).then_inc(o_done, 1)

            with dve.Fori(0, KV1) as g:
                for s in range(SLOTS1 + 2):
                    if s < SLOTS1:
                        qt = QT_OF[s]
                        n = max(qt + 1, 2) * P
                        seen = mask[:, 3 * P:5 * P] if qt == 0 else mask[:, 4 * P - n:4 * P]
                        for h in range(GROUP1):
                            dve.wait_ge(scored, GROUP1 * (SLOTS1 * g + s) + h + 1)
                            dve.memset(gate[:, h:h + 1], 0.0)
                            dve.tensor_tensor_reduce(probs[:, s % 2, h, 0:n], ps_s[h][:, 0:n], seen, 1.0, LOWEST,
                                                     ALU.add, ALU.max, row_max[:, s % 2, h:h + 1]).then_inc(masked, 1)
                        dve.wait_ge(masked, GROUP1 * (SLOTS1 * g + s + 1))
                        dve.tensor_scalar(neg_max[:, s % 2, :], row_max[:, s % 2, :], -SCALE1, None,
                                          ALU.mult).then_inc(max_done, 1)
                    if 1 <= s <= SLOTS1:
                        for kb in range(1, QT_OF[s - 1] + 1, 2):
                            dve.wait_ge(odd_ready, ODD_N * g + 4 + ODD_AT[("p", s - 1, kb)] + 1)
                            dve.tensor_copy(pT[:, kb, :], ps_odd[:, :]).then_inc(odd_read, 1)
                    if s >= 2:
                        finish(g, s - 2)
                    if s < 4:
                        read_stack(g, 1, s)
                    if s == 4:
                        low_parts(g + 1)
                    if 4 < s <= SLOTS1:
                        read_stack(g, 0, s - 5)
            for tile in range(TILES):
                at = slice(tile * P, (tile + 1) * P)
                dve.wait_ge(out_hi, tile + 1)
                dve.tensor_tensor(xT_lo[:, :, at], norm.bank(tile), xT_hi[:, :, at].bitcast(F32),
                                  ALU.subtract).then_inc(out_lo, 1)
            for tile in range(TILES):
                dve.wait_ge(y_ready, tile + 1)
                dve.tensor_tensor(rows[:, tile, :], ps_s[tile % 2][:, :], rows[:, tile, :], ALU.add).then_inc(y_added, 1)

        @block.tensor
        def _(pe):
            norm.on_tensor(pe)
            pe.wait_ge(w_lo_done, KC)
            pe.wait_ge(norm.lo_done, TILES)
            for tile in range(TILES):
                at = slice(tile * P, (tile + 1) * P)
                if tile >= 2:
                    pe.wait_ge(v_done, tile - 1)
                three(pe, ps_q[tile % 2][:, :], [(xT_hi[:, k, at], xT_lo[:, k, at], w_hi[:, k, 0:D], w_lo[:, k, 0:D])
                                                 for k in range(KC)], qkv_ready)
                three(pe, ps_kv[tile % 2][:, 0:KVW], [(xT_hi[:, k, at], xT_lo[:, k, at], w_hi[:, k, D:], w_lo[:, k, D:])
                                                      for k in range(KC)], qkv_ready)

            def stack(b, n):
                for j in range(SEQ_TILES):
                    tile = b * SEQ_TILES + j
                    if n < 2:
                        source = q_parts[:, tile, 2 * n:2 * n + 2, :, :].rearrange("p h n d -> p (h n d)")
                    else:
                        first = STACK if n == 2 else 0
                        source = k_parts[:, tile, first:first + 2 * STACK]
                    mm = pe.transpose(ps_odd[:, j * P:(j + 1) * P].bitcast(F32R), source, ident_r[:, :])
                mm.then_inc(odd_ready, 1)

            def score(g, s):
                b, qt = s // 4, QT_OF[s]
                n = max(qt + 1, 2) * P
                row = b * SEQ + qt * P
                for h in range(GROUP1):
                    if s >= 1:
                        pe.wait_ge(masked, GROUP1 * (SLOTS1 * g + s - 1) + h + 1)
                    pe.matmul(ps_s[h][:, 0:n], q_stack[:, h // 2, row:row + P], k_stack[:, h % 2, b * SEQ:b * SEQ + n],
                              start=True, stop=True).then_inc(scored, 1)

            def turn(g, s, kb):
                if kb % 2 == 0:
                    bank, ready, read, at = ps_even, even_ready, even_read, EVEN_N * g + EVEN_AT[(s, kb)]
                else:
                    bank, ready, read, at = ps_odd, odd_ready, odd_read, ODD_N * g + 4 + ODD_AT[("p", s, kb)]
                if kb % 2:
                    pe.wait_ge(read, at)
                for h in range(GROUP1):
                    mm = pe.transpose(bank[:, h * P:(h + 1) * P], probs[:, s % 2, h, kb * P:(kb + 1) * P], ident[:, :])
                mm.then_inc(ready, 1)

            def apply(g, s, kb):
                qt = QT_OF[s]
                if kb % 2 == 0:
                    pe.wait_ge(even_read, EVEN_N * g + EVEN_AT[(s, kb)] + 1)
                else:
                    pe.wait_ge(odd_read, ODD_N * g + 4 + ODD_AT[("p", s, kb)] + 1)
                mm = pe.matmul(ps_o[:, :], v_now[:, (s // 4) * SEQ_TILES + kb, :], pT[:, kb, :],
                               start=(kb == 0), stop=(kb == qt))
                if kb == qt:
                    mm.then_inc(o_ready, 1)

            def turn_out(g, s):
                pe.wait_ge(o_read, SLOTS1 * g + s + 1)
                if s >= 1:
                    pe.wait_ge(o_done, SLOTS1 * g + s)
                for h in range(GROUP1):
                    mm = pe.transpose(ps_oT[:, h * P:(h + 1) * P], oT_now[:, h * P:(h + 1) * P], ident[:, :])
                mm.then_inc(oT_ready, 1)

            pe.wait_ge(ident_done, 1)
            pe.wait_ge(part_copied, 2)
            pe.wait_ge(part_lo, 2)
            pe.wait_ge(pads_set, 6)
            for n in range(4):
                if n >= 1:
                    pe.wait_ge(odd_read, n)
                stack(0, n)
            with pe.Fori(0, KV1) as g:
                for s in range(SLOTS1 + 2):
                    if s < SLOTS1:
                        if s % 4 == 0:
                            pe.wait_ge(odd_read, ODD_N * g + 4 + (ODD_AT[("s", 1, 3)] + 1 if s else 0))
                        score(g, s)
                    if s >= 2:
                        turn_out(g, s - 2)
                    if 1 <= s <= SLOTS1:
                        last = QT_OF[s - 1]
                        pe.wait_ge(exp_done, GROUP1 * (SLOTS1 * g + s))
                        if s - 1 == 0:
                            pe.wait_ge(v_now_done, 2 * g + 1)
                        if s - 1 == 4:
                            pe.wait_ge(v_now_done, 2 * g + 2)
                        if s - 1 >= 1:
                            pe.wait_ge(o_read, SLOTS1 * g + s - 1)
                        turn(g, s - 1, 0)
                        for kb in range(last + 1):
                            if kb + 1 <= last:
                                turn(g, s - 1, kb + 1)
                            apply(g, s - 1, kb)
                    if s < 4:
                        pe.wait_ge(odd_read, ODD_N * g + 4 + ODD_AT[("s", 1, s)])
                        stack(1, s)
                    if 4 < s <= SLOTS1:
                        if s == 5:
                            pe.wait_ge(part_copied, 2 * (g + 2))
                            pe.wait_ge(part_lo, 2 * (g + 2))
                        pe.wait_ge(odd_read, ODD_N * g + 4 + ODD_AT[("s", 0, s - 5)])
                        stack(0, s - 5)
            pe.wait_ge(o_done, SLOTS1 * KV1)
            for tile in range(TILES):
                if tile >= 2:
                    pe.wait_ge(out_lo, tile - 1)
                for k in range(KC):
                    mm = pe.transpose(norm.banks[tile % 2][:, k * P:(k + 1) * P], o_tok[:, tile, k * P:(k + 1) * P],
                                      ident[:, :])
                mm.then_inc(out_turned, 1)
            pe.wait_ge(w_lo_done, 2 * KC)
            pe.wait_ge(out_lo, TILES)
            for tile in range(TILES):
                if tile >= 2:
                    pe.wait_ge(y_added, tile - 1)
                at = slice(tile * P, (tile + 1) * P)
                three(pe, ps_s[tile % 2][:, :], [(xT_hi[:, k, at], xT_lo[:, k, at], wo_hi[:, k, :], wo_lo[:, k, :])
                                                 for k in range(KC)], y_ready)


def layout1(inputs):
    qkv = np.concatenate([inputs["L1_attn_Wq"], inputs["L1_attn_Wk"], inputs["L1_attn_Wv"]], 1)
    return {"weights_qkv1": qkv.reshape(KC, P, D + 2 * KV1 * HD1), "weights_o1": inputs["L1_attn_Wo"].reshape(KC, P, D)}


def tables1():
    inv = (1.0 / 500000.0 ** (np.arange(0, HD1, 2, dtype=np.float32) / HD1)).astype(np.float32)
    ang = np.arange(SEQ, dtype=np.float32)[:, None] * inv[None, :]
    tile = lambda a: np.ascontiguousarray(a.astype(np.float32).reshape(SEQ_TILES, P, HD1).transpose(1, 0, 2))
    q, k = np.arange(P)[:, None], np.arange(P)[None, :]
    mask = np.concatenate([np.zeros((P, 3 * P)), np.where(k <= q, 0, MASKED), np.full((P, P), MASKED)], 1)
    return {"cos1": tile(np.concatenate([np.cos(ang), np.cos(ang)], 1)),
            "sin1": tile(np.concatenate([-np.sin(ang), np.sin(ang)], 1)), "mask1": mask.astype(np.float32)}


EXPERTS, RANK, GATE_H = 8, 16, 32
LORA = EXPERTS * RANK
CAPACITY = int(3.0 * TOK / EXPERTS)
ALPHA = 1.0 / RANK
SIDE = 256
SMALL = {"gb1": GATE_H, "gamma": GATE_H, "beta": GATE_H, "gw2": EXPERTS * GATE_H, "gb2": EXPERTS, "index": EXPERTS}
AHEAD = 6


def feed_forward1(nc, t, w_in, lora_b_in, small_in, out, psum):
    ctx = ExitStack()
    with ctx:
        def sb(name, shape, dt=F32):
            return ctx.enter_context(nc.sbuf_tensor("f1_" + name, shape, dt))

        sem = lambda name: ctx.enter_context(nc.semaphore("f1_" + name))
        rows, ident = t["rows"], t["ident"]
        xT_hi, xT_lo = (sb(f"xT_{n}", [P, KC, TOK], F32R) for n in ("hi", "lo"))
        w_hi, w_lo = (sb(f"w_{n}", [P, KC, D + SIDE], F32R) for n in ("hi", "lo"))
        b_hi, b_lo = (sb(f"b_{n}", [P, D], F32R) for n in ("hi", "lo"))
        staged = sb("staged", [P, KC, D + SIDE])
        b_staged = sb("b_staged", [P, D])
        small = sb("small", [P, sum(SMALL.values())])
        low = sb("low", [P, TILES, LORA])
        h = sb("h", [P, TILES, GATE_H])
        squares = sb("squares", [P, TILES, GATE_H])
        mean = sb("mean", [P, TILES])
        var = sb("var", [P, TILES])
        dev = sb("dev", [P, TILES])
        products = sb("products", [P, TILES, EXPERTS, GATE_H])
        gates = sb("gates", [P, TILES, EXPERTS])
        top = sb("top", [P, TILES, 8])
        top_index = sb("top_index", [P, TILES, 8], mybir.dt.uint32)
        top_at = sb("top_at", [P, TILES, 8])
        gap = sb("gap", [P, TILES])
        share = sb("share", [P, 2, TILES])
        total = sb("total", [P, TILES])
        chosen = sb("chosen", [P, 2, TILES, EXPERTS])
        count = sb("count", [P, 2, EXPERTS])
        allowed = sb("allowed", [P, 2, EXPERTS])
        weight = sb("weight", [P, 2, TILES, EXPERTS])
        ones = sb("ones", [P, P])
        low_T_hi, low_T_lo = (sb(f"low_T_{n}", [P, TOK], F32R) for n in ("hi", "lo"))

        names, at = {}, 0
        for name, width in SMALL.items():
            names[name] = small[:, at:at + width]
            at += width

        norm = Norm(ctx, nc, "n2", rows, ident, psum[6:8], xT_hi, xT_lo)
        last = Norm(ctx, nc, "n3", rows, ident, psum[6:8], None, None)
        ps_side, ps_y, ps_count, ps_low = psum[0:2], psum[0:6], psum[6], psum[6:8]
        weight_in, small_in_done, b_in = [sem(f"weight_in{k}") for k in range(KC)], sem("small_in"), sem("b_in")
        w_hi_done, w_lo_done = sem("w_hi_done"), sem("w_lo_done")
        side_ready, low_copied, h_copied = sem("side_ready"), sem("low_copied"), sem("h_copied")
        step_done, var_ready, dev_done, gap_ready, exp_done = (sem("step_done"), sem("var_ready"), sem("dev_done"),
                                                               sem("gap_ready"), sem("exp_done"))
        ones_set, count_ready, counted, weighted = sem("ones_set"), sem("count_ready"), sem("counted"), sem("weighted")
        low_turned, low_hi_done, low_lo_done = sem("low_turned"), sem("low_hi_done"), sem("low_lo_done")
        y_ready, y_added, stored = sem("y_ready"), sem("y_added"), sem("stored")

        block = ctx.enter_context(nc.Block())

        @block.sync
        def _(sp):
            for k in range(KC):
                sp.dma_start(staged[:, k, :], w_in[k]).then_inc(weight_in[k], 16)
            sp.dma_start(small[:, :], small_in).then_inc(small_in_done, 16)
            sp.dma_start(b_staged[:, :], lora_b_in).then_inc(b_in, 16)
            for tile in range(TILES):
                sp.wait_ge(last.normed, tile + 1)
                sp.dma_start(out[tile * P:(tile + 1) * P, :], rows[:, tile, :]).then_inc(stored, 16)
            sp.wait_ge(stored, 16 * TILES)

        @block.scalar
        def _(act):
            for k in range(KC):
                act.wait_ge(weight_in[k], 16)
                act.activation(w_hi[:, k, :], staged[:, k, :], ACT.Copy).then_inc(w_hi_done, 1)
            act.wait_ge(b_in, 16)
            act.activation(b_hi[:, :], b_staged[:, :], ACT.Copy).then_inc(w_hi_done, 1)
            norm.on_scalar(act)
            for tile in range(TILES):
                act.wait_ge(h_copied, tile + 1)
                act.activation(low[:, tile, :], ps_side[tile % 2][:, GATE_H:GATE_H + LORA],
                               ACT.Copy).then_inc(low_copied, 1)
            act.wait_ge(var_ready, 1)
            act.activation(dev[:, :], var[:, :], ACT.Sqrt, bias=norm.eps[:, 0:1],
                           scale=1.0 / GATE_H).then_inc(dev_done, 1)
            act.wait_ge(gap_ready, 1)
            act.activation(share[:, 1, :], gap[:, :], ACT.Exp).then_inc(exp_done, 1)
            for half in range(2):
                act.wait_ge(low_turned, half + 1)
                act.activation(low_T_hi[:, half * 512:(half + 1) * 512], ps_low[half][:, :], ACT.Copy).then_inc(low_hi_done, 1)
            act.wait_ge(y_added, TILES)
            last.on_scalar(act, transposed=False)

        @block.gpsimd
        def _(pool):
            pool.memset(ones[:, :], 1.0).then_inc(ones_set, 1)
            for k in range(KC):
                pool.wait_ge(w_hi_done, k + 1)
                pool.tensor_tensor(w_lo[:, k, :], staged[:, k, :], w_hi[:, k, :].bitcast(F32),
                                   ALU.subtract).then_inc(w_lo_done, 1)
            pool.wait_ge(w_hi_done, KC + 1)
            pool.tensor_tensor(b_lo[:, :], b_staged[:, :], b_hi[:, :].bitcast(F32), ALU.subtract).then_inc(w_lo_done, 1)

        @block.vector
        def _(dve):
            steps = [0]

            def step(instruction):
                steps[0] += 1
                instruction.then_inc(step_done, 1)
                dve.wait_ge(step_done, steps[0])

            def each_tile(name):
                return names[name].rearrange("p (a c) -> p a c", a=1).broadcast_to([P, TILES, SMALL[name]])

            def each_column(ap, n):
                return ap.rearrange("p (t a) -> p t a", a=1).broadcast_to([P, TILES, n])

            norm.on_vector(dve)
            for tile in range(TILES):
                dve.wait_ge(side_ready, tile + 1)
                dve.tensor_copy(h[:, tile, :], ps_side[tile % 2][:, 0:GATE_H]).then_inc(h_copied, 1)
            dve.wait_ge(small_in_done, 16)
            dve.wait_ge(h_copied, TILES)
            step(dve.tensor_tensor(h[:, :, :], h[:, :, :], each_tile("gb1"), ALU.add))
            step(dve.tensor_reduce(mean[:, :], h[:, :, :], mybir.AxisListType.X, ALU.add))
            step(dve.tensor_scalar(mean[:, :], mean[:, :], 1.0 / GATE_H, None, ALU.mult))
            step(dve.tensor_tensor(h[:, :, :], h[:, :, :], each_column(mean[:, :], GATE_H), ALU.subtract))
            step(dve.tensor_tensor(squares[:, :, :], h[:, :, :], h[:, :, :], ALU.mult))
            dve.tensor_reduce(var[:, :], squares[:, :, :], mybir.AxisListType.X, ALU.add).then_inc(var_ready, 1)
            dve.wait_ge(dev_done, 1)
            step(dve.reciprocal(dev[:, :], dev[:, :]))
            step(dve.tensor_tensor(h[:, :, :], h[:, :, :], each_column(dev[:, :], GATE_H), ALU.mult))
            step(dve.tensor_tensor(h[:, :, :], h[:, :, :], each_tile("gamma"), ALU.mult))
            step(dve.tensor_tensor(h[:, :, :], h[:, :, :], each_tile("beta"), ALU.add))
            step(dve.tensor_scalar(h[:, :, :], h[:, :, :], 0.0, None, ALU.max))
            for e in range(EXPERTS):
                row = names["gw2"][:, e * GATE_H:(e + 1) * GATE_H].rearrange("p (a c) -> p a c", a=1)
                mult = dve.tensor_tensor(products[:, :, e, :], h[:, :, :], row.broadcast_to([P, TILES, GATE_H]), ALU.mult)
            step(mult)
            step(dve.tensor_reduce(gates[:, :, :].rearrange("p t e -> p (t e)"),
                                   products[:, :, :, :].rearrange("p t e c -> p (t e) c"),
                                   mybir.AxisListType.X, ALU.add))
            step(dve.tensor_tensor(gates[:, :, :], gates[:, :, :], each_tile("gb2"), ALU.add))
            for tile in range(TILES):
                found = dve.max(top[:, tile, :], gates[:, tile, :])
            step(found)
            for tile in range(TILES):
                found = dve.max_index(top_index[:, tile, :], top[:, tile, :], gates[:, tile, :])
            step(found)
            step(dve.tensor_copy(top_at[:, :, :], top_index[:, :, :]))
            dve.tensor_tensor(gap[:, :], top[:, :, 1], top[:, :, 0], ALU.subtract).then_inc(gap_ready, 1)
            for n in range(2):
                found = dve.tensor_tensor(chosen[:, n, :, :], each_column(top_at[:, :, n], EXPERTS), each_tile("index"),
                                          ALU.is_equal)
            step(found)
            dve.tensor_reduce(count[:, :, :].rearrange("p n e -> p (n e)"),
                              chosen[:, :, :, :].rearrange("p n t e -> p n e t"), mybir.AxisListType.X,
                              ALU.add).then_inc(count_ready, 1)
            dve.wait_ge(exp_done, 1)
            step(dve.tensor_scalar(total[:, :], share[:, 1, :], 1.0, None, ALU.add))
            step(dve.reciprocal(share[:, 0, :], total[:, :]))
            step(dve.tensor_tensor(share[:, 1, :], share[:, 1, :], share[:, 0, :], ALU.mult))
            dve.wait_ge(counted, 1)
            step(dve.tensor_scalar(allowed[:, :, :].rearrange("p n e -> p (n e)"), ps_count[:, 0:2 * EXPERTS],
                                   float(CAPACITY), ALPHA, ALU.is_le, ALU.mult))
            for n in range(2):
                found = dve.tensor_tensor(weight[:, n, :, :], chosen[:, n, :, :], each_column(share[:, n, :], EXPERTS),
                                          ALU.mult)
            step(found)
            for n in range(2):
                found = dve.tensor_tensor(weight[:, n, :, :], weight[:, n, :, :],
                                          allowed[:, n, :].rearrange("p (a e) -> p a e", a=1).broadcast_to(
                                              [P, TILES, EXPERTS]), ALU.mult)
            step(found)
            step(dve.tensor_tensor(weight[:, 0, :, :], weight[:, 0, :, :], weight[:, 1, :, :], ALU.add))
            dve.wait_ge(low_copied, TILES)
            by_expert = low[:, :, :].rearrange("p t (e r) -> p (t e) r", r=RANK)
            dve.tensor_tensor(by_expert, by_expert,
                              weight[:, 0, :, :].rearrange("p t (e a) -> p (t e) a", a=1).broadcast_to(
                                  [P, TILES * EXPERTS, RANK]), ALU.mult).then_inc(weighted, 1)
            for half in range(2):
                dve.wait_ge(low_hi_done, half + 1)
                cols = slice(half * 512, (half + 1) * 512)
                dve.tensor_tensor(low_T_lo[:, cols], ps_low[half][:, :], low_T_hi[:, cols].bitcast(F32),
                                  ALU.subtract).then_inc(low_lo_done, 1)
            for tile in range(TILES):
                dve.wait_ge(y_ready, tile + 1)
                dve.tensor_tensor(rows[:, tile, :], ps_y[tile % AHEAD][:, :], rows[:, tile, :], ALU.add).then_inc(y_added, 1)
            dve.wait_ge(y_added, TILES)
            last.on_vector(dve, transposed=False)

        @block.tensor
        def _(pe):
            norm.on_tensor(pe)
            pe.wait_ge(w_lo_done, KC)
            pe.wait_ge(norm.lo_done, TILES)
            for tile in range(TILES):
                if tile >= 2:
                    pe.wait_ge(low_copied, tile - 1)
                at = slice(tile * P, (tile + 1) * P)
                three(pe, ps_side[tile % 2][:, 0:SIDE], [(xT_hi[:, k, at], xT_lo[:, k, at], w_hi[:, k, D:], w_lo[:, k, D:])
                                                         for k in range(KC)], side_ready)

            def dense(tile):
                at = slice(tile * P, (tile + 1) * P)
                for k in range(KC):
                    for a, b in ((xT_hi, w_hi), (xT_hi, w_lo), (xT_lo, w_hi)):
                        pe.matmul(ps_y[tile % AHEAD][:, :], a[:, k, at], b[:, k, 0:D],
                                  start=(k == 0 and a is xT_hi and b is w_hi), stop=False)

            def low_rank(tile):
                at = slice(tile * P, (tile + 1) * P)
                for a, b in ((low_T_hi, b_hi), (low_T_hi, b_lo), (low_T_lo, b_hi)):
                    mm = pe.matmul(ps_y[tile % AHEAD][:, :], a[:, at], b[:, :], start=False, stop=(a is low_T_lo))
                mm.then_inc(y_ready, 1)

            pe.wait_ge(low_copied, TILES)
            for tile in range(AHEAD):
                dense(tile)
            pe.wait_ge(ones_set, 1)
            pe.wait_ge(count_ready, 1)
            pe.matmul(ps_count[:, 0:2 * EXPERTS], ones[:, :], count[:, :, :].rearrange("p n e -> p (n e)"),
                      start=True, stop=True).then_inc(counted, 1)
            pe.wait_ge(weighted, 1)
            for half in range(2):
                for j in range(4):
                    mm = pe.transpose(ps_low[half][:, j * P:(j + 1) * P], low[:, 4 * half + j, :], ident[:, :])
                mm.then_inc(low_turned, 1)
            pe.wait_ge(w_lo_done, KC + 1)
            pe.wait_ge(low_lo_done, 2)
            for tile in range(AHEAD):
                low_rank(tile)
            for tile in range(AHEAD, TILES):
                pe.wait_ge(y_added, tile - AHEAD + 1)
                dense(tile)
                low_rank(tile)


def layout_ffn1(inputs):
    low = inputs["L1_ffn_lora_A"].transpose(1, 0, 2).reshape(D, LORA)
    pad = np.zeros((D, SIDE - GATE_H - LORA), np.float32)
    w = np.concatenate([inputs["L1_ffn_weight"].T, inputs["L1_ffn_gw1"].T, low, pad], 1)
    small = np.concatenate([inputs["L1_ffn_gb1"], inputs["L1_ffn_ln_gamma"], inputs["L1_ffn_ln_beta"],
                            inputs["L1_ffn_gw2"].reshape(-1), inputs["L1_ffn_gb2"],
                            np.arange(EXPERTS, dtype=np.float32)])
    return {"weights_f1": w.reshape(KC, P, D + SIDE), "lora_b": inputs["L1_ffn_lora_B"].reshape(LORA, D),
            "small_f1": np.ascontiguousarray(np.broadcast_to(small, (P, small.size)))}


def program(nc, a, out):
    with ExitStack() as ctx:
        rows = ctx.enter_context(nc.sbuf_tensor("rows", [P, TILES, D], F32))
        ident = ctx.enter_context(nc.sbuf_tensor("identity", [P, P], F32))
        psum = [ctx.enter_context(nc.psum_tensor(f"bank{n}", [P, 512], F32)) for n in range(8)]
        x_stage = rows[:, :, :].rearrange("p t d -> p (t d)").rearrange("p (k c) -> p k c", k=KC)
        t = {"rows": rows, "ident": ident, "x_stage": x_stage}
        attention0(nc, t, a["x_T"], a["weights0"], a["x_rows"], a["cos0"], a["sin0"], a["mask0"], a["ident"], psum)
        feed_forward0(nc, t, a["weights_f0"], psum)
        attention1(nc, t, a["weights_qkv1"], a["weights_o1"], a["cos1"], a["sin1"], a["mask1"], psum)
        feed_forward1(nc, t, a["weights_f1"], a["lora_b"], a["small_f1"], out, psum)


def kernel(**inputs):
    from concourse import bacc
    from concourse.bass_utils import run_bass_kernel_spmd

    inputs = {k: np.asarray(v) for k, v in inputs.items()}
    arrays = {**layout0(inputs), **tables0(), **layout_ffn0(inputs), **layout1(inputs), **tables1(), **layout_ffn1(inputs)}
    arrays = {k: np.ascontiguousarray(v) for k, v in arrays.items()}
    nc = bacc.Bacc("TRN2", target_bir_lowering=False, num_devices=1)
    args = {k: nc.dram_tensor(k, v.shape, F32, kind="ExternalInput").ap() for k, v in arrays.items()}
    out = nc.dram_tensor("out", (TOK, D), F32, kind="ExternalOutput").ap()
    program(nc, args, out)
    result = run_bass_kernel_spmd(nc, [arrays], core_ids=[0])
    return result.results[0]["out"].reshape(BATCH, SEQ, D)
```

```python
from contextlib import ExitStack

import numpy as np

import concourse.bass as bass
from concourse import mybir
from concourse.alu_op_type import AluOpType as ALU

F32 = mybir.dt.float32
F32R = mybir.dt.float32r
BF16 = mybir.dt.bfloat16
ACT = mybir.ActivationFunctionType

P = 128
BATCH, SEQ, D = 2, 512, 512
TOK = BATCH * SEQ
TILES = TOK // P
SEQ_TILES = SEQ // P
KC = D // P
EPS = 1e-5
MASKED = -1e30
LOWEST = -3e38

HEADS0, KV0, HD0 = 32, 8, 128
GROUP0 = HEADS0 // KV0
SCALE0 = HD0 ** -0.5
PAIRS = KV0 // 2
WEIGHT_ORDER = [
    (1, "k", 1, 0), (1, "q", 1, 0), (2, "q", 1, 1), (2, "q", 1, 2), (3, "q", 1, 3),
    (3, "o", 1, 0), (4, "o", 1, 1), (4, "o", 1, 2), (5, "o", 1, 3),
    (6, "v", 0, 0), (7, "v", 1, 0), (9, "k", 0, 0), (9, "q", 0, 0), (10, "q", 0, 1), (10, "q", 0, 2),
    (11, "q", 0, 3), (12, "o", 0, 0), (13, "o", 0, 1), (14, "o", 0, 2), (15, "o", 0, 3),
]
PER_PAIR = len(WEIGHT_ORDER)
FIRST_OF_NEXT = 9
HEAD_START = PER_PAIR - FIRST_OF_NEXT
WEIGHT_AT = {w[1:]: n for n, w in enumerate(WEIGHT_ORDER)}
SLOTS = 16
PIECES = {0: ["k", 0], 1: [1, 2], 2: [3], 3: []}


def weights_done(pair, kind, g, h=0):
    n = WEIGHT_AT[(kind, g, h)]
    if n >= FIRST_OF_NEXT:
        return pair * PER_PAIR + n - FIRST_OF_NEXT + 1
    return pair * PER_PAIR + HEAD_START + n + 1


def piece_index(unit, piece):
    return 5 * unit + (0 if piece == "k" else piece + 1)


def key_tiles(qt):
    return (0, 1) if qt == 0 else (qt - 1, 2)


def blocks_before(s):
    return (s // 4) * 7 + (0, 1, 3, 5)[s % 4]


def three(pe, out, terms, done):
    steps = [(a, b) for a_hi, a_lo, b_hi, b_lo in terms for a, b in ((a_hi, b_hi), (a_hi, b_lo), (a_lo, b_hi))]
    for n, (a, b) in enumerate(steps):
        mm = pe.matmul(out, a, b, start=(n == 0), stop=(n == len(steps) - 1))
    mm.then_inc(done, 1)


def attention0(nc, t, x_T, weight_stream, x_rows, cos_T, sin_T, masks, ident_in, psum):
    ctx = ExitStack()
    with ctx:
        def sb(name, shape, dt=F32):
            return ctx.enter_context(nc.sbuf_tensor(name, shape, dt))

        sem = lambda name: ctx.enter_context(nc.semaphore(name))

        xT_hi = sb("xT_hi", [P, KC, TOK], F32R)
        xT_lo = sb("xT_lo", [P, KC, TOK], F32R)
        wq_hi, wq_lo = (sb(f"wq_{n}", [P, GROUP0, KC, P], F32R) for n in ("hi", "lo"))
        wk_hi, wk_lo = (sb(f"wk_{n}", [P, KC, P], F32R) for n in ("hi", "lo"))
        wv_hi, wv_lo = (sb(f"wv_{n}", [P, KC, 2, P], F32R) for n in ("hi", "lo"))
        wo_hi, wo_lo = (sb(f"wo_{n}", [P, 2, GROUP0, D], F32R) for n in ("hi", "lo"))
        staged = sb("staged", [P, 2, 512])
        qT_hi, qT_lo = (sb(f"qT_{n}", [P, 2, GROUP0, SEQ], F32R) for n in ("hi", "lo"))
        kT_hi, kT_lo = (sb(f"kT_{n}", [P, 2, SEQ], F32R) for n in ("hi", "lo"))
        v_hi, v_lo = (sb(f"v_{n}", [P, TILES, 2 * P], F32R) for n in ("hi", "lo"))
        probs = sb("probs", [P, 2, GROUP0, 2 * P])
        pT_hi, pT_lo = (sb(f"pT_{n}", [P, 2, GROUP0 * P], F32R) for n in ("hi", "lo"))
        oT_hi, oT_lo = (sb(f"oT_{n}", [P, 2, GROUP0 * P], F32R) for n in ("hi", "lo"))
        cos = sb("cos", [P, SEQ])
        sin = sb("sin", [P, SEQ])
        mask = sb("mask", [P, 3 * P])
        turned = sb("turned", [P, 2, SEQ])
        by_cos = sb("by_cos", [P, 2, SEQ])
        row_max = sb("row_max", [P, 2, GROUP0])
        neg_max = sb("neg_max", [P, 2, GROUP0])
        row_sum = sb("row_sum", [P, 2, GROUP0])
        inv_sum = sb("inv_sum", [P, 2, GROUP0])
        gate = sb("gate", [P, 2])
        rows, ident = t["rows"], t["ident"]

        ps_s, ps_a, ps_t = psum[0:2], psum[2:4], psum[4:6]
        ps_o, ps_y = psum[6], psum[7]

        constants_in = sem("constants_in")
        xT_in = [sem(f"xT_in{k}") for k in range(KC)]
        weight_in = [sem("weight_in0"), sem("weight_in1")]
        xT_hi_done, xT_lo_done = sem("xT_hi_done"), sem("xT_lo_done")
        weight_hi_done, weight_lo_done = sem("weight_hi_done"), sem("weight_lo_done")
        projected = sem("projected")
        turned_done, sin_done, cos_done = sem("turned_done"), sem("sin_done"), sem("cos_done")
        roped, rope_hi, rope_lo = sem("roped"), sem("rope_hi"), sem("rope_lo")
        v_ready, v_hi_done, v_lo_done = sem("v_ready"), sem("v_hi_done"), sem("v_lo_done")
        scored, masked, max_done = sem("scored"), sem("masked"), sem("max_done")
        exp_done, inv_done, probs_done = sem("exp_done"), sem("inv_done"), sem("probs_done")
        pT_ready, pT_hi_done, pT_lo_done = sem("pT_ready"), sem("pT_hi_done"), sem("pT_lo_done")
        o_ready, o_hi_done, o_lo_done = sem("o_ready"), sem("o_hi_done"), sem("o_lo_done")
        y_ready, y_added = sem("y_ready"), sem("y_added")

        def weight_dest(n, hi):
            _, kind, g, h = WEIGHT_ORDER[n]
            if kind == "q":
                return (wq_hi if hi else wq_lo)[:, h, :, :]
            if kind == "k":
                return (wk_hi if hi else wk_lo)[:, :, :]
            if kind == "v":
                return (wv_hi if hi else wv_lo)[:, :, g, :]
            return (wo_hi if hi else wo_lo)[:, g, h, :]

        def staged_as(n, slot):
            v = staged[:, slot, :]
            return v if WEIGHT_ORDER[n][1] == "o" else v.rearrange("p (k c) -> p k c", k=KC)

        block = ctx.enter_context(nc.Block())

        @block.sync
        def _(sp):
            for k in range(KC):
                sp.dma_start(t["x_stage"][:, k, :],
                             x_T[k * P:(k + 1) * P, :]).then_inc(xT_in[k], 16)
            for n in range(HEAD_START):
                if n >= 2:
                    sp.wait_ge(weight_lo_done, n - 1)
                sp.dma_start(staged[:, n % 2, :], weight_stream[n]).then_inc(weight_in[n % 2], 16)
            sp.dma_start(cos[:, :], cos_T).then_inc(constants_in, 16)
            sp.dma_start(sin[:, :], sin_T).then_inc(constants_in, 16)
            sp.dma_start(mask[:, :], masks).then_inc(constants_in, 16)
            sp.dma_start(ident[:, :], ident_in).then_inc(constants_in, 16)
            sp.wait_ge(xT_lo_done, 2 * KC)
            sp.dma_start(rows[:, :, :], x_rows.rearrange("(t p) d -> p t d", p=P)).then_inc(constants_in, 16)
            with sp.Fori(0, PAIRS) as i:
                for n in range(PER_PAIR):
                    sp.wait_ge(weight_lo_done, i * PER_PAIR + HEAD_START + n - 1)
                    sp.dma_start(staged[:, (HEAD_START + n) % 2, :],
                                 weight_stream[bass.ds(i * PER_PAIR + HEAD_START + n, 1), :, :].rearrange(
                                     "a p c -> p (a c)")).then_inc(weight_in[(HEAD_START + n) % 2], 16)

        def loads(i, n):
            m = HEAD_START + n
            return i * (PER_PAIR // 2) * 16 + (m // 2 + 1) * 16, m % 2

        @block.scalar
        def _(act):
            for k in range(KC):
                act.wait_ge(xT_in[k], 16)
                for half in range(BATCH):
                    cols = slice(half * SEQ, (half + 1) * SEQ)
                    act.activation(xT_hi[:, k, cols], t["x_stage"][:, k, cols], ACT.Copy).then_inc(xT_hi_done, 1)
            for m in range(HEAD_START):
                act.wait_ge(weight_in[m % 2], (m // 2 + 1) * 16)
                n = m + FIRST_OF_NEXT
                act.activation(weight_dest(n, True), staged_as(n, m % 2), ACT.Copy).then_inc(weight_hi_done, 1)

            def turn(i, a):
                act.wait_ge(projected, 20 * i + a + 1)
                if a >= 2:
                    act.wait_ge(rope_lo, 20 * i + a - 1)
                half = HD0 // 2
                act.activation(turned[0:half, a % 2, :], ps_a[a % 2][half:P, :], ACT.Copy).then_inc(turned_done, 1)
                act.activation(turned[half:P, a % 2, :], ps_a[a % 2][0:half, :], ACT.Copy).then_inc(turned_done, 1)

            def rope_high(i, a):
                u, piece = a // 5, a % 5
                dest = kT_hi[:, u % 2, :] if piece == 0 else qT_hi[:, u % 2, piece - 1, :]
                act.wait_ge(roped, 20 * i + a + 1)
                act.activation(dest, turned[:, a % 2, :], ACT.Copy).then_inc(rope_hi, 1)

            with act.Fori(0, PAIRS) as i:
                for a in range(5):
                    if a >= 1:
                        rope_high(i, a - 1)
                    turn(i, a)
                rope_high(i, 4)
                for tile in range(TILES):
                    act.wait_ge(v_ready, TILES * i + tile + 1)
                    act.activation(v_hi[:, tile, :], ps_t[tile % 2][:, 0:2 * P], ACT.Copy).then_inc(v_hi_done, 1)
                for s in range(SLOTS + 1):
                    u, qt = divmod(s, 4)
                    if s >= 1:
                        for kb in range(key_tiles((s - 1) % 4)[1]):
                            act.wait_ge(pT_ready, 28 * i + blocks_before(s - 1) + kb + 1)
                            act.activation(pT_hi[:, kb, :], ps_t[kb][:, :], ACT.Copy).then_inc(pT_hi_done, 1)
                    if s < SLOTS:
                        act.wait_ge(max_done, 16 * i + s + 1)
                        for h in range(GROUP0):
                            act.activation(probs[:, s % 2, h, :], probs[:, s % 2, h, :], ACT.Exp,
                                           bias=neg_max[:, s % 2, h:h + 1], scale=SCALE0,
                                           accum_out=row_sum[:, s % 2, h:h + 1]).then_inc(exp_done, 1)
                    if 1 <= s < 13:
                        before = (s - 1) // 4
                        for piece in PIECES[(s - 1) % 4]:
                            rope_high(i, piece_index(before + 1, piece))
                    if s < 12:
                        for piece in PIECES[qt]:
                            turn(i, piece_index(u + 1, piece))
                    if s >= 1:
                        act.wait_ge(o_ready, 16 * i + s)
                        act.activation(oT_hi[:, (s - 1) % 2, :], ps_o[:, :], ACT.Copy).then_inc(o_hi_done, 1)
                    for n, (slot, kind, g, h) in enumerate(WEIGHT_ORDER):
                        if slot != s:
                            continue
                        if kind == "v":
                            act.wait_ge(v_ready, TILES * (i + 1))
                        elif kind == "o" and g == 0:
                            act.wait_ge(y_ready, 16 * i + 8)
                        elif kind == "o":
                            pass
                        else:
                            last = piece_index(1 if g == 1 else 3, "k" if kind == "k" else h)
                            act.wait_ge(projected, 20 * i + last + 1)
                        count, stage = loads(i, n)
                        act.wait_ge(weight_in[stage], count)
                        act.activation(weight_dest(n, True), staged_as(n, stage), ACT.Copy).then_inc(weight_hi_done, 1)

        @block.gpsimd
        def _(pool):
            for m in range(HEAD_START):
                n = m + FIRST_OF_NEXT
                pool.wait_ge(weight_hi_done, m + 1)
                pool.tensor_tensor(weight_dest(n, False), staged_as(n, m % 2), weight_dest(n, True).bitcast(F32),
                                   ALU.subtract).then_inc(weight_lo_done, 1)
            pool.wait_ge(constants_in, 80)

            def rotate(i, a):
                pool.wait_ge(turned_done, 2 * (20 * i + a + 1))
                pool.tensor_tensor(turned[:, a % 2, :], turned[:, a % 2, :], sin[:, :], ALU.mult).then_inc(sin_done, 1)
                pool.wait_ge(sin_done, 20 * i + a + 1)
                pool.wait_ge(cos_done, 20 * i + a + 1)
                pool.tensor_tensor(turned[:, a % 2, :], turned[:, a % 2, :], by_cos[:, a % 2, :],
                                   ALU.add).then_inc(roped, 1)

            with pool.Fori(0, PAIRS) as i:
                for a in range(5):
                    rotate(i, a)
                for s in range(SLOTS):
                    if s < 12:
                        for piece in PIECES[s % 4]:
                            rotate(i, piece_index(s // 4 + 1, piece))
                    for n, (slot, *_rest) in enumerate(WEIGHT_ORDER):
                        if slot == s:
                            count, stage = loads(i, n)
                            pool.wait_ge(weight_hi_done, i * PER_PAIR + HEAD_START + n + 1)
                            pool.tensor_tensor(weight_dest(n, False), staged_as(n, stage),
                                               weight_dest(n, True).bitcast(F32),
                                               ALU.subtract).then_inc(weight_lo_done, 1)

        @block.vector
        def _(dve):
            for k in range(KC):
                for half in range(BATCH):
                    cols = slice(half * SEQ, (half + 1) * SEQ)
                    dve.wait_ge(xT_hi_done, 2 * k + half + 1)
                    dve.tensor_tensor(xT_lo[:, k, cols], t["x_stage"][:, k, cols],
                                      xT_hi[:, k, cols].bitcast(F32), ALU.subtract).then_inc(xT_lo_done, 1)
            dve.wait_ge(constants_in, 80)

            def times_cos(i, a):
                dve.wait_ge(turned_done, 2 * (20 * i + a + 1))
                if a >= 2:
                    dve.wait_ge(roped, 20 * i + a - 1)
                dve.tensor_tensor(by_cos[:, a % 2, :], ps_a[a % 2][:, :], cos[:, :], ALU.mult).then_inc(cos_done, 1)

            def rope_low(i, a):
                u, piece = a // 5, a % 5
                hi = kT_hi[:, u % 2, :] if piece == 0 else qT_hi[:, u % 2, piece - 1, :]
                lo = kT_lo[:, u % 2, :] if piece == 0 else qT_lo[:, u % 2, piece - 1, :]
                dve.wait_ge(rope_hi, 20 * i + a + 1)
                dve.tensor_tensor(lo, turned[:, a % 2, :], hi.bitcast(F32), ALU.subtract).then_inc(rope_lo, 1)

            with dve.Fori(0, PAIRS) as i:
                for a in range(5):
                    if a >= 1:
                        rope_low(i, a - 1)
                    times_cos(i, a)
                rope_low(i, 4)
                for tile in range(TILES):
                    dve.wait_ge(v_hi_done, TILES * i + tile + 1)
                    dve.tensor_tensor(v_lo[:, tile, :], ps_t[tile % 2][:, 0:2 * P],
                                      v_hi[:, tile, :].bitcast(F32), ALU.subtract).then_inc(v_lo_done, 1)
                for s in range(SLOTS + 2):
                    u, qt = divmod(s, 4)
                    if s < SLOTS:
                        seen = mask[:, P:3 * P] if qt == 0 else mask[:, 0:2 * P]
                        for h in range(GROUP0):
                            if h % 2 == 0:
                                dve.wait_ge(scored, 2 * (16 * i + s) + h // 2 + 1)
                                dve.memset(gate[:, h // 2:h // 2 + 1], 0.0)
                            dve.tensor_tensor_reduce(
                                probs[:, s % 2, h, :], ps_s[h // 2][:, (h % 2) * 2 * P:(h % 2 + 1) * 2 * P], seen,
                                1.0, LOWEST, ALU.add, ALU.max, row_max[:, s % 2, h:h + 1]).then_inc(masked, 1)
                        dve.wait_ge(masked, 4 * (16 * i + s + 1))
                        dve.tensor_scalar(neg_max[:, s % 2, :], row_max[:, s % 2, :], -SCALE0, None,
                                          ALU.mult).then_inc(max_done, 1)
                    if 1 <= s <= SLOTS:
                        for kb in range(key_tiles((s - 1) % 4)[1]):
                            dve.wait_ge(pT_hi_done, 28 * i + blocks_before(s - 1) + kb + 1)
                            dve.tensor_tensor(pT_lo[:, kb, :], ps_t[kb][:, :], pT_hi[:, kb, :].bitcast(F32),
                                              ALU.subtract).then_inc(pT_lo_done, 1)
                    if s < SLOTS:
                        dve.wait_ge(exp_done, 4 * (16 * i + s + 1))
                        dve.reciprocal(inv_sum[:, s % 2, :], row_sum[:, s % 2, :]).then_inc(inv_done, 1)
                        dve.wait_ge(inv_done, 16 * i + s + 1)
                        for h in range(GROUP0):
                            dve.tensor_scalar(probs[:, s % 2, h, :], probs[:, s % 2, h, :],
                                              inv_sum[:, s % 2, h:h + 1], None, ALU.mult).then_inc(probs_done, 1)
                    if 1 <= s < 13:
                        before = (s - 1) // 4
                        for piece in PIECES[(s - 1) % 4]:
                            rope_low(i, piece_index(before + 1, piece))
                    if s < 12:
                        for piece in PIECES[qt]:
                            times_cos(i, piece_index(u + 1, piece))
                    if 1 <= s <= SLOTS:
                        dve.wait_ge(o_hi_done, 16 * i + s)
                        dve.tensor_tensor(oT_lo[:, (s - 1) % 2, :], ps_o[:, :],
                                          oT_hi[:, (s - 1) % 2, :].bitcast(F32), ALU.subtract).then_inc(o_lo_done, 1)
                    if s >= 2:
                        b, tile = ((s - 2) // 4) % 2, (s - 2) % 4
                        row = rows[:, b * SEQ_TILES + tile, :]
                        dve.wait_ge(y_ready, 16 * i + s - 1)
                        dve.tensor_tensor(row, ps_y[:, :], row, ALU.add).then_inc(y_added, 1)

        @block.tensor
        def _(pe):
            def project(i, u, piece):
                a = piece_index(u, piece)
                g, b = divmod(u, 2)
                cols = slice(b * SEQ, (b + 1) * SEQ)
                pe.wait_ge(weight_lo_done, weights_done(i, "k" if piece == "k" else "q", g, 0 if piece == "k" else piece))
                if a >= 2:
                    pe.wait_ge(cos_done, 20 * i + a - 1)
                w = (wk_hi, wk_lo) if piece == "k" else (wq_hi[:, piece, :, :], wq_lo[:, piece, :, :])
                three(pe, ps_a[a % 2][:, :], [(w[0][:, k, :], w[1][:, k, :], xT_hi[:, k, cols], xT_lo[:, k, cols])
                                          for k in range(KC)], projected)

            def values(i, tile):
                if tile == 0:
                    pe.wait_ge(weight_lo_done, weights_done(i, "v", 1))
                if tile >= 2:
                    pe.wait_ge(v_lo_done, TILES * i + tile - 1)
                at = slice(tile * P, (tile + 1) * P)
                three(pe, ps_t[tile % 2][:, 0:2 * P],
                      [(xT_hi[:, k, at], xT_lo[:, k, at], wv_hi[:, k, :, :].rearrange("p g c -> p (g c)"),
                        wv_lo[:, k, :, :].rearrange("p g c -> p (g c)")) for k in range(KC)], v_ready)

            def scores(i, s):
                u, qt = divmod(s, 4)
                first, _ = key_tiles(qt)
                keys = slice(first * P, (first + 2) * P)
                at = slice(qt * P, (qt + 1) * P)
                for pair in range(2):
                    if s >= 1:
                        pe.wait_ge(masked, 4 * (16 * i + s - 1) + 2 * pair + 2)
                    for h in (2 * pair, 2 * pair + 1):
                        if qt == 0:
                            pe.wait_ge(rope_lo, 20 * i + piece_index(u, h) + 1)
                        steps = [(qT_hi, kT_hi), (qT_hi, kT_lo), (qT_lo, kT_hi)]
                        for n, (q, k) in enumerate(steps):
                            mm = pe.matmul(ps_s[pair][:, (h % 2) * 2 * P:(h % 2 + 1) * 2 * P], q[:, u % 2, h, at],
                                           k[:, u % 2, keys], start=(n == 0), stop=(n == 2))
                    mm.then_inc(scored, 1)

            def turn_probs(i, s):
                pe.wait_ge(probs_done, 4 * (16 * i + s + 1))
                if s == 0:
                    pe.wait_ge(v_lo_done, TILES * (i + 1))
                for kb in range(key_tiles(s % 4)[1]):
                    for h in range(GROUP0):
                        mm = pe.transpose(ps_t[kb][:, h * P:(h + 1) * P], probs[:, s % 2, h, kb * P:(kb + 1) * P],
                                          ident[:, :])
                    mm.then_inc(pT_ready, 1)

            def apply_probs(i, s):
                u, qt = divmod(s, 4)
                g, b = divmod(u, 2)
                first, count = key_tiles(qt)
                if s >= 1:
                    pe.wait_ge(o_lo_done, 16 * i + s)
                terms = []
                for kb in range(count):
                    tile = b * SEQ_TILES + first + kb
                    at = slice(g * P, (g + 1) * P)
                    terms.append((kb, v_hi[:, tile, at], v_lo[:, tile, at], pT_hi[:, kb, :], pT_lo[:, kb, :]))
                pe.wait_ge(pT_lo_done, 28 * i + blocks_before(s) + count)
                three(pe, ps_o[:, :], [x[1:] for x in terms], o_ready)

            def project_out(i, s):
                g = s // 8
                pe.wait_ge(weight_lo_done, weights_done(i, "o", g, GROUP0 - 1))
                pe.wait_ge(o_lo_done, 16 * i + s + 1)
                if s >= 1:
                    pe.wait_ge(y_added, 16 * i + s)
                three(pe, ps_y[:, :], [(oT_hi[:, s % 2, h * P:(h + 1) * P], oT_lo[:, s % 2, h * P:(h + 1) * P],
                                    wo_hi[:, g, h, :], wo_lo[:, g, h, :]) for h in range(GROUP0)], y_ready)

            pe.wait_ge(xT_lo_done, 2 * KC)
            pe.wait_ge(constants_in, 80)
            with pe.Fori(0, PAIRS) as i:
                for piece in ("k", 0, 1, 2, 3):
                    project(i, 0, piece)
                for tile in range(TILES):
                    values(i, tile)
                for s in range(SLOTS + 2):
                    u, qt = divmod(s, 4)
                    if s < SLOTS:
                        scores(i, s)
                    if 1 <= s <= SLOTS:
                        turn_probs(i, s - 1)
                    if s < 12:
                        for piece in PIECES[qt]:
                            project(i, u + 1, piece)
                    if 1 <= s <= SLOTS:
                        apply_probs(i, s - 1)
                    if s >= 2:
                        project_out(i, s - 2)


def layout0(inputs):
    x = inputs["L0_attn_x"].reshape(TOK, D)
    wq = inputs["L0_attn_wq"].reshape(KC, P, KV0, GROUP0, HD0)
    wk = inputs["L0_attn_wk"].reshape(KC, P, KV0, HD0)
    wv = inputs["L0_attn_wv"].reshape(KC, P, KV0, HD0)
    wo = inputs["L0_attn_wo"].reshape(KV0, GROUP0, P, D)
    blocks = []
    def add(pair, n):
        _, kind, g, h = WEIGHT_ORDER[n]
        kv = 2 * pair + g
        if kind == "o":
            blocks.append(wo[kv, h])
        else:
            w = {"q": wq[:, :, kv, h, :] if kind == "q" else None, "k": wk[:, :, kv], "v": wv[:, :, kv]}[kind]
            blocks.append(w.transpose(1, 0, 2).reshape(P, 512))
    for n in range(FIRST_OF_NEXT, PER_PAIR):
        add(0, n)
    for pair in range(PAIRS):
        for n in range(PER_PAIR):
            add(pair if n < FIRST_OF_NEXT else (pair + 1) % PAIRS, n)
    return {"x_T": np.ascontiguousarray(x.T), "x_rows": x, "weights0": np.stack(blocks)}


def tables0():
    half = HD0 // 2
    inv = 10000.0 ** (-np.arange(half, dtype=np.float32) / half)
    ang = (np.arange(SEQ, dtype=np.float32)[:, None] * inv[None, :].astype(np.float32)).T
    cos = np.concatenate([np.cos(ang), np.cos(ang)]).astype(np.float32)
    sin = np.concatenate([-np.sin(ang), np.sin(ang)]).astype(np.float32)
    q, k = np.arange(P)[:, None], np.arange(P)[None, :]
    mask = np.concatenate([np.where(k > q, 0, MASKED), np.where(k <= q, 0, MASKED), np.full((P, P), MASKED)], 1)
    return {"cos0": cos, "sin0": sin, "mask0": mask.astype(np.float32), "ident": np.eye(P, dtype=np.float32)}

F0 = 1376
F_TILES = -(-F0 // P)


class Norm:

    def __init__(self, ctx, nc, name, rows, ident, banks, xT_hi, xT_lo, xT=None):
        sb = lambda n, shape: ctx.enter_context(nc.sbuf_tensor(f"{name}_{n}", shape, F32))
        sem = lambda n: ctx.enter_context(nc.semaphore(f"{name}_{n}"))
        self.rows, self.ident, self.banks = rows, ident, banks
        self.xT_hi, self.xT_lo, self.xT = xT_hi, xT_lo, xT
        self.stats = sb("stats", [P, TILES, 6])
        self.mean_var = sb("mean_var", [P, TILES, 2])
        self.deviation = sb("deviation", [P, TILES])
        self.inv_deviation = sb("inv_deviation", [P, TILES])
        self.eps = sb("eps", [P, 1])
        self.eps_set, self.stats_done, self.var_done = sem("eps_set"), sem("stats_done"), sem("var_done")
        self.sqrt_done, self.inv_done, self.normed = sem("sqrt_done"), sem("inv_done"), sem("normed")
        self.turned, self.hi_done, self.lo_done = sem("turned"), sem("hi_done"), sem("lo_done")

    def on_vector(self, dve, transposed=True):
        dve.memset(self.eps[:, :], EPS).then_inc(self.eps_set, 1)
        for t in range(TILES):
            dve.bn_stats(self.stats[:, t, :], self.rows[:, t, :]).then_inc(self.stats_done, 1)
        for t in range(TILES):
            dve.wait_ge(self.stats_done, t + 1)
            dve.bn_aggr(self.mean_var[:, t, :], self.stats[:, t, :]).then_inc(self.var_done, 1)
        dve.wait_ge(self.sqrt_done, 1)
        dve.reciprocal(self.inv_deviation[:, :], self.deviation[:, :]).then_inc(self.inv_done, 1)
        dve.wait_ge(self.inv_done, 1)
        for t in range(TILES):
            dve.tensor_scalar(self.rows[:, t, :], self.rows[:, t, :], self.mean_var[:, t, 0:1],
                              self.inv_deviation[:, t:t + 1], ALU.subtract, ALU.mult).then_inc(self.normed, 1)
        if transposed:
            for t in range(TILES):
                at = slice(t * P, (t + 1) * P)
                dve.wait_ge(self.hi_done, t + 1)
                dve.tensor_tensor(self.xT_lo[:, :, at], self.bank(t), self.xT_hi[:, :, at].bitcast(F32),
                                  ALU.subtract).then_inc(self.lo_done, 1)

    def bank(self, t):
        return self.banks[t % 2][:, :].rearrange("p (k c) -> p k c", k=KC)

    def on_scalar(self, act, transposed=True):
        act.wait_ge(self.eps_set, 1)
        act.wait_ge(self.var_done, TILES)
        act.activation(self.deviation[:, :], self.mean_var[:, :, 1], ACT.Sqrt,
                       bias=self.eps[:, 0:1]).then_inc(self.sqrt_done, 1)
        if transposed:
            for t in range(TILES):
                act.wait_ge(self.turned, t + 1)
                act.activation(self.xT_hi[:, :, t * P:(t + 1) * P], self.bank(t), ACT.Copy).then_inc(self.hi_done, 1)

    def on_tensor(self, pe):
        for t in range(TILES):
            pe.wait_ge(self.normed, t + 1)
            if t >= 2:
                pe.wait_ge(self.lo_done, t - 1)
            for k in range(KC):
                mm = pe.transpose(self.banks[t % 2][:, k * P:(k + 1) * P], self.rows[:, t, k * P:(k + 1) * P],
                                  self.ident[:, :])
            mm.then_inc(self.turned, 1)


def feed_forward0(nc, t, weight_stream, psum):
    ctx = ExitStack()
    with ctx:
        def sb(name, shape, dt=F32):
            return ctx.enter_context(nc.sbuf_tensor(name, shape, dt))

        sem = lambda name: ctx.enter_context(nc.semaphore(name))
        rows = t["rows"]
        xT_hi, xT_lo = (sb(f"f0_xT_{n}", [P, KC, TOK], F32R) for n in ("hi", "lo"))
        hT_hi, hT_lo = (sb(f"f0_hT_{n}", [P, F_TILES, TOK], F32R) for n in ("hi", "lo"))
        wg_hi, wg_lo, wu_hi, wu_lo = (sb(f"f0_w{n}", [P, KC, P], F32R) for n in ("g_hi", "g_lo", "u_hi", "u_lo"))
        wd_hi, wd_lo = (sb(f"f0_wd_{n}", [P, F_TILES, D], F32R) for n in ("hi", "lo"))
        staged = sb("f0_staged", [P, 3, 512])
        gated = sb("f0_gated", [P, BATCH, SEQ])
        hidden = sb("f0_hidden", [P, BATCH, SEQ])
        ps_g, ps_u, ps_y = psum[0:2], psum[2:4], psum[4:6]

        norm = Norm(ctx, nc, "n0", rows, t["ident"], psum[6:8], xT_hi, xT_lo)
        weight_in = {k: sem(f"f0_in_{k}") for k in "gud"}
        w_hi_done = {k: sem(f"f0_hi_{k}") for k in "gud"}
        w_lo_done = {k: sem(f"f0_lo_{k}") for k in "gud"}
        gate_ready, up_ready = sem("f0_gate_ready"), sem("f0_up_ready")
        gated_done, hidden_done = sem("f0_gated_done"), sem("f0_hidden_done")
        h_hi_done, h_lo_done = sem("f0_h_hi_done"), sem("f0_h_lo_done")
        y_ready, y_added = sem("f0_y_ready"), sem("f0_y_added")

        def dest(kind, f, hi):
            if kind == "d":
                return (wd_hi if hi else wd_lo)[:, bass.ds(f, 1), :].rearrange("p a c -> p (a c)")
            pair = {"g": (wg_hi, wg_lo), "u": (wu_hi, wu_lo)}[kind]
            return pair[0 if hi else 1][:, :, :].rearrange("p k c -> p (k c)")

        block = ctx.enter_context(nc.Block())

        @block.sync
        def _(sp):
            def load(f, kind):
                n = "gud".index(kind)
                sp.dma_start(staged[:, n, :], weight_stream[bass.ds(3 * f + n, 1), :, :].rearrange(
                    "a p c -> p (a c)")).then_inc(weight_in[kind], 16)

            for kind in "gud":
                load(0, kind)
            with sp.Fori(1, F_TILES) as f:
                for kind in "gud":
                    sp.wait_ge(w_lo_done[kind], f)
                    load(f, kind)

        @block.scalar
        def _(act):
            def split(kind, f):
                act.wait_ge(weight_in[kind], 16 * (f + 1))
                act.activation(dest(kind, f, True), staged[:, "gud".index(kind), :],
                               ACT.Copy).then_inc(w_hi_done[kind], 1)

            def gates(f):
                for b in range(BATCH):
                    act.wait_ge(gate_ready, 2 * f + b + 1)
                    act.activation(gated[:, b, :], ps_g[b][:, :], ACT.Silu).then_inc(gated_done, 1)

            def high(f):
                for b in range(BATCH):
                    act.wait_ge(hidden_done, 2 * f + b + 1)
                    act.activation(hT_hi[:, bass.ds(f, 1), b * SEQ:(b + 1) * SEQ].rearrange("p a c -> p (a c)"),
                                   hidden[:, b, :], ACT.Copy).then_inc(h_hi_done, 1)

            split("g", 0)
            split("u", 0)
            norm.on_scalar(act)
            with act.Fori(0, F_TILES - 1) as f:
                gates(f)
                split("g", f + 1)
                split("d", f)
                high(f)
                act.wait_ge(up_ready, 2 * f + 2)
                split("u", f + 1)
            gates(F_TILES - 1)
            split("d", F_TILES - 1)
            high(F_TILES - 1)

        @block.gpsimd
        def _(pool):
            def rest(kind, f):
                pool.wait_ge(w_hi_done[kind], f + 1)
                pool.tensor_tensor(dest(kind, f, False), staged[:, "gud".index(kind), :],
                                   dest(kind, f, True).bitcast(F32), ALU.subtract).then_inc(w_lo_done[kind], 1)

            rest("g", 0)
            rest("u", 0)
            with pool.Fori(0, F_TILES - 1) as f:
                rest("g", f + 1)
                rest("d", f)
                rest("u", f + 1)
            rest("d", F_TILES - 1)

        @block.vector
        def _(dve):
            norm.on_vector(dve)
            with dve.Fori(0, F_TILES) as f:
                for b in range(BATCH):
                    dve.wait_ge(up_ready, 2 * f + b + 1)
                    dve.wait_ge(gated_done, 2 * f + b + 1)
                    dve.tensor_tensor(hidden[:, b, :], ps_u[b][:, :], gated[:, b, :], ALU.mult).then_inc(hidden_done, 1)
                for b in range(BATCH):
                    at = lambda x: x[:, bass.ds(f, 1), b * SEQ:(b + 1) * SEQ].rearrange("p a c -> p (a c)")
                    dve.wait_ge(h_hi_done, 2 * f + b + 1)
                    dve.tensor_tensor(at(hT_lo), hidden[:, b, :], at(hT_hi).bitcast(F32),
                                      ALU.subtract).then_inc(h_lo_done, 1)
                dve.wait_ge(h_lo_done, 2 * f + 2)
            for tile in range(TILES):
                dve.wait_ge(y_ready, tile + 1)
                dve.tensor_tensor(rows[:, tile, :], ps_y[tile % 2][:, :], rows[:, tile, :],
                                  ALU.add).then_inc(y_added, 1)

        @block.tensor
        def _(pe):
            norm.on_tensor(pe)
            pe.wait_ge(norm.lo_done, TILES)
            with pe.Fori(0, F_TILES) as f:
                pe.wait_ge(w_lo_done["g"], f + 1)
                for b in range(BATCH):
                    three(pe, ps_g[b][:, :], [(wg_hi[:, k, :], wg_lo[:, k, :], xT_hi[:, k, b * SEQ:(b + 1) * SEQ],
                                               xT_lo[:, k, b * SEQ:(b + 1) * SEQ]) for k in range(KC)], gate_ready)
                pe.wait_ge(w_lo_done["u"], f + 1)
                for b in range(BATCH):
                    three(pe, ps_u[b][:, :], [(wu_hi[:, k, :], wu_lo[:, k, :], xT_hi[:, k, b * SEQ:(b + 1) * SEQ],
                                               xT_lo[:, k, b * SEQ:(b + 1) * SEQ]) for k in range(KC)], up_ready)
            pe.wait_ge(w_lo_done["d"], F_TILES)
            pe.wait_ge(h_lo_done, 2 * F_TILES)
            for tile in range(TILES):
                if tile >= 2:
                    pe.wait_ge(y_added, tile - 1)
                at = slice(tile * P, (tile + 1) * P)
                three(pe, ps_y[tile % 2][:, :], [(hT_hi[:, f, at], hT_lo[:, f, at], wd_hi[:, f, :], wd_lo[:, f, :])
                                                 for f in range(F_TILES)], y_ready)


def layout_ffn0(inputs):
    pad = F_TILES * P - F0
    blocks = []
    up, gate = (np.pad(inputs[n], ((0, pad), (0, 0))).T.reshape(KC, P, F_TILES, P).transpose(2, 1, 0, 3)
                for n in ("L0_ffn_W_up", "L0_ffn_W_gate"))
    down = np.pad(inputs["L0_ffn_W_down"], ((0, 0), (0, pad))).T.reshape(F_TILES, P, D)
    for f in range(F_TILES):
        blocks += [gate[f].reshape(P, 512), up[f].reshape(P, 512), down[f]]
    return {"weights_f0": np.stack(blocks)}

HEADS1, KV1 = 32, 8
HD1 = D // HEADS1
GROUP1 = HEADS1 // KV1
SCALE1 = HD1 ** -0.5
GQ = GROUP1 * HD1
PARTS = 3
STACK = PARTS * HD1
PAIR = 2 * STACK
QUAD = 32
UNITS1 = KV1 * BATCH
PADS = 7
SCORE_BLOCKS = ([(3, h, 1) for h in range(GROUP1)] + [(2, h, 1) for h in range(GROUP1)] + [(1, 0, 2), (1, 2, 2)]
                + [(0, 0, 2), (0, 2, 2)])
STACK_BLOCKS = 3
PER_UNIT = STACK_BLOCKS + len(SCORE_BLOCKS)
TURNED_SCORES = {0: (0, 0, 0), 1: (1, 0, 1), 3: (2, 0, 2), 2: (2, 2 * P, 2)}
EXP_SPANS = [(0, SEQ, 0), (0, 3 * P, SEQ), (P, 3 * P, SEQ + 4 * P)]
HEAD_PROBS = SEQ + 7 * P
PROBS_AT = {0: 0, 1: SEQ, 3: SEQ + 3 * P, 2: SEQ + 5 * P}
SPLIT_SPANS = [(0, SEQ + 3 * P), (SEQ + 4 * P, HEAD_PROBS)]
HALF = P // 2
LOW_HEAD = GROUP1 - 1


def attention1(nc, t, w_qkv, w_o, cos_in, sin_in, mask_in, ones_in, psum):
    ctx = ExitStack()
    with ctx:
        def sb(name, shape, dt=F32):
            return ctx.enter_context(nc.sbuf_tensor("a1_" + name, shape, dt))

        sem = lambda name: ctx.enter_context(nc.semaphore("a1_" + name))
        rows, ident = t["rows"], t["ident"]
        KVW = 2 * KV1 * HD1
        xT = sb("xT", [P, 2, KC, TOK], F32R)
        xT_hi, xT_lo = xT[:, 0, :, :], xT[:, 1, :, :]
        w_hi, w_lo = (sb(f"w_{n}", [P, KC, D + KVW], F32R) for n in ("hi", "lo"))
        wo_hi, wo_lo = w_hi[:, :, 0:D], w_lo[:, :, 0:D]
        staged = sb("staged", [P, 2, D + KVW])
        q_tok = sb("q_tok", [P, TILES, (KV1 + 1) * GQ])
        k_tok = sb("k_tok", [P, TILES, (KV1 + 1) * HD1])
        v_tok = sb("v_tok", [P, TILES, (KV1 + 1) * HD1])
        q_parts = sb("q_parts", [P, SEQ_TILES, GROUP1, PARTS, HD1], F32R)
        k_parts = sb("k_parts", [P, SEQ_TILES, STACK + STACK + STACK], F32R)
        q_stack = sb("q_stack", [P, 2, TOK], F32R)
        k_stack = sb("k_stack", [P, 2, TOK], F32R)
        v_now = sb("v_now", [P, TILES, 3 * HALF], F32R)
        v_at = HALF
        probs_T = sb("probs_T", [P, GROUP1, HEAD_PROBS])
        ones_staged = probs_T[PAIR:P, 0:2, 0:TOK]
        probs_lo = sb("probs_lo", [P, GROUP1, HEAD_PROBS], F32R)
        probs_hi = xT[:, :, :, :].rearrange("p a k c -> p (a k c)")[:, 0:GROUP1 * HEAD_PROBS].rearrange(
            "p (h c) -> p h c", h=GROUP1)
        oT_now = sb("oT_now", [P, SEQ])
        o_tok = sb("o_tok", [P, TILES, D])
        cos = sb("cos", [P, SEQ_TILES, HD1])
        sin = sb("sin", [P, SEQ_TILES, HD1])
        mask = sb("mask", [P, 2 * P])
        mask_half = sb("mask_half", [P, 2 * P], BF16)
        ident_half = sb("ident_half", [P, P], BF16)
        ident_r = sb("ident_r", [P, P], F32R)
        by_cos = sb("by_cos", [P, D + KV1 * HD1])
        by_sin = sb("by_sin", [P, D + KV1 * HD1])
        row_max = sb("row_max", [P, SEQ_TILES, GROUP1])
        neg_max = sb("neg_max", [P, SEQ_TILES, GROUP1])
        max_parts = sb("max_parts", [P, SEQ_TILES, P // QUAD, QUAD], F32R)
        inv_sum = sb("inv_sum", [P, SEQ_TILES, 2])
        o_sum = sb("o_sum", [P, SEQ_TILES, 2, HD1])

        norm = Norm(ctx, nc, "n1", rows, ident, psum[4:6], xT_hi, xT_lo)
        ps_q, ps_kv = psum[0:2], psum[2:4]
        ps_exp, ps_o, ps_s, ps_turn = psum[0:3], psum[3], psum[4:7], psum[7]
        ps_y = psum[0:2]

        constants_in = sem("constants_in")
        weight_in = [sem("weight_in0"), sem("weight_in1")]
        w_hi_done, w_lo_done, ident_done, pads_set = sem("w_hi_done"), sem("w_lo_done"), sem("ident_done"), sem("pads_set")
        v_now_cleared, gaps_set = sem("v_now_cleared"), sem("gaps_set")
        qkv_ready, cos_done, sin_done, v_done = sem("qkv_ready"), sem("cos_done"), sem("sin_done"), sem("v_done")
        tok_done = sem("tok_done")
        part_hi, part_lo, v_hi_done, v_lo_done = sem("part_hi"), sem("part_lo"), sem("v_hi_done"), sem("v_lo_done")
        scored, score_read, turn_ready, turn_read = sem("scored"), sem("score_read"), sem("turn_ready"), sem("turn_read")
        maxed, neg_done, max_hi_done, max_done = sem("maxed"), sem("neg_done"), sem("max_hi_done"), sem("max_done")
        exp_ready, exp_done, probs_hi_done = sem("exp_ready"), sem("exp_done"), sem("probs_hi_done")
        probs_lo_done, last_lo_done = sem("probs_lo_done"), sem("last_lo_done")
        o_ready, o_read, inv_done, summed = sem("o_ready"), sem("o_read"), sem("inv_done"), sem("summed")
        out_turned, out_hi, out_lo = sem("out_turned"), sem("out_hi"), sem("out_lo")
        y_ready, y_added = sem("y_ready"), sem("y_added")

        heads = lambda ap, n: ap.rearrange("p (h d) -> p h d", d=HD1)
        half = HD1 // 2
        block = ctx.enter_context(nc.Block())

        @block.sync
        def _(sp):
            for k in range(KC):
                if k >= 2:
                    sp.wait_ge(w_lo_done, k - 1)
                sp.dma_start(staged[:, k % 2, :], w_qkv[k]).then_inc(weight_in[k % 2], 16)
            sp.dma_start(cos[:, :, :], cos_in).then_inc(constants_in, 16)
            sp.dma_start(sin[:, :, :], sin_in).then_inc(constants_in, 16)
            sp.dma_start(mask[:, :], mask_in).then_inc(constants_in, 16)
            sp.dma_start(ones_staged, ones_in).then_inc(constants_in, 16)
            for k in range(KC, 2 * KC):
                sp.wait_ge(w_lo_done, k - 1)
                sp.dma_start(staged[:, k % 2, 0:D], w_o[k - KC]).then_inc(weight_in[k % 2], 16)

        def weight_block(k):
            hi, lo = (w_hi, w_lo) if k < KC else (wo_hi, wo_lo)
            width = D + KVW if k < KC else D
            return hi[:, k % KC, :], lo[:, k % KC, :], staged[:, k % 2, 0:width]

        def q_part(n):
            return q_parts[:, :, :, n, :]

        def k_part(n):
            return k_parts[:, :, STACK + n * HD1:STACK + (n + 1) * HD1]

        def batch_tiles(b):
            return slice(b * SEQ_TILES, (b + 1) * SEQ_TILES)

        def q_of(g, b):
            return q_tok[:, batch_tiles(b), bass.ds(g * GQ, GQ)].rearrange("p t (h d) -> p t h d", d=HD1)

        def k_of(g, b):
            return k_tok[:, batch_tiles(b), bass.ds(g * HD1, HD1)]

        FIRST_TURNED = 3

        def next_maxima_at(u):
            return 4 * u + FIRST_TURNED

        def output_at(u, pair):
            return 4 * u + FIRST_TURNED + 1 + 2 * pair

        def later_keys_at(u):
            return 4 * u + FIRST_TURNED + 2

        def split_low(engine, u, h, done):
            for n, (first, end) in enumerate(SPLIT_SPANS):
                engine.wait_ge(probs_hi_done, 2 * (GROUP1 * u + h) + n + 1)
                engine.tensor_tensor(probs_lo[:, h, first:end], probs_T[:, h, first:end],
                                     probs_hi[:, h, first:end].bitcast(F32), ALU.subtract).then_inc(done, 1)

        @block.scalar
        def _(act):
            norm.on_scalar(act, transposed=False)
            for k in range(KC):
                act.wait_ge(weight_in[k % 2], 16 * (k // 2 + 1))
                hi, _, raw = weight_block(k)
                act.activation(hi, raw, ACT.Copy).then_inc(w_hi_done, 1)
            for tile in range(TILES):
                act.wait_ge(norm.turned, tile + 1)
                act.activation(xT_hi[:, :, tile * P:(tile + 1) * P], norm.bank(tile), ACT.Copy).then_inc(norm.hi_done, 1)
            act.activation(ident_r[:, :], ident[:, :], ACT.Copy).then_inc(ident_done, 1)
            act.activation(ident_half[:, :], ident[:, :], ACT.Copy).then_inc(ident_done, 1)
            act.wait_ge(constants_in, 64)
            act.activation(mask_half[:, :], mask[:, :], ACT.Copy).then_inc(ident_done, 1)
            act.activation(k_stack[PAIR:P, :, :], ones_staged, ACT.Copy).then_inc(ident_done, 1)
            for tile in range(TILES):
                act.wait_ge(sin_done, 4 * (tile + 1))
                act.activation(v_tok[:, tile, 0:KV1 * HD1], ps_kv[tile % 2][:, KV1 * HD1:KVW], ACT.Copy).then_inc(v_done, 1)
            for k in range(KC, 2 * KC):
                act.wait_ge(weight_in[k % 2], 16 * (k // 2 + 1))
                hi, _, raw = weight_block(k)
                act.activation(hi, raw, ACT.Copy).then_inc(w_hi_done, 1)

            def high_parts(g, b):
                for n in (0, 1):
                    act.activation(q_part(n), q_of(g, b), ACT.Copy).then_inc(part_hi, 1)
                for n in (0, 2):
                    act.activation(k_part(n), k_of(g, b), ACT.Copy).then_inc(part_hi, 1)

            def values(g, b):
                act.activation(v_now[:, batch_tiles(b), v_at:v_at + HD1],
                               v_tok[:, batch_tiles(b), bass.ds(g * HD1, HD1)], ACT.Copy).then_inc(v_hi_done, 1)

            def last_keys(b, at):
                act.wait_ge(turn_ready, at + 1)
                act.activation(k_stack[0:PAIR, 1, b * SEQ:(b + 1) * SEQ], ps_turn[0:PAIR, :],
                               ACT.Copy).then_inc(turn_read, 1)

            def maxima(b, at):
                act.wait_ge(turn_ready, at + 1)
                for pair in range(2):
                    copied = act.activation(q_stack[PAIR:P, pair, b * SEQ:(b + 1) * SEQ],
                                            ps_turn[pair * QUAD:(pair + 1) * QUAD, :], ACT.Copy)
                copied.then_inc(turn_read, 1)

            def exps(u, h):
                for bank, (first, n, to) in enumerate(EXP_SPANS):
                    act.wait_ge(exp_ready, 3 * (GROUP1 * u + h) + bank + 1)
                    act.activation(probs_T[:, h, to:to + n], ps_exp[bank][:, first:first + n], ACT.Exp,
                                   scale=SCALE1).then_inc(exp_done, 1)

            def high_probs(u, h):
                act.wait_ge(exp_done, 3 * (GROUP1 * u + h + 1))
                for first, end in SPLIT_SPANS:
                    act.activation(probs_hi[:, h, first:end], probs_T[:, h, first:end],
                                   ACT.Copy).then_inc(probs_hi_done, 1)

            def evacuate(u, pair):
                act.wait_ge(o_ready, 2 * u + pair + 1)
                act.activation(oT_now[:, :], ps_o[:, :], ACT.Copy).then_inc(o_read, 1)

            act.wait_ge(tok_done, 2 * TILES)
            act.wait_ge(pads_set, PADS)
            high_parts(0, 0)
            last_keys(0, 0)
            high_parts(0, 1)
            values(0, 0)
            values(0, 1)
            maxima(0, 1)
            last_keys(1, 2)
            for h in (0, 1):
                exps(0, h)
                high_probs(0, h)
            with act.Fori(0, KV1) as g:
                for b in range(BATCH):
                    u = BATCH * g + b
                    exps(u, 2)
                    high_probs(u, 2)
                    high_parts(g + 1, b)
                    exps(u, 3)
                    high_probs(u, 3)
                    evacuate(u, 0)
                    maxima(1 - b, next_maxima_at(u))
                    exps(u + 1, 0)
                    high_probs(u + 1, 0)
                    last_keys(b, later_keys_at(u))
                    exps(u + 1, 1)
                    evacuate(u, 1)
                    high_probs(u + 1, 1)
                    values(g + 1, b)
            for tile in range(TILES):
                act.wait_ge(out_turned, tile + 1)
                act.activation(xT_hi[:, :, tile * P:(tile + 1) * P], norm.bank(tile), ACT.Copy).then_inc(out_hi, 1)

        @block.gpsimd
        def _(pool):
            pool.memset(q_tok[:, :, KV1 * GQ:], 0.0).then_inc(pads_set, 1)
            pool.memset(k_tok[:, :, KV1 * HD1:], 0.0).then_inc(pads_set, 1)
            pool.memset(v_tok[:, :, KV1 * HD1:], 0.0).then_inc(pads_set, 1)
            pool.memset(v_now[:, :, :].bitcast(F32), 0.0).then_inc(v_now_cleared, 1)
            pool.wait_ge(v_now_cleared, 1)
            pool.memset(v_now[:, :, v_at + HD1:v_at + HD1 + 1].bitcast(F32), 1.0).then_inc(pads_set, 1)
            pool.memset(k_parts[:, :, 0:STACK].bitcast(F32), 0.0).then_inc(pads_set, 1)
            pool.memset(k_parts[:, :, 2 * STACK:].bitcast(F32), 0.0).then_inc(pads_set, 1)
            pool.memset(max_parts[:, :, :, :].bitcast(F32), 0.0).then_inc(pads_set, 1)

            def weights(ks):
                for k in ks:
                    hi, lo, raw = weight_block(k)
                    pool.wait_ge(w_hi_done, k + 1)
                    pool.tensor_tensor(lo, raw, hi.bitcast(F32), ALU.subtract).then_inc(w_lo_done, 1)

            weights(range(KC))
            for tile in range(TILES):
                pool.wait_ge(sin_done, 4 * (tile + 1))
                pool.tensor_tensor(q_tok[:, tile, 0:D], by_cos[:, 0:D], by_sin[:, 0:D], ALU.add).then_inc(tok_done, 1)
                pool.tensor_tensor(k_tok[:, tile, 0:KV1 * HD1], by_cos[:, D:], by_sin[:, D:], ALU.add).then_inc(tok_done, 1)
            weights(range(KC, 2 * KC))
            pool.wait_ge(qkv_ready, 2 * TILES)
            for part in (probs_hi, probs_lo):
                pool.memset(part[:, :, SPLIT_SPANS[0][1]:SPLIT_SPANS[1][0]].bitcast(F32), 0.0).then_inc(gaps_set, 1)
            with pool.Fori(0, KV1) as g:
                for b in range(BATCH):
                    split_low(pool, BATCH * g + b, LOW_HEAD, last_lo_done)

        @block.vector
        def _(dve):
            norm.on_vector(dve)
            dve.wait_ge(constants_in, 64)
            for tile in range(TILES):
                q_in = ps_q[tile % 2][:, 0:D].rearrange("p (h d) -> p h d", d=HD1)
                k_in = ps_kv[tile % 2][:, 0:KV1 * HD1].rearrange("p (h d) -> p h d", d=HD1)
                c, s_ = cos[:, tile % SEQ_TILES, :], sin[:, tile % SEQ_TILES, :]
                dve.wait_ge(qkv_ready, 2 * (tile + 1))
                if tile >= 1:
                    dve.wait_ge(tok_done, 2 * tile)
                for source, n, at in ((q_in, HEADS1, 0), (k_in, KV1, D)):
                    out = by_cos[:, at:at + n * HD1].rearrange("p (h d) -> p h d", d=HD1)
                    dve.tensor_tensor(out, source, c.rearrange("p (a d) -> p a d", a=1).broadcast_to([P, n, HD1]),
                                      ALU.mult).then_inc(cos_done, 1)
                    out = by_sin[:, at:at + n * HD1].rearrange("p (h d) -> p h d", d=HD1)
                    for to, of in ((slice(0, half), slice(half, HD1)), (slice(half, HD1), slice(0, half))):
                        dve.tensor_tensor(out[:, :, to], source[:, :, of],
                                          s_[:, to].rearrange("p (a d) -> p a d", a=1).broadcast_to([P, n, half]),
                                          ALU.mult).then_inc(sin_done, 1)

            def low_parts(g, b):
                dve.wait_ge(part_hi, 4 * (BATCH * g + b + 1))
                dve.tensor_tensor(q_part(2), q_of(g, b), q_part(0).bitcast(F32), ALU.subtract).then_inc(part_lo, 1)
                dve.tensor_tensor(k_part(1), k_of(g, b), k_part(0).bitcast(F32), ALU.subtract).then_inc(part_lo, 1)

            def stacks(u, b):
                for n in range(STACK_BLOCKS):
                    to = (q_stack if n < 2 else k_stack)[0:PAIR, n % 2, b * SEQ:(b + 1) * SEQ]
                    dve.wait_ge(scored, PER_UNIT * u + n + 1)
                    dve.tensor_copy(to, ps_s[n][0:PAIR, :]).then_inc(score_read, 1)

            def maxima(u, blocks):
                for n in blocks:
                    qt, h, heads_n = SCORE_BLOCKS[n]
                    seen = (qt + 1) * P
                    bank = ps_s[(STACK_BLOCKS + n) % 3]
                    dve.wait_ge(scored, PER_UNIT * u + STACK_BLOCKS + n + 1)
                    if heads_n == 1:
                        dve.tensor_reduce(row_max[:, qt, h:h + 1], bank[:, 0:seen], mybir.AxisListType.X,
                                          ALU.max).then_inc(score_read, 1)
                    else:
                        dve.tensor_reduce(row_max[:, qt, h:h + 2],
                                          bank[:, :].rearrange("p (h c) -> p h c", h=2)[:, :, 0:seen],
                                          mybir.AxisListType.X, ALU.max).then_inc(score_read, 1)

            def split_maxima(u):
                part = lambda n: max_parts[:, :, 0:2, n:4:2]
                by_pair = lambda x: x[:, :, :].rearrange("p t (a h) -> p t a h", a=2)
                dve.wait_ge(score_read, PER_UNIT * (u + 1))
                dve.tensor_scalar(neg_max[:, :, :], row_max[:, :, :], -1.0, None, ALU.mult).then_inc(neg_done, 1)
                dve.wait_ge(neg_done, u + 1)
                dve.tensor_copy(part(0), by_pair(neg_max)).then_inc(max_hi_done, 1)
                dve.wait_ge(max_hi_done, u + 1)
                dve.tensor_tensor(part(1), by_pair(neg_max), part(0).bitcast(F32), ALU.subtract).then_inc(max_done, 1)

            def low_values(g, b):
                dve.wait_ge(v_hi_done, BATCH * g + b + 1)
                dve.tensor_tensor(v_now[:, batch_tiles(b), v_at + QUAD:v_at + QUAD + HD1],
                                  v_tok[:, batch_tiles(b), bass.ds(g * HD1, HD1)],
                                  v_now[:, batch_tiles(b), v_at:v_at + HD1].bitcast(F32),
                                  ALU.subtract).then_inc(v_lo_done, 1)

            def finish(u, g, b, pair):
                turned = ps_turn[:, :].rearrange("p (t h d) -> p t h d", t=SEQ_TILES, h=2)
                at = g * GQ + pair * 2 * HD1
                dve.wait_ge(turn_ready, output_at(u, pair) + 1)
                dve.reciprocal(inv_sum[:, :, :], turned[:, :, :, HD1]).then_inc(inv_done, 1)
                dve.tensor_copy(o_sum[:, :, :, :], turned[:, :, :, QUAD:QUAD + HD1]).then_inc(summed, 1)
                dve.wait_ge(summed, 2 * (2 * u + pair) + 1)
                dve.tensor_tensor(o_sum[:, :, :, :], turned[:, :, :, 0:HD1], o_sum[:, :, :, :],
                                  ALU.add).then_inc(summed, 1)
                dve.wait_ge(inv_done, 2 * u + pair + 1)
                dve.wait_ge(summed, 2 * (2 * u + pair) + 2)
                dve.tensor_tensor(
                    o_tok[:, batch_tiles(b), bass.ds(at, 2 * HD1)].rearrange("p t (h d) -> p t h d", d=HD1),
                    o_sum[:, :, :, :],
                    inv_sum[:, :, :].rearrange("p t (h a) -> p t h a", a=1).broadcast_to([P, SEQ_TILES, 2, HD1]),
                    ALU.mult).then_inc(turn_read, 1)

            dve.wait_ge(pads_set, PADS)
            low_parts(0, 0)
            stacks(0, 0)
            low_parts(0, 1)
            low_values(0, 0)
            low_values(0, 1)
            maxima(0, range(12))
            split_maxima(0)
            stacks(1, 1)
            maxima(1, range(0, 4))
            split_low(dve, 0, 0, probs_lo_done)
            with dve.Fori(0, KV1) as g:
                for b in range(BATCH):
                    u = BATCH * g + b
                    maxima(u + 1, range(4, 8))
                    split_low(dve, u, 1, probs_lo_done)
                    maxima(u + 1, range(8, 12))
                    split_maxima(u + 1)
                    low_parts(g + 1, b)
                    split_low(dve, u, 2, probs_lo_done)
                    stacks(u + 2, b)
                    finish(u, g, b, 0)
                    split_low(dve, u + 1, 0, probs_lo_done)
                    maxima(u + 2, range(0, 4))
                    low_values(g + 1, b)
                    finish(u, g, b, 1)
            for tile in range(TILES):
                at = slice(tile * P, (tile + 1) * P)
                dve.wait_ge(out_hi, tile + 1)
                dve.tensor_tensor(xT_lo[:, :, at], norm.bank(tile), xT_hi[:, :, at].bitcast(F32),
                                  ALU.subtract).then_inc(out_lo, 1)
            for tile in range(TILES):
                dve.wait_ge(y_ready, tile + 1)
                dve.tensor_tensor(rows[:, tile, :], ps_y[tile % 2][:, :], rows[:, tile, :], ALU.add).then_inc(y_added, 1)

        @block.tensor
        def _(pe):
            norm.on_tensor(pe)
            pe.wait_ge(w_lo_done, KC)
            pe.wait_ge(norm.lo_done, TILES)
            for tile in range(TILES):
                at = slice(tile * P, (tile + 1) * P)
                if tile >= 2:
                    pe.wait_ge(v_done, tile - 1)
                three(pe, ps_q[tile % 2][:, :], [(xT_hi[:, k, at], xT_lo[:, k, at], w_hi[:, k, 0:D], w_lo[:, k, 0:D])
                                                 for k in range(KC)], qkv_ready)
                three(pe, ps_kv[tile % 2][:, 0:KVW], [(xT_hi[:, k, at], xT_lo[:, k, at], w_hi[:, k, D:], w_lo[:, k, D:])
                                                      for k in range(KC)], qkv_ready)

            def first_unit(u):
                return isinstance(u, int) and u == 0

            def stack(u, n, at):
                bank = ps_s[n] if n < STACK_BLOCKS else ps_turn
                if n < STACK_BLOCKS:
                    if not first_unit(u):
                        pe.wait_ge(score_read, PER_UNIT * u + n - 2)
                elif not first_unit(u):
                    pe.wait_ge(turn_read, at)
                for j in range(SEQ_TILES):
                    if n < 2:
                        source = q_parts[:, j, 2 * n:2 * n + 2, :, :].rearrange("p h n d -> p (h n d)")
                    else:
                        first = STACK if n == 2 else 0
                        source = k_parts[:, j, first:first + PAIR]
                    mm = pe.transpose(bank[0:PAIR, j * P:(j + 1) * P].bitcast(F32R), source, ident_r[:, :])
                mm.then_inc(scored if n < STACK_BLOCKS else turn_ready, 1)

            def stacks(u, at, blocks):
                if 0 in blocks:
                    pe.wait_ge(part_hi, 4 * (u + 1))
                    pe.wait_ge(part_lo, 2 * (u + 1))
                for n in blocks:
                    stack(u, n, at)

            def score(u, b, blocks):
                for n in blocks:
                    qt, first, heads_n = SCORE_BLOCKS[n]
                    width = max(qt + 1, 2) * P
                    row = b * SEQ + qt * P
                    bank = ps_s[(STACK_BLOCKS + n) % 3]
                    pe.wait_ge(score_read, PER_UNIT * u + STACK_BLOCKS + max(n - 2, 0))
                    for i in range(heads_n):
                        h = first + i
                        pe.matmul(bank[:, i * width:(i + 1) * width], q_stack[0:PAIR, h // 2, row:row + P],
                                  k_stack[0:PAIR, h % 2, b * SEQ:b * SEQ + width], start=True, stop=False)
                        own = i * width + qt * P
                        mm = pe.matmul(bank[:, own:own + P], ident_half[:, :], mask_half[:, 0:P], start=False, stop=True)
                    mm.then_inc(scored, 1)

            def score_turned(u, b, h):
                for kb, (bank, at, qt) in TURNED_SCORES.items():
                    if at == 0 and not (first_unit(u) and h == 0):
                        pe.wait_ge(exp_done, 3 * (GROUP1 * u + h - 1) + bank + 1)
                    width = SEQ - qt * P
                    own = at + (kb - qt) * P
                    pe.matmul(ps_exp[bank][:, at:at + width], k_stack[:, h % 2, b * SEQ + kb * P:b * SEQ + (kb + 1) * P],
                              q_stack[:, h // 2, b * SEQ + qt * P:(b + 1) * SEQ], start=True, stop=False)
                    mm = pe.matmul(ps_exp[bank][:, own:own + P], ident_half[:, :], mask_half[:, P:2 * P],
                                   start=False, stop=True)
                    if kb != 3:
                        mm.then_inc(exp_ready, 1)

            def apply(u, b, h):
                if h == 0:
                    pe.wait_ge(v_lo_done, u + 1)
                if h == 2:
                    pe.wait_ge(o_read, 2 * u + 1)
                for kb in (0, 1, 3, 2):
                    if kb in (0, 3):
                        lo_done, blocks = (last_lo_done, u) if h == LOW_HEAD else (probs_lo_done, LOW_HEAD * u + h)
                        pe.wait_ge(lo_done, 2 * blocks + (1 if kb == 0 else 2))
                    qt = TURNED_SCORES[kb][2]
                    window = v_at - (h % 2) * HALF
                    for part in (probs_hi, probs_lo):
                        mm = pe.matmul(ps_o[:, qt * P:SEQ], v_now[:, b * SEQ_TILES + kb, window:window + P],
                                       part[:, h, PROBS_AT[kb]:PROBS_AT[kb] + SEQ - qt * P],
                                       start=(kb == 0 and h % 2 == 0 and part is probs_hi),
                                       stop=(kb == 2 and h % 2 == 1 and part is probs_lo))
                if h % 2 == 1:
                    mm.then_inc(o_ready, 1)

            def turn_maxima(u, at):
                pe.wait_ge(max_done, u + 1)
                pe.wait_ge(turn_read, at)
                for j in range(SEQ_TILES):
                    mm = pe.transpose(ps_turn[:, j * P:(j + 1) * P].bitcast(F32R),
                                      max_parts[:, j, :, :].rearrange("p a c -> p (a c)"), ident_r[:, :])
                mm.then_inc(turn_ready, 1)

            def turn_output(u, pair):
                pe.wait_ge(o_read, 2 * u + pair + 1)
                pe.wait_ge(turn_read, output_at(u, pair))
                for j in range(SEQ_TILES):
                    mm = pe.transpose(ps_turn[:, j * P:(j + 1) * P], oT_now[:, j * P:(j + 1) * P], ident[:, :])
                mm.then_inc(turn_ready, 1)

            pe.wait_ge(ident_done, 4)
            pe.wait_ge(pads_set, PADS)
            stacks(0, 0, range(4))
            pe.wait_ge(turn_read, 1)
            score(0, 0, range(12))
            turn_maxima(0, 1)
            stacks(1, 2, range(4))
            score_turned(0, 0, 0)
            score_turned(0, 0, 1)
            pe.wait_ge(turn_read, 3)
            score(1, 1, range(0, 4))
            pe.wait_ge(gaps_set, 2)
            with pe.Fori(0, KV1) as g:
                for b in range(BATCH):
                    u = BATCH * g + b
                    score_turned(u, b, 2)
                    score(u + 1, 1 - b, range(4, 8))
                    apply(u, b, 0)
                    score_turned(u, b, 3)
                    score(u + 1, 1 - b, range(8, 12))
                    apply(u, b, 1)
                    turn_maxima(u + 1, next_maxima_at(u))
                    stacks(u + 2, 0, range(0, 3))
                    apply(u, b, 2)
                    turn_output(u, 0)
                    score_turned(u + 1, 1 - b, 0)
                    stacks(u + 2, later_keys_at(u), range(3, 4))
                    score_turned(u + 1, 1 - b, 1)
                    apply(u, b, 3)
                    pe.wait_ge(turn_read, later_keys_at(u) + 1)
                    score(u + 2, b, range(0, 4))
                    turn_output(u, 1)
            pe.wait_ge(turn_read, 4 * UNITS1 + FIRST_TURNED)
            pe.wait_ge(score_read, PER_UNIT * (UNITS1 + 1) + STACK_BLOCKS + 4)
            for tile in range(TILES):
                if tile >= 2:
                    pe.wait_ge(out_lo, tile - 1)
                for k in range(KC):
                    mm = pe.transpose(norm.banks[tile % 2][:, k * P:(k + 1) * P], o_tok[:, tile, k * P:(k + 1) * P],
                                      ident[:, :])
                mm.then_inc(out_turned, 1)
            pe.wait_ge(w_lo_done, 2 * KC)
            pe.wait_ge(out_lo, TILES)
            pe.wait_ge(exp_done, 3 * (GROUP1 * UNITS1 + 2))
            for tile in range(TILES):
                if tile >= 2:
                    pe.wait_ge(y_added, tile - 1)
                at = slice(tile * P, (tile + 1) * P)
                three(pe, ps_y[tile % 2][:, :], [(xT_hi[:, k, at], xT_lo[:, k, at], wo_hi[:, k, :], wo_lo[:, k, :])
                                                 for k in range(KC)], y_ready)


def layout1(inputs):
    qkv = np.concatenate([inputs["L1_attn_Wq"], inputs["L1_attn_Wk"], inputs["L1_attn_Wv"]], 1)
    return {"weights_qkv1": qkv.reshape(KC, P, D + 2 * KV1 * HD1), "weights_o1": inputs["L1_attn_Wo"].reshape(KC, P, D)}


def tables1():
    inv = (1.0 / 500000.0 ** (np.arange(0, HD1, 2, dtype=np.float32) / HD1)).astype(np.float32)
    ang = np.arange(SEQ, dtype=np.float32)[:, None] * inv[None, :]
    tile = lambda a: np.ascontiguousarray(a.astype(np.float32).reshape(SEQ_TILES, P, HD1).transpose(1, 0, 2))
    q, k = np.arange(P)[:, None], np.arange(P)[None, :]
    mask = np.where(k <= q, 0, MASKED).astype(np.float32)
    ones = np.zeros((QUAD, 2, TOK), np.float32)
    ones[0:2, 0] = ones[2:4, 1] = 1
    return {"cos1": tile(np.concatenate([np.cos(ang), np.cos(ang)], 1)),
            "sin1": tile(np.concatenate([-np.sin(ang), np.sin(ang)], 1)),
            "mask1": np.concatenate([mask, mask.T], 1), "ones1": ones}



EXPERTS, RANK, GATE_H = 8, 16, 32
LORA = EXPERTS * RANK
CAPACITY = int(3.0 * TOK / EXPERTS)
ALPHA = 1.0 / RANK
SIDE = 256
SMALL = {"gb1": GATE_H, "gamma": GATE_H, "beta": GATE_H, "gw2": EXPERTS * GATE_H, "gb2": EXPERTS, "index": EXPERTS}
AHEAD = 6


def feed_forward1(nc, t, w_in, lora_b_in, small_in, out, psum):
    ctx = ExitStack()
    with ctx:
        def sb(name, shape, dt=F32):
            return ctx.enter_context(nc.sbuf_tensor("f1_" + name, shape, dt))

        sem = lambda name: ctx.enter_context(nc.semaphore("f1_" + name))
        rows, ident = t["rows"], t["ident"]
        xT_hi, xT_lo = (sb(f"xT_{n}", [P, KC, TOK], F32R) for n in ("hi", "lo"))
        w_hi, w_lo = (sb(f"w_{n}", [P, KC, D + SIDE], F32R) for n in ("hi", "lo"))
        b_hi, b_lo = (sb(f"b_{n}", [P, D], F32R) for n in ("hi", "lo"))
        staged = sb("staged", [P, KC, D + SIDE])
        b_staged = sb("b_staged", [P, D])
        small = sb("small", [P, sum(SMALL.values())])
        low = sb("low", [P, TILES, LORA])
        h = sb("h", [P, TILES, GATE_H])
        squares = sb("squares", [P, TILES, GATE_H])
        mean = sb("mean", [P, TILES])
        var = sb("var", [P, TILES])
        dev = sb("dev", [P, TILES])
        products = sb("products", [P, TILES, EXPERTS, GATE_H])
        gates = sb("gates", [P, TILES, EXPERTS])
        top = sb("top", [P, TILES, 8])
        top_index = sb("top_index", [P, TILES, 8], mybir.dt.uint32)
        top_at = sb("top_at", [P, TILES, 8])
        gap = sb("gap", [P, TILES])
        share = sb("share", [P, 2, TILES])
        total = sb("total", [P, TILES])
        chosen = sb("chosen", [P, 2, TILES, EXPERTS])
        count = sb("count", [P, 2, EXPERTS])
        allowed = sb("allowed", [P, 2, EXPERTS])
        weight = sb("weight", [P, 2, TILES, EXPERTS])
        ones = sb("ones", [P, P])
        low_T_hi, low_T_lo = (sb(f"low_T_{n}", [P, TOK], F32R) for n in ("hi", "lo"))

        names, at = {}, 0
        for name, width in SMALL.items():
            names[name] = small[:, at:at + width]
            at += width

        norm = Norm(ctx, nc, "n2", rows, ident, psum[6:8], xT_hi, xT_lo)
        last = Norm(ctx, nc, "n3", rows, ident, psum[6:8], None, None)
        ps_side, ps_y, ps_count, ps_low = psum[0:2], psum[0:6], psum[6], psum[6:8]
        weight_in, small_in_done, b_in = [sem(f"weight_in{k}") for k in range(KC)], sem("small_in"), sem("b_in")
        w_hi_done, w_lo_done = sem("w_hi_done"), sem("w_lo_done")
        side_ready, low_copied, h_copied = sem("side_ready"), sem("low_copied"), sem("h_copied")
        step_done, var_ready, dev_done, gap_ready, exp_done = (sem("step_done"), sem("var_ready"), sem("dev_done"),
                                                               sem("gap_ready"), sem("exp_done"))
        ones_set, count_ready, counted, weighted = sem("ones_set"), sem("count_ready"), sem("counted"), sem("weighted")
        low_turned, low_hi_done, low_lo_done = sem("low_turned"), sem("low_hi_done"), sem("low_lo_done")
        y_ready, y_added, stored = sem("y_ready"), sem("y_added"), sem("stored")

        block = ctx.enter_context(nc.Block())

        @block.sync
        def _(sp):
            for k in range(KC):
                sp.dma_start(staged[:, k, :], w_in[k]).then_inc(weight_in[k], 16)
            sp.dma_start(small[:, :], small_in).then_inc(small_in_done, 16)
            sp.dma_start(b_staged[:, :], lora_b_in).then_inc(b_in, 16)
            for tile in range(TILES):
                sp.wait_ge(last.normed, tile + 1)
                sp.dma_start(out[tile * P:(tile + 1) * P, :], rows[:, tile, :]).then_inc(stored, 16)
            sp.wait_ge(stored, 16 * TILES)

        @block.scalar
        def _(act):
            for k in range(KC):
                act.wait_ge(weight_in[k], 16)
                act.activation(w_hi[:, k, :], staged[:, k, :], ACT.Copy).then_inc(w_hi_done, 1)
            act.wait_ge(b_in, 16)
            act.activation(b_hi[:, :], b_staged[:, :], ACT.Copy).then_inc(w_hi_done, 1)
            norm.on_scalar(act)
            for tile in range(TILES):
                act.wait_ge(h_copied, tile + 1)
                act.activation(low[:, tile, :], ps_side[tile % 2][:, GATE_H:GATE_H + LORA],
                               ACT.Copy).then_inc(low_copied, 1)
            act.wait_ge(var_ready, 1)
            act.activation(dev[:, :], var[:, :], ACT.Sqrt, bias=norm.eps[:, 0:1],
                           scale=1.0 / GATE_H).then_inc(dev_done, 1)
            act.wait_ge(gap_ready, 1)
            act.activation(share[:, 1, :], gap[:, :], ACT.Exp).then_inc(exp_done, 1)
            for half in range(2):
                act.wait_ge(low_turned, half + 1)
                act.activation(low_T_hi[:, half * 512:(half + 1) * 512], ps_low[half][:, :], ACT.Copy).then_inc(low_hi_done, 1)
            act.wait_ge(y_added, TILES)
            last.on_scalar(act, transposed=False)

        @block.gpsimd
        def _(pool):
            pool.memset(ones[:, :], 1.0).then_inc(ones_set, 1)
            for k in range(KC):
                pool.wait_ge(w_hi_done, k + 1)
                pool.tensor_tensor(w_lo[:, k, :], staged[:, k, :], w_hi[:, k, :].bitcast(F32),
                                   ALU.subtract).then_inc(w_lo_done, 1)
            pool.wait_ge(w_hi_done, KC + 1)
            pool.tensor_tensor(b_lo[:, :], b_staged[:, :], b_hi[:, :].bitcast(F32), ALU.subtract).then_inc(w_lo_done, 1)

        @block.vector
        def _(dve):
            steps = [0]

            def step(instruction):
                steps[0] += 1
                instruction.then_inc(step_done, 1)
                dve.wait_ge(step_done, steps[0])

            def each_tile(name):
                return names[name].rearrange("p (a c) -> p a c", a=1).broadcast_to([P, TILES, SMALL[name]])

            def each_column(ap, n):
                return ap.rearrange("p (t a) -> p t a", a=1).broadcast_to([P, TILES, n])

            norm.on_vector(dve)
            for tile in range(TILES):
                dve.wait_ge(side_ready, tile + 1)
                dve.tensor_copy(h[:, tile, :], ps_side[tile % 2][:, 0:GATE_H]).then_inc(h_copied, 1)
            dve.wait_ge(small_in_done, 16)
            dve.wait_ge(h_copied, TILES)
            step(dve.tensor_tensor(h[:, :, :], h[:, :, :], each_tile("gb1"), ALU.add))
            step(dve.tensor_reduce(mean[:, :], h[:, :, :], mybir.AxisListType.X, ALU.add))
            step(dve.tensor_scalar(mean[:, :], mean[:, :], 1.0 / GATE_H, None, ALU.mult))
            step(dve.tensor_tensor(h[:, :, :], h[:, :, :], each_column(mean[:, :], GATE_H), ALU.subtract))
            step(dve.tensor_tensor(squares[:, :, :], h[:, :, :], h[:, :, :], ALU.mult))
            dve.tensor_reduce(var[:, :], squares[:, :, :], mybir.AxisListType.X, ALU.add).then_inc(var_ready, 1)
            dve.wait_ge(dev_done, 1)
            step(dve.reciprocal(dev[:, :], dev[:, :]))
            step(dve.tensor_tensor(h[:, :, :], h[:, :, :], each_column(dev[:, :], GATE_H), ALU.mult))
            step(dve.tensor_tensor(h[:, :, :], h[:, :, :], each_tile("gamma"), ALU.mult))
            step(dve.tensor_tensor(h[:, :, :], h[:, :, :], each_tile("beta"), ALU.add))
            step(dve.tensor_scalar(h[:, :, :], h[:, :, :], 0.0, None, ALU.max))
            for e in range(EXPERTS):
                row = names["gw2"][:, e * GATE_H:(e + 1) * GATE_H].rearrange("p (a c) -> p a c", a=1)
                mult = dve.tensor_tensor(products[:, :, e, :], h[:, :, :], row.broadcast_to([P, TILES, GATE_H]), ALU.mult)
            step(mult)
            step(dve.tensor_reduce(gates[:, :, :].rearrange("p t e -> p (t e)"),
                                   products[:, :, :, :].rearrange("p t e c -> p (t e) c"),
                                   mybir.AxisListType.X, ALU.add))
            step(dve.tensor_tensor(gates[:, :, :], gates[:, :, :], each_tile("gb2"), ALU.add))
            for tile in range(TILES):
                found = dve.max(top[:, tile, :], gates[:, tile, :])
            step(found)
            for tile in range(TILES):
                found = dve.max_index(top_index[:, tile, :], top[:, tile, :], gates[:, tile, :])
            step(found)
            step(dve.tensor_copy(top_at[:, :, :], top_index[:, :, :]))
            dve.tensor_tensor(gap[:, :], top[:, :, 1], top[:, :, 0], ALU.subtract).then_inc(gap_ready, 1)
            for n in range(2):
                found = dve.tensor_tensor(chosen[:, n, :, :], each_column(top_at[:, :, n], EXPERTS), each_tile("index"),
                                          ALU.is_equal)
            step(found)
            dve.tensor_reduce(count[:, :, :].rearrange("p n e -> p (n e)"),
                              chosen[:, :, :, :].rearrange("p n t e -> p n e t"), mybir.AxisListType.X,
                              ALU.add).then_inc(count_ready, 1)
            dve.wait_ge(exp_done, 1)
            step(dve.tensor_scalar(total[:, :], share[:, 1, :], 1.0, None, ALU.add))
            step(dve.reciprocal(share[:, 0, :], total[:, :]))
            step(dve.tensor_tensor(share[:, 1, :], share[:, 1, :], share[:, 0, :], ALU.mult))
            dve.wait_ge(counted, 1)
            step(dve.tensor_scalar(allowed[:, :, :].rearrange("p n e -> p (n e)"), ps_count[:, 0:2 * EXPERTS],
                                   float(CAPACITY), ALPHA, ALU.is_le, ALU.mult))
            for n in range(2):
                found = dve.tensor_tensor(weight[:, n, :, :], chosen[:, n, :, :], each_column(share[:, n, :], EXPERTS),
                                          ALU.mult)
            step(found)
            for n in range(2):
                found = dve.tensor_tensor(weight[:, n, :, :], weight[:, n, :, :],
                                          allowed[:, n, :].rearrange("p (a e) -> p a e", a=1).broadcast_to(
                                              [P, TILES, EXPERTS]), ALU.mult)
            step(found)
            step(dve.tensor_tensor(weight[:, 0, :, :], weight[:, 0, :, :], weight[:, 1, :, :], ALU.add))
            dve.wait_ge(low_copied, TILES)
            by_expert = low[:, :, :].rearrange("p t (e r) -> p (t e) r", r=RANK)
            dve.tensor_tensor(by_expert, by_expert,
                              weight[:, 0, :, :].rearrange("p t (e a) -> p (t e) a", a=1).broadcast_to(
                                  [P, TILES * EXPERTS, RANK]), ALU.mult).then_inc(weighted, 1)
            for half in range(2):
                dve.wait_ge(low_hi_done, half + 1)
                cols = slice(half * 512, (half + 1) * 512)
                dve.tensor_tensor(low_T_lo[:, cols], ps_low[half][:, :], low_T_hi[:, cols].bitcast(F32),
                                  ALU.subtract).then_inc(low_lo_done, 1)
            for tile in range(TILES):
                dve.wait_ge(y_ready, tile + 1)
                dve.tensor_tensor(rows[:, tile, :], ps_y[tile % AHEAD][:, :], rows[:, tile, :], ALU.add).then_inc(y_added, 1)
            dve.wait_ge(y_added, TILES)
            last.on_vector(dve, transposed=False)

        @block.tensor
        def _(pe):
            norm.on_tensor(pe)
            pe.wait_ge(w_lo_done, KC)
            pe.wait_ge(norm.lo_done, TILES)
            for tile in range(TILES):
                if tile >= 2:
                    pe.wait_ge(low_copied, tile - 1)
                at = slice(tile * P, (tile + 1) * P)
                three(pe, ps_side[tile % 2][:, 0:SIDE], [(xT_hi[:, k, at], xT_lo[:, k, at], w_hi[:, k, D:], w_lo[:, k, D:])
                                                         for k in range(KC)], side_ready)

            def dense(tile):
                at = slice(tile * P, (tile + 1) * P)
                for k in range(KC):
                    for a, b in ((xT_hi, w_hi), (xT_hi, w_lo), (xT_lo, w_hi)):
                        pe.matmul(ps_y[tile % AHEAD][:, :], a[:, k, at], b[:, k, 0:D],
                                  start=(k == 0 and a is xT_hi and b is w_hi), stop=False)

            def low_rank(tile):
                at = slice(tile * P, (tile + 1) * P)
                for a, b in ((low_T_hi, b_hi), (low_T_hi, b_lo), (low_T_lo, b_hi)):
                    mm = pe.matmul(ps_y[tile % AHEAD][:, :], a[:, at], b[:, :], start=False, stop=(a is low_T_lo))
                mm.then_inc(y_ready, 1)

            pe.wait_ge(low_copied, TILES)
            for tile in range(AHEAD):
                dense(tile)
            pe.wait_ge(ones_set, 1)
            pe.wait_ge(count_ready, 1)
            pe.matmul(ps_count[:, 0:2 * EXPERTS], ones[:, :], count[:, :, :].rearrange("p n e -> p (n e)"),
                      start=True, stop=True).then_inc(counted, 1)
            pe.wait_ge(weighted, 1)
            for half in range(2):
                for j in range(4):
                    mm = pe.transpose(ps_low[half][:, j * P:(j + 1) * P], low[:, 4 * half + j, :], ident[:, :])
                mm.then_inc(low_turned, 1)
            pe.wait_ge(w_lo_done, KC + 1)
            pe.wait_ge(low_lo_done, 2)
            for tile in range(AHEAD):
                low_rank(tile)
            for tile in range(AHEAD, TILES):
                pe.wait_ge(y_added, tile - AHEAD + 1)
                dense(tile)
                low_rank(tile)


def layout_ffn1(inputs):
    low = inputs["L1_ffn_lora_A"].transpose(1, 0, 2).reshape(D, LORA)
    pad = np.zeros((D, SIDE - GATE_H - LORA), np.float32)
    w = np.concatenate([inputs["L1_ffn_weight"].T, inputs["L1_ffn_gw1"].T, low, pad], 1)
    small = np.concatenate([inputs["L1_ffn_gb1"], inputs["L1_ffn_ln_gamma"], inputs["L1_ffn_ln_beta"],
                            inputs["L1_ffn_gw2"].reshape(-1), inputs["L1_ffn_gb2"],
                            np.arange(EXPERTS, dtype=np.float32)])
    return {"weights_f1": w.reshape(KC, P, D + SIDE), "lora_b": inputs["L1_ffn_lora_B"].reshape(LORA, D),
            "small_f1": np.ascontiguousarray(np.broadcast_to(small, (P, small.size)))}


def program(nc, a, out):
    with ExitStack() as ctx:
        rows = ctx.enter_context(nc.sbuf_tensor("rows", [P, TILES, D], F32))
        ident = ctx.enter_context(nc.sbuf_tensor("identity", [P, P], F32))
        psum = [ctx.enter_context(nc.psum_tensor(f"bank{n}", [P, 512], F32)) for n in range(8)]
        x_stage = rows[:, :, :].rearrange("p t d -> p (t d)").rearrange("p (k c) -> p k c", k=KC)
        t = {"rows": rows, "ident": ident, "x_stage": x_stage}
        attention0(nc, t, a["x_T"], a["weights0"], a["x_rows"], a["cos0"], a["sin0"], a["mask0"], a["ident"], psum)
        feed_forward0(nc, t, a["weights_f0"], psum)
        attention1(nc, t, a["weights_qkv1"], a["weights_o1"], a["cos1"], a["sin1"], a["mask1"], a["ones1"], psum)
        feed_forward1(nc, t, a["weights_f1"], a["lora_b"], a["small_f1"], out, psum)


def kernel(**inputs):
    from concourse import bacc
    from concourse.bass_utils import run_bass_kernel_spmd

    inputs = {k: np.asarray(v) for k, v in inputs.items()}
    arrays = {**layout0(inputs), **tables0(), **layout_ffn0(inputs), **layout1(inputs), **tables1(), **layout_ffn1(inputs)}
    arrays = {k: np.ascontiguousarray(v) for k, v in arrays.items()}
    nc = bacc.Bacc("TRN2", target_bir_lowering=False, num_devices=1)
    args = {k: nc.dram_tensor(k, v.shape, F32, kind="ExternalInput").ap() for k, v in arrays.items()}
    out = nc.dram_tensor("out", (TOK, D), F32, kind="ExternalOutput").ap()
    program(nc, args, out)
    result = run_bass_kernel_spmd(nc, [arrays], core_ids=[0])
    return result.results[0]["out"].reshape(BATCH, SEQ, D)
```

```python
from contextlib import ExitStack

import numpy as np

import concourse.bass as bass
from concourse import mybir
from concourse.alu_op_type import AluOpType as ALU

F32 = mybir.dt.float32
F32R = mybir.dt.float32r
BF16 = mybir.dt.bfloat16
ACT = mybir.ActivationFunctionType

P = 128
BATCH, SEQ, D = 2, 512, 512
TOK = BATCH * SEQ
TILES = TOK // P
SEQ_TILES = SEQ // P
KC = D // P
EPS = 1e-5
MASKED = -1e30
LOWEST = -3e38

HEADS0, KV0, HD0 = 32, 8, 128
GROUP0 = HEADS0 // KV0
SCALE0 = HD0 ** -0.5
PAIRS = KV0 // 2
WEIGHT_ORDER = [
    (0, "k", 1, 0), (0, "q", 1, 0), (1, "q", 1, 1), (1, "q", 1, 2), (2, "q", 1, 3),
    (3, "o", 1, 0), (3, "o", 1, 1), (4, "o", 1, 2), (5, "o", 1, 3),
    (6, "k", 0, 0), (7, "q", 0, 0), (7, "q", 0, 1), (8, "q", 0, 2), (9, "q", 0, 3), (9, "v", 0, 0),
    (10, "v", 1, 0), (11, "o", 0, 0), (12, "o", 0, 1), (13, "o", 0, 2), (14, "o", 0, 3),
]
PER_PAIR = len(WEIGHT_ORDER)
FIRST_OF_NEXT = 9
HEAD_START = PER_PAIR - FIRST_OF_NEXT
WEIGHT_AT = {w[1:]: n for n, w in enumerate(WEIGHT_ORDER)}
SLOTS = 16
UNIT_PIECES = 5
PAIR_PIECES = 4 * UNIT_PIECES
PIECES_AHEAD = 9
PIECES_OF, _a = [], PIECES_AHEAD
for _s in range(SLOTS):
    _n = 2 if _s % 4 == 2 else 1
    PIECES_OF.append(list(range(_a, _a + _n)))
    _a += _n
VALUES_IN = {**{s: s + SEQ_TILES for s in range(SEQ_TILES)}, **{s: s - 12 + TILES for s in range(12, 16)}}
AHEAD0 = 2
BEFORE_VALUES = 4


def weights_done(pair, kind, g, h=0):
    n = WEIGHT_AT[(kind, g, h)]
    if n >= FIRST_OF_NEXT:
        return pair * PER_PAIR + n - FIRST_OF_NEXT + 1
    return pair * PER_PAIR + HEAD_START + n + 1


def key_tiles(qt):
    return (0, 1) if qt == 0 else (qt - 1, 2)


def blocks_before(s):
    return (s // 4) * 7 + (0, 1, 3, 5)[s % 4]


def three(pe, out, terms, done):
    steps = [(a, b) for a_hi, a_lo, b_hi, b_lo in terms for a, b in ((a_hi, b_hi), (a_hi, b_lo), (a_lo, b_hi))]
    for n, (a, b) in enumerate(steps):
        mm = pe.matmul(out, a, b, start=(n == 0), stop=(n == len(steps) - 1))
    mm.then_inc(done, 1)


def attention0(nc, t, x_T, weight_stream, x_rows, cos_T, sin_T, masks, ident_in, psum):
    ctx = ExitStack()
    with ctx:
        def sb(name, shape, dt=F32):
            return ctx.enter_context(nc.sbuf_tensor(name, shape, dt))

        sem = lambda name: ctx.enter_context(nc.semaphore(name))

        xT_hi = sb("xT_hi", [P, KC, TOK], F32R)
        xT_lo = sb("xT_lo", [P, KC, TOK], F32R)
        wq_hi, wq_lo = (sb(f"wq_{n}", [P, GROUP0, KC, P], F32R) for n in ("hi", "lo"))
        wk_hi, wk_lo = (sb(f"wk_{n}", [P, KC, P], F32R) for n in ("hi", "lo"))
        wv_hi, wv_lo = (sb(f"wv_{n}", [P, KC, 2, P], F32R) for n in ("hi", "lo"))
        wo_hi, wo_lo = (sb(f"wo_{n}", [P, 2, GROUP0, D], F32R) for n in ("hi", "lo"))
        staged = sb("staged", [P, 2, 512])
        qT_hi, qT_lo = (sb(f"qT_{n}", [P, 2, GROUP0, SEQ], F32R) for n in ("hi", "lo"))
        kT_hi, kT_lo = (sb(f"kT_{n}", [P, 2, SEQ], F32R) for n in ("hi", "lo"))
        v_hi, v_lo = (sb(f"v_{n}", [P, TILES, 2 * P], F32R) for n in ("hi", "lo"))
        probs = sb("probs", [P, 2, GROUP0, 2 * P])
        pT_hi, pT_lo = (sb(f"pT_{n}", [P, 2, GROUP0 * P], F32R) for n in ("hi", "lo"))
        oT_hi, oT_lo = (sb(f"oT_{n}", [P, 2, GROUP0 * P], F32R) for n in ("hi", "lo"))
        cos = sb("cos", [P, SEQ])
        sin = sb("sin", [P, SEQ])
        mask = sb("mask", [P, 3 * P])
        turned = sb("turned", [P, 2, SEQ])
        by_cos = sb("by_cos", [P, 2, SEQ])
        row_max = sb("row_max", [P, 2, GROUP0])
        neg_max = sb("neg_max", [P, 2, GROUP0])
        row_sum = sb("row_sum", [P, 2, GROUP0])
        inv_sum = sb("inv_sum", [P, 2, GROUP0])
        gate = sb("gate", [P, 2])
        rows, ident = t["rows"], t["ident"]

        ps_s, ps_a, ps_t = psum[0:2], psum[2:4], psum[4:6]
        ps_o, ps_y = psum[6], psum[7]

        constants_in = sem("constants_in")
        rows_in = sem("rows_in")
        xT_in = [sem(f"xT_in{b}") for b in range(BATCH)]
        weight_in = [sem("weight_in0"), sem("weight_in1")]
        xT_hi_done, xT_lo_done = sem("xT_hi_done"), sem("xT_lo_done")
        weight_hi_done, weight_lo_done = sem("weight_hi_done"), sem("weight_lo_done")
        projected = sem("projected")
        turned_done, sin_done, cos_done = sem("turned_done"), sem("sin_done"), sem("cos_done")
        roped, rope_hi, rope_lo = sem("roped"), sem("rope_hi"), sem("rope_lo")
        v_ready, v_hi_done, v_lo_done = sem("v_ready"), sem("v_hi_done"), sem("v_lo_done")
        scored, masked, max_done = sem("scored"), sem("masked"), sem("max_done")
        exp_done, inv_done, probs_done = sem("exp_done"), sem("inv_done"), sem("probs_done")
        pT_ready, pT_hi_done, pT_lo_done = sem("pT_ready"), sem("pT_hi_done"), sem("pT_lo_done")
        o_ready, o_hi_done, o_lo_done = sem("o_ready"), sem("o_hi_done"), sem("o_lo_done")
        y_ready, y_added = sem("y_ready"), sem("y_added")

        def weight_dest(n, hi):
            _, kind, g, h = WEIGHT_ORDER[n]
            if kind == "q":
                return (wq_hi if hi else wq_lo)[:, h, :, :]
            if kind == "k":
                return (wk_hi if hi else wk_lo)[:, :, :]
            if kind == "v":
                return (wv_hi if hi else wv_lo)[:, :, g, :]
            return (wo_hi if hi else wo_lo)[:, g, h, :]

        def staged_as(n, slot):
            v = staged[:, slot, :]
            return v if WEIGHT_ORDER[n][1] == "o" else v.rearrange("p (k c) -> p k c", k=KC)

        block = ctx.enter_context(nc.Block())

        @block.sync
        def _(sp):
            for n in range(HEAD_START):
                if n >= 2:
                    sp.wait_ge(weight_lo_done, n - 1)
                sp.dma_start(staged[:, n % 2, :], weight_stream[n]).then_inc(weight_in[n % 2], 16)
            sp.wait_ge(xT_lo_done, 2 * KC)
            sp.dma_start(rows[:, :, :], x_rows.rearrange("(t p) d -> p t d", p=P)).then_inc(rows_in, 16)

            def load(i, n):
                sp.wait_ge(weight_lo_done, i * PER_PAIR + HEAD_START + n - 1)
                source = weight_stream[bass.ds(i * PER_PAIR + HEAD_START + n, 1), :, :].rearrange("a p c -> p (a c)")
                sp.dma_start(staged[:, (HEAD_START + n) % 2, :], source).then_inc(weight_in[(HEAD_START + n) % 2], 16)

            with sp.Fori(0, PAIRS - 1) as i:
                for n in range(PER_PAIR):
                    load(i, n)
            for n in range(FIRST_OF_NEXT):
                load(PAIRS - 1, n)

        def loads(i, n):
            m = HEAD_START + n
            return i * (PER_PAIR // 2) * 16 + (m // 2 + 1) * 16, m % 2

        def pieces_of(s, last):
            return [a for a in PIECES_OF[s] if not last or a < PAIR_PIECES]

        def pieces_before(s, last):
            return [PIECES_AHEAD - 1] if s == 0 else pieces_of(s - 1, last)

        def weights_of(s, last):
            return [(n, *w[1:]) for n, w in enumerate(WEIGHT_ORDER) if w[0] == s and (not last or n < FIRST_OF_NEXT)]

        def values_in(s, last):
            return [VALUES_IN[s]] if s in VALUES_IN and (not last or VALUES_IN[s] < TILES) else []

        def scores_ahead(s, last):
            return [s + AHEAD0] if not last or s + AHEAD0 < SLOTS else []

        @block.scalar
        def _(act):
            for b in range(BATCH):
                for k in range(KC):
                    act.dma_start(t["x_stage"][:, k, b * SEQ:(b + 1) * SEQ],
                                  x_T[k * P:(k + 1) * P, b * SEQ:(b + 1) * SEQ]).then_inc(xT_in[b], 16)
                if b == 0:
                    act.dma_start(cos[:, :], cos_T).then_inc(constants_in, 16)
                    act.dma_start(sin[:, :], sin_T).then_inc(constants_in, 16)
            act.dma_start(mask[:, :], masks).then_inc(constants_in, 16)
            act.dma_start(ident[:, :], ident_in).then_inc(constants_in, 16)

            def high_input(b):
                cols = slice(b * SEQ, (b + 1) * SEQ)
                act.wait_ge(xT_in[b], 16 * KC)
                for k in range(KC):
                    act.activation(xT_hi[:, k, cols], t["x_stage"][:, k, cols], ACT.Copy).then_inc(xT_hi_done, 1)

            def first_weight(m):
                act.wait_ge(weight_in[m % 2], (m // 2 + 1) * 16)
                act.activation(weight_dest(m + FIRST_OF_NEXT, True), staged_as(m + FIRST_OF_NEXT, m % 2),
                               ACT.Copy).then_inc(weight_hi_done, 1)

            def turn(i, a):
                act.wait_ge(projected, PAIR_PIECES * i + a + 1)
                if a >= 2:
                    act.wait_ge(rope_lo, PAIR_PIECES * i + a - 1)
                half = HD0 // 2
                act.activation(turned[0:half, a % 2, :], ps_a[a % 2][half:P, :], ACT.Copy).then_inc(turned_done, 1)
                act.activation(turned[half:P, a % 2, :], ps_a[a % 2][0:half, :], ACT.Copy).then_inc(turned_done, 1)

            def rope_high(i, a):
                u, piece = divmod(a, UNIT_PIECES)
                dest = kT_hi[:, u % 2, :] if piece == 0 else qT_hi[:, u % 2, piece - 1, :]
                act.wait_ge(roped, PAIR_PIECES * i + a + 1)
                act.activation(dest, turned[:, a % 2, :], ACT.Copy).then_inc(rope_hi, 1)

            def high_values(i, tile):
                act.wait_ge(v_ready, TILES * i + tile + 1)
                act.activation(v_hi[:, tile % TILES, :], ps_t[1][:, 0:2 * P], ACT.Copy).then_inc(v_hi_done, 1)

            def exps(i, s):
                act.wait_ge(max_done, SLOTS * i + s + 1)
                for h in range(GROUP0):
                    act.activation(probs[:, s % 2, h, :], probs[:, s % 2, h, :], ACT.Exp,
                                   bias=neg_max[:, s % 2, h:h + 1], scale=SCALE0,
                                   accum_out=row_sum[:, s % 2, h:h + 1]).then_inc(exp_done, 1)

            def split_weight(i, n, kind, g, h):
                if kind == "v":
                    act.wait_ge(v_ready, TILES * (i + 1))
                elif kind == "o" and g == 0:
                    act.wait_ge(y_ready, SLOTS * i + 8)
                elif kind != "o":
                    last_use = UNIT_PIECES * (1 if g == 1 else 3) + (0 if kind == "k" else h + 1)
                    act.wait_ge(projected, PAIR_PIECES * i + last_use + 1)
                count, stage = loads(i, n)
                act.wait_ge(weight_in[stage], count)
                act.activation(weight_dest(n, True), staged_as(n, stage), ACT.Copy).then_inc(weight_hi_done, 1)

            high_input(0)
            first_weight(0)
            first_weight(1)
            high_input(1)
            first_weight(2)
            turn(0, 0)
            first_weight(3)
            for a in range(1, UNIT_PIECES):
                turn(0, a)
                if a + 3 < 7:
                    first_weight(a + 3)
                rope_high(0, a - 1)
                if a >= 3:
                    high_values(0, a - 3)
            for tile in range(2, SEQ_TILES):
                high_values(0, tile)
            rope_high(0, 4)
            first_weight(7)
            first_weight(8)
            exps(0, 0)
            turn(0, 5)
            turn(0, 6)
            exps(0, 1)
            for a in (7, 8):
                rope_high(0, a - 2)
                turn(0, a)
            rope_high(0, 7)
            first_weight(9)
            first_weight(10)

            def slots(i, last=False):
                for s in range(SLOTS):
                    for kb in range(key_tiles(s % 4)[1]):
                        act.wait_ge(pT_ready, 28 * i + blocks_before(s) + kb + 1)
                        act.activation(pT_hi[:, kb, :], ps_t[kb][:, :], ACT.Copy).then_inc(pT_hi_done, 1)
                    for a in pieces_before(s, last):
                        rope_high(i, a)
                    pieces = pieces_of(s, last)
                    if len(pieces) == 2:
                        turn(i, pieces[0])
                    act.wait_ge(o_ready, SLOTS * i + s + 1)
                    act.activation(oT_hi[:, s % 2, :], ps_o[:, :], ACT.Copy).then_inc(o_hi_done, 1)
                    for later in scores_ahead(s, last):
                        exps(i, later)
                    for tile in values_in(s, last):
                        high_values(i, tile)
                    for a in pieces[-1:]:
                        turn(i, a)
                    for w in weights_of(s, last):
                        split_weight(i, *w)

            with act.Fori(0, PAIRS - 1) as i:
                slots(i)
            slots(PAIRS - 1, last=True)

        @block.gpsimd
        def _(pool):
            def rotate(i, a):
                done = PAIR_PIECES * i + a + 1
                pool.wait_ge(turned_done, 2 * done)
                pool.tensor_tensor(turned[:, a % 2, :], turned[:, a % 2, :], sin[:, :], ALU.mult).then_inc(sin_done, 1)
                pool.wait_ge(sin_done, done)
                pool.wait_ge(cos_done, done)
                pool.tensor_tensor(turned[:, a % 2, :], turned[:, a % 2, :], by_cos[:, a % 2, :],
                                   ALU.add).then_inc(roped, 1)

            pool.wait_ge(constants_in, 64)
            for a in range(PIECES_AHEAD):
                rotate(0, a)
            pool.wait_ge(weight_lo_done, HEAD_START)

            def slots(i, last=False):
                for s in range(SLOTS):
                    for a in pieces_of(s, last):
                        rotate(i, a)
                    for n, *_rest in weights_of(s, last):
                        _, stage = loads(i, n)
                        pool.wait_ge(weight_hi_done, i * PER_PAIR + HEAD_START + n + 1)
                        pool.tensor_tensor(weight_dest(n, False), staged_as(n, stage), weight_dest(n, True).bitcast(F32),
                                           ALU.subtract).then_inc(weight_lo_done, 1)

            with pool.Fori(0, PAIRS - 1) as i:
                slots(i)
            slots(PAIRS - 1, last=True)

        @block.vector
        def _(dve):
            def low_input(b):
                cols = slice(b * SEQ, (b + 1) * SEQ)
                for k in range(KC):
                    dve.wait_ge(xT_hi_done, KC * b + k + 1)
                    dve.tensor_tensor(xT_lo[:, k, cols], t["x_stage"][:, k, cols],
                                      xT_hi[:, k, cols].bitcast(F32), ALU.subtract).then_inc(xT_lo_done, 1)

            def first_weight(m):
                n = m + FIRST_OF_NEXT
                dve.wait_ge(weight_hi_done, m + 1)
                dve.tensor_tensor(weight_dest(n, False), staged_as(n, m % 2), weight_dest(n, True).bitcast(F32),
                                   ALU.subtract).then_inc(weight_lo_done, 1)

            def times_cos(i, a):
                dve.wait_ge(turned_done, 2 * (PAIR_PIECES * i + a + 1))
                if a >= 2:
                    dve.wait_ge(roped, PAIR_PIECES * i + a - 1)
                dve.tensor_tensor(by_cos[:, a % 2, :], ps_a[a % 2][:, :], cos[:, :], ALU.mult).then_inc(cos_done, 1)

            def rope_low(i, a):
                u, piece = divmod(a, UNIT_PIECES)
                hi = kT_hi[:, u % 2, :] if piece == 0 else qT_hi[:, u % 2, piece - 1, :]
                lo = kT_lo[:, u % 2, :] if piece == 0 else qT_lo[:, u % 2, piece - 1, :]
                dve.wait_ge(rope_hi, PAIR_PIECES * i + a + 1)
                dve.tensor_tensor(lo, turned[:, a % 2, :], hi.bitcast(F32), ALU.subtract).then_inc(rope_lo, 1)

            def low_values(i, tile):
                dve.wait_ge(v_hi_done, TILES * i + tile + 1)
                dve.tensor_tensor(v_lo[:, tile % TILES, :], ps_t[1][:, 0:2 * P],
                                  v_hi[:, tile % TILES, :].bitcast(F32), ALU.subtract).then_inc(v_lo_done, 1)

            def mask_rows(i, s):
                seen = mask[:, P:3 * P] if s % 4 == 0 else mask[:, 0:2 * P]
                for h in range(GROUP0):
                    if h % 2 == 0:
                        dve.wait_ge(scored, 2 * (SLOTS * i + s) + h // 2 + 1)
                        dve.memset(gate[:, h // 2:h // 2 + 1], 0.0)
                    dve.tensor_tensor_reduce(
                        probs[:, s % 2, h, :], ps_s[h // 2][:, (h % 2) * 2 * P:(h % 2 + 1) * 2 * P], seen,
                        1.0, LOWEST, ALU.add, ALU.max, row_max[:, s % 2, h:h + 1]).then_inc(masked, 1)
                dve.wait_ge(masked, GROUP0 * (SLOTS * i + s + 1))
                dve.tensor_scalar(neg_max[:, s % 2, :], row_max[:, s % 2, :], -SCALE0, None,
                                  ALU.mult).then_inc(max_done, 1)

            def normalise(i, s):
                dve.wait_ge(exp_done, GROUP0 * (SLOTS * i + s + 1))
                dve.reciprocal(inv_sum[:, s % 2, :], row_sum[:, s % 2, :]).then_inc(inv_done, 1)
                dve.wait_ge(inv_done, SLOTS * i + s + 1)
                for h in range(GROUP0):
                    dve.tensor_scalar(probs[:, s % 2, h, :], probs[:, s % 2, h, :], inv_sum[:, s % 2, h:h + 1], None,
                                      ALU.mult).then_inc(probs_done, 1)

            low_input(0)
            first_weight(0)
            first_weight(1)
            low_input(1)
            first_weight(2)
            dve.wait_ge(constants_in, 64)
            times_cos(0, 0)
            first_weight(3)
            for a in range(1, UNIT_PIECES):
                times_cos(0, a)
                if a + 3 < 7:
                    first_weight(a + 3)
                rope_low(0, a - 1)
                if a >= 3:
                    low_values(0, a - 3)
            for tile in range(2, SEQ_TILES):
                low_values(0, tile)
            rope_low(0, 4)
            first_weight(7)
            first_weight(8)
            mask_rows(0, 0)
            times_cos(0, 5)
            normalise(0, 0)
            times_cos(0, 6)
            mask_rows(0, 1)
            for a in (7, 8):
                rope_low(0, a - 2)
                times_cos(0, a)
            rope_low(0, 7)
            normalise(0, 1)
            first_weight(9)
            first_weight(10)
            dve.wait_ge(rows_in, 16)

            def slots(i, last=False):
                for s in range(SLOTS):
                    for kb in range(key_tiles(s % 4)[1]):
                        dve.wait_ge(pT_hi_done, 28 * i + blocks_before(s) + kb + 1)
                        dve.tensor_tensor(pT_lo[:, kb, :], ps_t[kb][:, :], pT_hi[:, kb, :].bitcast(F32),
                                          ALU.subtract).then_inc(pT_lo_done, 1)
                    for later in scores_ahead(s, last):
                        mask_rows(i, later)
                    pieces = pieces_of(s, last)
                    if len(pieces) == 2:
                        times_cos(i, pieces[0])
                    dve.wait_ge(o_hi_done, SLOTS * i + s + 1)
                    dve.tensor_tensor(oT_lo[:, s % 2, :], ps_o[:, :], oT_hi[:, s % 2, :].bitcast(F32),
                                      ALU.subtract).then_inc(o_lo_done, 1)
                    for a in pieces_before(s, last):
                        rope_low(i, a)
                    for tile in values_in(s, last):
                        low_values(i, tile)
                    for later in scores_ahead(s, last):
                        normalise(i, later)
                    for a in pieces[-1:]:
                        times_cos(i, a)
                    row = rows[:, (s // 4) % 2 * SEQ_TILES + s % 4, :]
                    dve.wait_ge(y_ready, SLOTS * i + s + 1)
                    dve.tensor_tensor(row, ps_y[:, :], row, ALU.add).then_inc(y_added, 1)
                    if last and s >= SLOTS - TILES:
                        dve.wait_ge(y_added, SLOTS * i + s + 1)
                        t["norms"][0].take(dve, s - (SLOTS - TILES))

            with dve.Fori(0, PAIRS - 1) as i:
                slots(i)
            slots(PAIRS - 1, last=True)

        @block.tensor
        def _(pe):
            def project(i, a, steps=(0, 3 * KC)):
                u, piece = divmod(a, UNIT_PIECES)
                pair, (g, b) = i + u // 4, divmod(u % 4, 2)
                cols = slice(b * SEQ, (b + 1) * SEQ)
                if steps[0] == 0:
                    pe.wait_ge(weight_lo_done, weights_done(pair, "k", g) if piece == 0 else
                               weights_done(pair, "q", g, piece - 1))
                    if a >= 2:
                        pe.wait_ge(cos_done, PAIR_PIECES * i + a - 1)
                w = (wk_hi, wk_lo) if piece == 0 else (wq_hi[:, piece - 1, :, :], wq_lo[:, piece - 1, :, :])
                for n in range(*steps):
                    k, (hi, part) = n // 3, ((0, xT_hi), (0, xT_lo), (1, xT_hi))[n % 3]
                    mm = pe.matmul(ps_a[a % 2][:, :], w[hi][:, k, :], part[:, k, cols], start=(n == 0),
                                   stop=(n == 3 * KC - 1))
                if steps[1] == 3 * KC:
                    mm.then_inc(projected, 1)

            def values(i, tile):
                if tile % SEQ_TILES == 0:
                    pe.wait_ge(weight_lo_done, weights_done(i + tile // TILES, "v", 1))
                if tile >= 1:
                    pe.wait_ge(v_lo_done, TILES * i + tile)
                at = slice((tile % TILES) * P, (tile % TILES + 1) * P)
                three(pe, ps_t[1][:, 0:2 * P],
                      [(xT_hi[:, k, at], xT_lo[:, k, at], wv_hi[:, k, :, :].rearrange("p g c -> p (g c)"),
                        wv_lo[:, k, :, :].rearrange("p g c -> p (g c)")) for k in range(KC)], v_ready)

            def scores(i, s):
                u, qt = divmod(s, 4)
                first, _ = key_tiles(qt)
                keys = slice(first * P, (first + 2) * P)
                at = slice(qt * P, (qt + 1) * P)
                for pair in range(2):
                    if s >= 1:
                        pe.wait_ge(masked, GROUP0 * (SLOTS * i + s - 1) + 2 * pair + 2)
                    for h in (2 * pair, 2 * pair + 1):
                        if qt == 0:
                            pe.wait_ge(rope_lo, PAIR_PIECES * i + UNIT_PIECES * u + h + 2)
                        steps = [(qT_hi, kT_hi), (qT_hi, kT_lo), (qT_lo, kT_hi)]
                        for n, (q, k) in enumerate(steps):
                            mm = pe.matmul(ps_s[pair][:, (h % 2) * 2 * P:(h % 2 + 1) * 2 * P], q[:, u % 2, h, at],
                                           k[:, u % 2, keys], start=(n == 0), stop=(n == 2))
                    mm.then_inc(scored, 1)

            def turn_probs(i, s, last):
                pe.wait_ge(probs_done, GROUP0 * (SLOTS * i + s + 1))
                for kb in range(key_tiles(s % 4)[1]):
                    if kb == 1:
                        for tile in values_in(s - 1, last):
                            pe.wait_ge(v_lo_done, TILES * i + tile + 1)
                    for h in range(GROUP0):
                        mm = pe.transpose(ps_t[kb][:, h * P:(h + 1) * P], probs[:, s % 2, h, kb * P:(kb + 1) * P],
                                          ident[:, :])
                    mm.then_inc(pT_ready, 1)

            def apply_probs(i, s):
                u, qt = divmod(s, 4)
                g, b = divmod(u, 2)
                first, count = key_tiles(qt)
                if s in (0, 4):
                    pe.wait_ge(v_lo_done, TILES * i + s + SEQ_TILES)
                terms = []
                for kb in range(count):
                    tile = b * SEQ_TILES + first + kb
                    at = slice(g * P, (g + 1) * P)
                    terms.append((v_hi[:, tile, at], v_lo[:, tile, at], pT_hi[:, kb, :], pT_lo[:, kb, :]))
                pe.wait_ge(pT_lo_done, 28 * i + blocks_before(s) + count)
                three(pe, ps_o[:, :], terms, o_ready)

            def project_out(i, s):
                g = s // 8
                if s % 8 == 0:
                    pe.wait_ge(weight_lo_done, weights_done(i, "o", g, GROUP0 - 1))
                pe.wait_ge(o_lo_done, SLOTS * i + s + 1)
                three(pe, ps_y[:, :], [(oT_hi[:, s % 2, h * P:(h + 1) * P], oT_lo[:, s % 2, h * P:(h + 1) * P],
                                    wo_hi[:, g, h, :], wo_lo[:, g, h, :]) for h in range(GROUP0)], y_ready)

            pe.wait_ge(xT_lo_done, KC)
            for a in range(UNIT_PIECES):
                project(0, a)
                if a >= 3:
                    values(0, a - 3)
            for tile in range(2, SEQ_TILES):
                values(0, tile)
            scores(0, 0)
            pe.wait_ge(xT_lo_done, 2 * KC)
            project(0, 5)
            project(0, 6)
            scores(0, 1)
            project(0, 7)
            project(0, 8)
            pe.wait_ge(constants_in, 64)

            def slots(i, last=False):
                for s in range(SLOTS):
                    turn_probs(i, s, last)
                    for later in scores_ahead(s, last):
                        scores(i, later)
                    pieces = pieces_of(s, last)
                    if len(pieces) == 2:
                        project(i, pieces[0])
                    for a in pieces[0:1] if len(pieces) == 1 else []:
                        project(i, a, (0, BEFORE_VALUES))
                    apply_probs(i, s)
                    for tile in values_in(s, last):
                        values(i, tile)
                    for a in pieces[0:1] if len(pieces) == 1 else []:
                        project(i, a, (BEFORE_VALUES, 3 * KC))
                    if len(pieces) == 2:
                        project(i, pieces[1])
                    project_out(i, s)

            with pe.Fori(0, PAIRS - 1) as i:
                slots(i)
            slots(PAIRS - 1, last=True)


def layout0(inputs):
    x = inputs["L0_attn_x"].reshape(TOK, D)
    wq = inputs["L0_attn_wq"].reshape(KC, P, KV0, GROUP0, HD0)
    wk = inputs["L0_attn_wk"].reshape(KC, P, KV0, HD0)
    wv = inputs["L0_attn_wv"].reshape(KC, P, KV0, HD0)
    wo = inputs["L0_attn_wo"].reshape(KV0, GROUP0, P, D)
    blocks = []
    def add(pair, n):
        _, kind, g, h = WEIGHT_ORDER[n]
        kv = 2 * pair + g
        if kind == "o":
            blocks.append(wo[kv, h])
        else:
            w = {"q": wq[:, :, kv, h, :] if kind == "q" else None, "k": wk[:, :, kv], "v": wv[:, :, kv]}[kind]
            blocks.append(w.transpose(1, 0, 2).reshape(P, 512))
    for n in range(FIRST_OF_NEXT, PER_PAIR):
        add(0, n)
    for pair in range(PAIRS):
        for n in range(PER_PAIR):
            add(pair if n < FIRST_OF_NEXT else (pair + 1) % PAIRS, n)
    return {"x_T": np.ascontiguousarray(x.T), "x_rows": x, "weights0": np.stack(blocks)}


def tables0():
    half = HD0 // 2
    inv = 10000.0 ** (-np.arange(half, dtype=np.float32) / half)
    ang = (np.arange(SEQ, dtype=np.float32)[:, None] * inv[None, :].astype(np.float32)).T
    cos = np.concatenate([np.cos(ang), np.cos(ang)]).astype(np.float32)
    sin = np.concatenate([-np.sin(ang), np.sin(ang)]).astype(np.float32)
    q, k = np.arange(P)[:, None], np.arange(P)[None, :]
    mask = np.concatenate([np.where(k > q, 0, MASKED), np.where(k <= q, 0, MASKED), np.full((P, P), MASKED)], 1)
    return {"cos0": cos, "sin0": sin, "mask0": mask.astype(np.float32), "ident": np.eye(P, dtype=np.float32)}

F0 = 1376
F_TILES = -(-F0 // P)


class Norm:

    def __init__(self, ctx, nc, name, rows, ident, transposed=True):
        sb = lambda n, shape: ctx.enter_context(nc.sbuf_tensor(f"{name}_{n}", shape, F32))
        sem = lambda n: ctx.enter_context(nc.semaphore(f"{name}_{n}"))
        self.rows, self.ident = rows, ident
        self.stats = sb("stats", [P, TILES, 6])
        self.mean_var = sb("mean_var", [P, TILES, 2])
        self.deviation = sb("deviation", [P, TILES])
        self.inv_deviation = sb("inv_deviation", [P, TILES])
        self.eps = sb("eps", [P, 1])
        self.eps_set, self.stats_done, self.var_done = sem("eps_set"), sem("stats_done"), sem("var_done")
        self.sqrt_done, self.inv_done, self.normed = sem("sqrt_done"), sem("inv_done"), sem("normed")
        if transposed:
            self.turned, self.hi_done, self.lo_done = sem("turned"), sem("hi_done"), sem("lo_done")

    def attach(self, banks, xT_hi, xT_lo):
        self.banks, self.xT_hi, self.xT_lo = banks, xT_hi, xT_lo
        return self

    def take(self, dve, t):
        dve.bn_stats(self.stats[:, t, :], self.rows[:, t, :]).then_inc(self.stats_done, 1)

    def on_vector(self, dve, transposed=True):
        dve.memset(self.eps[:, :], EPS).then_inc(self.eps_set, 1)
        for t in range(TILES):
            dve.wait_ge(self.stats_done, t + 1)
            dve.bn_aggr(self.mean_var[:, t, :], self.stats[:, t, :]).then_inc(self.var_done, 1)
        dve.wait_ge(self.sqrt_done, 1)
        dve.reciprocal(self.inv_deviation[:, :], self.deviation[:, :]).then_inc(self.inv_done, 1)
        dve.wait_ge(self.inv_done, 1)
        for t in range(TILES):
            dve.tensor_scalar(self.rows[:, t, :], self.rows[:, t, :], self.mean_var[:, t, 0:1],
                              self.inv_deviation[:, t:t + 1], ALU.subtract, ALU.mult).then_inc(self.normed, 1)
            if transposed and t >= 2:
                self.split_low(dve, t - 2)
        if transposed:
            self.split_low(dve, TILES - 2)
            self.split_low(dve, TILES - 1)

    def split_low(self, dve, t):
        at = slice(t * P, (t + 1) * P)
        dve.wait_ge(self.hi_done, t + 1)
        dve.tensor_tensor(self.xT_lo[:, :, at], self.bank(t), self.xT_hi[:, :, at].bitcast(F32),
                          ALU.subtract).then_inc(self.lo_done, 1)

    def bank(self, t):
        return self.banks[t % 2][:, :].rearrange("p (k c) -> p k c", k=KC)

    def on_scalar(self, act, transposed=True):
        act.wait_ge(self.eps_set, 1)
        act.wait_ge(self.var_done, TILES)
        act.activation(self.deviation[:, :], self.mean_var[:, :, 1], ACT.Sqrt,
                       bias=self.eps[:, 0:1]).then_inc(self.sqrt_done, 1)
        if transposed:
            for t in range(TILES):
                act.wait_ge(self.turned, t + 1)
                act.activation(self.xT_hi[:, :, t * P:(t + 1) * P], self.bank(t), ACT.Copy).then_inc(self.hi_done, 1)

    def on_tensor(self, pe, tiles=range(TILES)):
        for t in tiles:
            pe.wait_ge(self.normed, t + 1)
            if t >= 2:
                pe.wait_ge(self.lo_done, t - 1)
            for k in range(KC):
                mm = pe.transpose(self.banks[t % 2][:, k * P:(k + 1) * P], self.rows[:, t, k * P:(k + 1) * P],
                                  self.ident[:, :])
            mm.then_inc(self.turned, 1)


def feed_forward0(nc, t, weight_stream, psum):
    ctx = ExitStack()
    with ctx:
        def sb(name, shape, dt=F32):
            return ctx.enter_context(nc.sbuf_tensor(name, shape, dt))

        sem = lambda name: ctx.enter_context(nc.semaphore(name))
        rows = t["rows"]
        xT_hi, xT_lo = (sb(f"f0_xT_{n}", [P, KC, TOK], F32R) for n in ("hi", "lo"))
        hT_hi, hT_lo = (sb(f"f0_hT_{n}", [P, F_TILES, TOK], F32R) for n in ("hi", "lo"))
        wg_hi, wg_lo, wu_hi, wu_lo = (sb(f"f0_w{n}", [P, KC, P], F32R) for n in ("g_hi", "g_lo", "u_hi", "u_lo"))
        wd_hi, wd_lo = (sb(f"f0_wd_{n}", [P, F_TILES, D], F32R) for n in ("hi", "lo"))
        staged = sb("f0_staged", [P, 3, 512])
        gated = sb("f0_gated", [P, BATCH, SEQ])
        hidden = sb("f0_hidden", [P, BATCH, SEQ])
        ps_g, ps_u, ps_y = psum[0:2], psum[2:4], psum[4:6]

        norm = t["norms"][0].attach(psum[6:8], xT_hi, xT_lo)
        next_norm = t["norms"][1]
        weight_in = {k: sem(f"f0_in_{k}") for k in "gud"}
        w_hi_done = {k: sem(f"f0_hi_{k}") for k in "gud"}
        w_lo_done = {k: sem(f"f0_lo_{k}") for k in "gud"}
        gate_ready, up_ready = sem("f0_gate_ready"), sem("f0_up_ready")
        gated_done, hidden_done = sem("f0_gated_done"), sem("f0_hidden_done")
        h_hi_done, h_lo_done = sem("f0_h_hi_done"), sem("f0_h_lo_done")
        y_ready, y_added = sem("f0_y_ready"), sem("f0_y_added")

        def dest(kind, f, hi):
            if kind == "d":
                return (wd_hi if hi else wd_lo)[:, bass.ds(f, 1), :].rearrange("p a c -> p (a c)")
            pair = {"g": (wg_hi, wg_lo), "u": (wu_hi, wu_lo)}[kind]
            return pair[0 if hi else 1][:, :, :].rearrange("p k c -> p (k c)")

        block = ctx.enter_context(nc.Block())

        @block.sync
        def _(sp):
            def load(f, kind):
                n = "gud".index(kind)
                sp.dma_start(staged[:, n, :], weight_stream[bass.ds(3 * f + n, 1), :, :].rearrange(
                    "a p c -> p (a c)")).then_inc(weight_in[kind], 16)

            for kind in "gud":
                load(0, kind)
            with sp.Fori(1, F_TILES) as f:
                for kind in "gud":
                    sp.wait_ge(w_lo_done[kind], f)
                    load(f, kind)

        @block.scalar
        def _(act):
            def split(kind, f):
                act.wait_ge(weight_in[kind], 16 * (f + 1))
                act.activation(dest(kind, f, True), staged[:, "gud".index(kind), :],
                               ACT.Copy).then_inc(w_hi_done[kind], 1)

            def gates(f):
                for b in range(BATCH):
                    act.wait_ge(gate_ready, 2 * f + b + 1)
                    act.activation(gated[:, b, :], ps_g[b][:, :], ACT.Silu).then_inc(gated_done, 1)

            def high(f):
                for b in range(BATCH):
                    act.wait_ge(hidden_done, 2 * f + b + 1)
                    act.activation(hT_hi[:, bass.ds(f, 1), b * SEQ:(b + 1) * SEQ].rearrange("p a c -> p (a c)"),
                                   hidden[:, b, :], ACT.Copy).then_inc(h_hi_done, 1)

            split("g", 0)
            split("u", 0)
            norm.on_scalar(act)
            with act.Fori(0, F_TILES - 1) as f:
                gates(f)
                split("g", f + 1)
                split("d", f)
                high(f)
                act.wait_ge(up_ready, 2 * f + 2)
                split("u", f + 1)
            gates(F_TILES - 1)
            split("d", F_TILES - 1)
            high(F_TILES - 1)

        @block.gpsimd
        def _(pool):
            def rest(kind, f):
                pool.wait_ge(w_hi_done[kind], f + 1)
                pool.tensor_tensor(dest(kind, f, False), staged[:, "gud".index(kind), :],
                                   dest(kind, f, True).bitcast(F32), ALU.subtract).then_inc(w_lo_done[kind], 1)

            rest("g", 0)
            rest("u", 0)
            with pool.Fori(0, F_TILES - 1) as f:
                rest("g", f + 1)
                rest("d", f)
                rest("u", f + 1)
            rest("d", F_TILES - 1)

        @block.vector
        def _(dve):
            norm.on_vector(dve)
            with dve.Fori(0, F_TILES) as f:
                for b in range(BATCH):
                    dve.wait_ge(up_ready, 2 * f + b + 1)
                    dve.wait_ge(gated_done, 2 * f + b + 1)
                    dve.tensor_tensor(hidden[:, b, :], ps_u[b][:, :], gated[:, b, :], ALU.mult).then_inc(hidden_done, 1)
                for b in range(BATCH):
                    at = lambda x: x[:, bass.ds(f, 1), b * SEQ:(b + 1) * SEQ].rearrange("p a c -> p (a c)")
                    dve.wait_ge(h_hi_done, 2 * f + b + 1)
                    dve.tensor_tensor(at(hT_lo), hidden[:, b, :], at(hT_hi).bitcast(F32),
                                      ALU.subtract).then_inc(h_lo_done, 1)
                dve.wait_ge(h_lo_done, 2 * f + 2)
            for tile in range(TILES):
                dve.wait_ge(y_ready, tile + 1)
                dve.tensor_tensor(rows[:, tile, :], ps_y[tile % 2][:, :], rows[:, tile, :],
                                  ALU.add).then_inc(y_added, 1)
                dve.wait_ge(y_added, tile + 1)
                next_norm.take(dve, tile)

        @block.tensor
        def _(pe):
            norm.on_tensor(pe)
            with pe.Fori(0, F_TILES) as f:
                pe.wait_ge(w_lo_done["g"], f + 1)
                for b in range(BATCH):
                    pe.wait_ge(norm.lo_done, (b + 1) * SEQ_TILES)
                    three(pe, ps_g[b][:, :], [(wg_hi[:, k, :], wg_lo[:, k, :], xT_hi[:, k, b * SEQ:(b + 1) * SEQ],
                                               xT_lo[:, k, b * SEQ:(b + 1) * SEQ]) for k in range(KC)], gate_ready)
                pe.wait_ge(w_lo_done["u"], f + 1)
                for b in range(BATCH):
                    three(pe, ps_u[b][:, :], [(wu_hi[:, k, :], wu_lo[:, k, :], xT_hi[:, k, b * SEQ:(b + 1) * SEQ],
                                               xT_lo[:, k, b * SEQ:(b + 1) * SEQ]) for k in range(KC)], up_ready)
            pe.wait_ge(w_lo_done["d"], F_TILES)
            pe.wait_ge(h_lo_done, 2 * F_TILES)
            for tile in range(TILES):
                if tile >= 2:
                    pe.wait_ge(y_added, tile - 1)
                at = slice(tile * P, (tile + 1) * P)
                three(pe, ps_y[tile % 2][:, :], [(hT_hi[:, f, at], hT_lo[:, f, at], wd_hi[:, f, :], wd_lo[:, f, :])
                                                 for f in range(F_TILES)], y_ready)


def layout_ffn0(inputs):
    pad = F_TILES * P - F0
    blocks = []
    up, gate = (np.pad(inputs[n], ((0, pad), (0, 0))).T.reshape(KC, P, F_TILES, P).transpose(2, 1, 0, 3)
                for n in ("L0_ffn_W_up", "L0_ffn_W_gate"))
    down = np.pad(inputs["L0_ffn_W_down"], ((0, 0), (0, pad))).T.reshape(F_TILES, P, D)
    for f in range(F_TILES):
        blocks += [gate[f].reshape(P, 512), up[f].reshape(P, 512), down[f]]
    return {"weights_f0": np.stack(blocks)}

HEADS1, KV1 = 32, 8
HD1 = D // HEADS1
GROUP1 = HEADS1 // KV1
SCALE1 = HD1 ** -0.5
GQ = GROUP1 * HD1
PARTS = 3
STACK = PARTS * HD1
PAIR = 2 * STACK
QUAD = 32
UNITS1 = KV1 * BATCH
PADS = 7
SCORE_BLOCKS = ([(3, h, 1) for h in range(GROUP1)] + [(2, h, 1) for h in range(GROUP1)] + [(1, 0, 2), (1, 2, 2)]
                + [(0, 0, 2), (0, 2, 2)])
STACK_BLOCKS = 3
PER_UNIT = STACK_BLOCKS + len(SCORE_BLOCKS)
TURNED_SCORES = {0: (0, 0, 0), 1: (1, 0, 1), 3: (2, 0, 2), 2: (2, 2 * P, 2)}
EXP_SPANS = [(0, SEQ, 0), (0, 3 * P, SEQ), (P, 3 * P, SEQ + 4 * P)]
HEAD_PROBS = SEQ + 7 * P
PROBS_AT = {0: 0, 1: SEQ, 3: SEQ + 3 * P, 2: SEQ + 5 * P}
SPLIT_SPANS = [(0, SEQ + 3 * P), (SEQ + 4 * P, HEAD_PROBS)]
HALF = P // 2
LOW_HEAD = GROUP1 - 1


def attention1(nc, t, w_qkv, w_o, cos_in, sin_in, mask_in, ones_in, psum):
    ctx = ExitStack()
    with ctx:
        def sb(name, shape, dt=F32):
            return ctx.enter_context(nc.sbuf_tensor("a1_" + name, shape, dt))

        sem = lambda name: ctx.enter_context(nc.semaphore("a1_" + name))
        rows, ident = t["rows"], t["ident"]
        KVW = 2 * KV1 * HD1
        xT = sb("xT", [P, 2, KC, TOK], F32R)
        xT_hi, xT_lo = xT[:, 0, :, :], xT[:, 1, :, :]
        w_hi, w_lo = (sb(f"w_{n}", [P, KC, D + KVW], F32R) for n in ("hi", "lo"))
        wo_hi, wo_lo = w_hi[:, :, 0:D], w_lo[:, :, 0:D]
        staged = sb("staged", [P, 2, D + KVW])
        q_tok = sb("q_tok", [P, TILES, (KV1 + 1) * GQ])
        k_tok = sb("k_tok", [P, TILES, (KV1 + 1) * HD1])
        v_tok = sb("v_tok", [P, TILES, (KV1 + 1) * HD1])
        q_parts = sb("q_parts", [P, SEQ_TILES, GROUP1, PARTS, HD1], F32R)
        k_parts = sb("k_parts", [P, SEQ_TILES, STACK + STACK + STACK], F32R)
        q_stack = sb("q_stack", [P, 2, TOK], F32R)
        k_stack = sb("k_stack", [P, 2, TOK], F32R)
        v_now = sb("v_now", [P, TILES, 3 * HALF], F32R)
        v_at = HALF
        probs_T = sb("probs_T", [P, GROUP1, HEAD_PROBS])
        ones_staged = probs_T[PAIR:P, 0:2, 0:TOK]
        probs_lo = sb("probs_lo", [P, GROUP1, HEAD_PROBS], F32R)
        probs_hi = xT[:, :, :, :].rearrange("p a k c -> p (a k c)")[:, 0:GROUP1 * HEAD_PROBS].rearrange(
            "p (h c) -> p h c", h=GROUP1)
        oT_now = sb("oT_now", [P, SEQ])
        o_tok = sb("o_tok", [P, TILES, D])
        cos = sb("cos", [P, SEQ_TILES, HD1])
        sin = sb("sin", [P, SEQ_TILES, HD1])
        mask = sb("mask", [P, 2 * P])
        mask_half = sb("mask_half", [P, 2 * P], BF16)
        ident_half = sb("ident_half", [P, P], BF16)
        ident_r = sb("ident_r", [P, P], F32R)
        by_cos = sb("by_cos", [P, D + KV1 * HD1])
        by_sin = sb("by_sin", [P, D + KV1 * HD1])
        row_max = sb("row_max", [P, SEQ_TILES, GROUP1])
        neg_max = sb("neg_max", [P, SEQ_TILES, GROUP1])
        max_parts = sb("max_parts", [P, SEQ_TILES, P // QUAD, QUAD], F32R)
        inv_sum = sb("inv_sum", [P, SEQ_TILES, 2])
        o_sum = sb("o_sum", [P, SEQ_TILES, 2, HD1])

        norm = t["norms"][1].attach(psum[4:6], xT_hi, xT_lo)
        next_norm = t["norms"][2]
        ps_q, ps_kv = psum[0:2], psum[2:4]
        ps_exp, ps_o, ps_s, ps_turn = psum[0:3], psum[3], psum[4:7], psum[7]
        ps_y = psum[0:2]

        constants_in = sem("constants_in")
        weight_in = [sem(f"weight_in{k}") for k in range(KC)]
        w_hi_done, w_lo_done, ident_done, pads_set = sem("w_hi_done"), sem("w_lo_done"), sem("ident_done"), sem("pads_set")
        v_now_cleared, gaps_set = sem("v_now_cleared"), sem("gaps_set")
        qkv_ready, cos_done, sin_done, v_done = sem("qkv_ready"), sem("cos_done"), sem("sin_done"), sem("v_done")
        tok_done = sem("tok_done")
        part_hi, part_lo, v_hi_done, v_lo_done = sem("part_hi"), sem("part_lo"), sem("v_hi_done"), sem("v_lo_done")
        scored, score_read, turn_ready, turn_read = sem("scored"), sem("score_read"), sem("turn_ready"), sem("turn_read")
        maxed, neg_done, max_hi_done, max_done = sem("maxed"), sem("neg_done"), sem("max_hi_done"), sem("max_done")
        exp_ready, exp_done, probs_hi_done = sem("exp_ready"), sem("exp_done"), sem("probs_hi_done")
        probs_lo_done, last_lo_done = sem("probs_lo_done"), sem("last_lo_done")
        o_ready, o_read, inv_done, summed = sem("o_ready"), sem("o_read"), sem("inv_done"), sem("summed")
        out_turned, out_hi, out_lo = sem("out_turned"), sem("out_hi"), sem("out_lo")
        y_ready, y_added = sem("y_ready"), sem("y_added")

        half = HD1 // 2
        block = ctx.enter_context(nc.Block())

        def weight_block(k):
            hi, lo = (w_hi, w_lo) if k < KC else (wo_hi, wo_lo)
            width = D + KVW if k < KC else D
            raw = probs_T[:, k, 0:width] if k in (2, 3) else staged[:, k % 2, 0:width]
            return hi[:, k % KC, :], lo[:, k % KC, :], raw

        @block.sync
        def _(sp):
            for k in range(KC):
                sp.dma_start(weight_block(k)[2], w_qkv[k]).then_inc(weight_in[k % KC], 16)
            sp.dma_start(cos[:, :, :], cos_in).then_inc(constants_in, 16)
            sp.dma_start(sin[:, :, :], sin_in).then_inc(constants_in, 16)
            sp.dma_start(mask[:, :], mask_in).then_inc(constants_in, 16)
            sp.dma_start(ones_staged, ones_in).then_inc(constants_in, 16)
            for k in range(KC, 2 * KC):
                sp.wait_ge(w_lo_done, KC if k < KC + 2 else k - 1)
                sp.dma_start(weight_block(k)[2], w_o[k - KC]).then_inc(weight_in[k % KC], 16)

        def q_part(n):
            return q_parts[:, :, :, n, :]

        def k_part(n):
            return k_parts[:, :, STACK + n * HD1:STACK + (n + 1) * HD1]

        def batch_tiles(b):
            return slice(b * SEQ_TILES, (b + 1) * SEQ_TILES)

        def q_of(g, b):
            return q_tok[:, batch_tiles(b), bass.ds(g * GQ, GQ)].rearrange("p t (h d) -> p t h d", d=HD1)

        def k_of(g, b):
            return k_tok[:, batch_tiles(b), bass.ds(g * HD1, HD1)]

        FIRST_TURNED = 3

        def next_maxima_at(u):
            return 4 * u + FIRST_TURNED

        def output_at(u, pair):
            return 4 * u + FIRST_TURNED + 1 + 2 * pair

        def later_keys_at(u):
            return 4 * u + FIRST_TURNED + 2

        def split_low(engine, u, h, done):
            for n, (first, end) in enumerate(SPLIT_SPANS):
                engine.wait_ge(probs_hi_done, 2 * (GROUP1 * u + h) + n + 1)
                engine.tensor_tensor(probs_lo[:, h, first:end], probs_T[:, h, first:end],
                                     probs_hi[:, h, first:end].bitcast(F32), ALU.subtract).then_inc(done, 1)

        @block.scalar
        def _(act):
            def high_weight(k):
                act.wait_ge(weight_in[k % KC], 16 * (k // KC + 1))
                hi, _, raw = weight_block(k)
                act.activation(hi, raw, ACT.Copy).then_inc(w_hi_done, 1)

            norm.on_scalar(act, transposed=False)
            high_weight(0)
            for tile in range(TILES):
                if tile < KC - 1:
                    high_weight(tile + 1)
                act.wait_ge(norm.turned, tile + 1)
                act.activation(xT_hi[:, :, tile * P:(tile + 1) * P], norm.bank(tile), ACT.Copy).then_inc(norm.hi_done, 1)
            def copy_values(tile):
                act.wait_ge(sin_done, 4 * (tile + 1))
                act.activation(v_tok[:, tile, 0:KV1 * HD1], ps_kv[tile % 2][:, KV1 * HD1:KVW], ACT.Copy).then_inc(v_done, 1)

            def high_parts(g, b):
                for n in (0, 1):
                    act.activation(q_part(n), q_of(g, b), ACT.Copy).then_inc(part_hi, 1)
                for n in (0, 2):
                    act.activation(k_part(n), k_of(g, b), ACT.Copy).then_inc(part_hi, 1)

            def values(g, b):
                act.activation(v_now[:, batch_tiles(b), v_at:v_at + HD1],
                               v_tok[:, batch_tiles(b), bass.ds(g * HD1, HD1)], ACT.Copy).then_inc(v_hi_done, 1)

            def last_keys(b, at):
                act.wait_ge(turn_ready, at + 1)
                act.activation(k_stack[0:PAIR, 1, b * SEQ:(b + 1) * SEQ], ps_turn[0:PAIR, :],
                               ACT.Copy).then_inc(turn_read, 1)

            def maxima(b, at):
                act.wait_ge(turn_ready, at + 1)
                for pair in range(2):
                    copied = act.activation(q_stack[PAIR:P, pair, b * SEQ:(b + 1) * SEQ],
                                            ps_turn[pair * QUAD:(pair + 1) * QUAD, :], ACT.Copy)
                copied.then_inc(turn_read, 1)

            def exps(u, h):
                for bank, (first, n, to) in enumerate(EXP_SPANS):
                    act.wait_ge(exp_ready, 3 * (GROUP1 * u + h) + bank + 1)
                    act.activation(probs_T[:, h, to:to + n], ps_exp[bank][:, first:first + n], ACT.Exp,
                                   scale=SCALE1).then_inc(exp_done, 1)

            def high_probs(u, h):
                act.wait_ge(exp_done, 3 * (GROUP1 * u + h + 1))
                for first, end in SPLIT_SPANS:
                    act.activation(probs_hi[:, h, first:end], probs_T[:, h, first:end],
                                   ACT.Copy).then_inc(probs_hi_done, 1)

            def evacuate(u, pair):
                act.wait_ge(o_ready, 2 * u + pair + 1)
                act.activation(oT_now[:, :], ps_o[:, :], ACT.Copy).then_inc(o_read, 1)

            for tile in range(TILES):
                if tile == 5:
                    act.wait_ge(tok_done, 2 * SEQ_TILES)
                    act.wait_ge(pads_set, PADS)
                    high_parts(0, 0)
                if tile == TILES - 1:
                    last_keys(0, 0)
                copy_values(tile)
                if tile == 3:
                    act.activation(ident_r[:, :], ident[:, :], ACT.Copy).then_inc(ident_done, 1)
                    act.activation(ident_half[:, :], ident[:, :], ACT.Copy).then_inc(ident_done, 1)
                    act.wait_ge(constants_in, 64)
                    act.activation(mask_half[:, :], mask[:, :], ACT.Copy).then_inc(ident_done, 1)
                    act.activation(k_stack[PAIR:P, :, :], ones_staged, ACT.Copy).then_inc(ident_done, 1)
            act.wait_ge(tok_done, 2 * TILES)
            high_parts(0, 1)
            act.wait_ge(v_done, TILES)
            values(0, 0)
            values(0, 1)
            maxima(0, 1)
            last_keys(1, 2)
            for h in (0, 1):
                exps(0, h)
                high_probs(0, h)
            for k in range(KC, 2 * KC):
                high_weight(k)
            with act.Fori(0, KV1) as g:
                for b in range(BATCH):
                    u = BATCH * g + b
                    exps(u, 2)
                    high_probs(u, 2)
                    high_parts(g + 1, b)
                    exps(u, 3)
                    high_probs(u, 3)
                    evacuate(u, 0)
                    maxima(1 - b, next_maxima_at(u))
                    exps(u + 1, 0)
                    high_probs(u + 1, 0)
                    last_keys(b, later_keys_at(u))
                    exps(u + 1, 1)
                    evacuate(u, 1)
                    high_probs(u + 1, 1)
                    values(g + 1, b)
            for tile in range(TILES):
                act.wait_ge(out_turned, tile + 1)
                act.activation(xT_hi[:, :, tile * P:(tile + 1) * P], norm.bank(tile), ACT.Copy).then_inc(out_hi, 1)

        @block.gpsimd
        def _(pool):
            pool.memset(q_tok[:, :, KV1 * GQ:], 0.0).then_inc(pads_set, 1)
            pool.memset(k_tok[:, :, KV1 * HD1:], 0.0).then_inc(pads_set, 1)
            pool.memset(v_tok[:, :, KV1 * HD1:], 0.0).then_inc(pads_set, 1)
            pool.memset(v_now[:, :, :].bitcast(F32), 0.0).then_inc(v_now_cleared, 1)
            pool.wait_ge(v_now_cleared, 1)
            pool.memset(v_now[:, :, v_at + HD1:v_at + HD1 + 1].bitcast(F32), 1.0).then_inc(pads_set, 1)
            pool.memset(k_parts[:, :, 0:STACK].bitcast(F32), 0.0).then_inc(pads_set, 1)
            pool.memset(k_parts[:, :, 2 * STACK:].bitcast(F32), 0.0).then_inc(pads_set, 1)
            pool.memset(max_parts[:, :, :, :].bitcast(F32), 0.0).then_inc(pads_set, 1)

            def weights(ks):
                for k in ks:
                    hi, lo, raw = weight_block(k)
                    pool.wait_ge(w_hi_done, k + 1)
                    pool.tensor_tensor(lo, raw, hi.bitcast(F32), ALU.subtract).then_inc(w_lo_done, 1)

            weights(range(KC))
            for tile in range(TILES):
                pool.wait_ge(sin_done, 4 * (tile + 1))
                pool.tensor_tensor(q_tok[:, tile, 0:D], by_cos[:, 0:D], by_sin[:, 0:D], ALU.add).then_inc(tok_done, 1)
                pool.tensor_tensor(k_tok[:, tile, 0:KV1 * HD1], by_cos[:, D:], by_sin[:, D:], ALU.add).then_inc(tok_done, 1)
            pool.wait_ge(qkv_ready, 2 * TILES)
            for part in (probs_hi, probs_lo):
                pool.memset(part[:, :, SPLIT_SPANS[0][1]:SPLIT_SPANS[1][0]].bitcast(F32), 0.0).then_inc(gaps_set, 1)
            weights(range(KC, 2 * KC))
            with pool.Fori(0, KV1) as g:
                for b in range(BATCH):
                    split_low(pool, BATCH * g + b, LOW_HEAD, last_lo_done)

        @block.vector
        def _(dve):
            norm.on_vector(dve)
            dve.wait_ge(constants_in, 64)

            def rotate(tile):
                q_in = ps_q[tile % 2][:, 0:D].rearrange("p (h d) -> p h d", d=HD1)
                k_in = ps_kv[tile % 2][:, 0:KV1 * HD1].rearrange("p (h d) -> p h d", d=HD1)
                c, s_ = cos[:, tile % SEQ_TILES, :], sin[:, tile % SEQ_TILES, :]
                dve.wait_ge(qkv_ready, 2 * (tile + 1))
                if tile >= 1:
                    dve.wait_ge(tok_done, 2 * tile)
                for source, n, at in ((q_in, HEADS1, 0), (k_in, KV1, D)):
                    out = by_cos[:, at:at + n * HD1].rearrange("p (h d) -> p h d", d=HD1)
                    dve.tensor_tensor(out, source, c.rearrange("p (a d) -> p a d", a=1).broadcast_to([P, n, HD1]),
                                      ALU.mult).then_inc(cos_done, 1)
                    out = by_sin[:, at:at + n * HD1].rearrange("p (h d) -> p h d", d=HD1)
                    for to, of in ((slice(0, half), slice(half, HD1)), (slice(half, HD1), slice(0, half))):
                        dve.tensor_tensor(out[:, :, to], source[:, :, of],
                                          s_[:, to].rearrange("p (a d) -> p a d", a=1).broadcast_to([P, n, half]),
                                          ALU.mult).then_inc(sin_done, 1)

            def low_parts(g, b):
                dve.wait_ge(part_hi, 4 * (BATCH * g + b + 1))
                dve.tensor_tensor(q_part(2), q_of(g, b), q_part(0).bitcast(F32), ALU.subtract).then_inc(part_lo, 1)
                dve.tensor_tensor(k_part(1), k_of(g, b), k_part(0).bitcast(F32), ALU.subtract).then_inc(part_lo, 1)

            def stacks(u, b):
                for n in range(STACK_BLOCKS):
                    to = (q_stack if n < 2 else k_stack)[0:PAIR, n % 2, b * SEQ:(b + 1) * SEQ]
                    dve.wait_ge(scored, PER_UNIT * u + n + 1)
                    dve.tensor_copy(to, ps_s[n][0:PAIR, :]).then_inc(score_read, 1)

            def maxima(u, blocks):
                for n in blocks:
                    qt, h, heads_n = SCORE_BLOCKS[n]
                    seen = (qt + 1) * P
                    bank = ps_s[(STACK_BLOCKS + n) % 3]
                    dve.wait_ge(scored, PER_UNIT * u + STACK_BLOCKS + n + 1)
                    if heads_n == 1:
                        dve.tensor_reduce(row_max[:, qt, h:h + 1], bank[:, 0:seen], mybir.AxisListType.X,
                                          ALU.max).then_inc(score_read, 1)
                    else:
                        dve.tensor_reduce(row_max[:, qt, h:h + 2],
                                          bank[:, :].rearrange("p (h c) -> p h c", h=2)[:, :, 0:seen],
                                          mybir.AxisListType.X, ALU.max).then_inc(score_read, 1)

            def split_maxima(u):
                part = lambda n: max_parts[:, :, 0:2, n:4:2]
                by_pair = lambda x: x[:, :, :].rearrange("p t (a h) -> p t a h", a=2)
                dve.wait_ge(score_read, PER_UNIT * (u + 1))
                dve.tensor_scalar(neg_max[:, :, :], row_max[:, :, :], -1.0, None, ALU.mult).then_inc(neg_done, 1)
                dve.wait_ge(neg_done, u + 1)
                dve.tensor_copy(part(0), by_pair(neg_max)).then_inc(max_hi_done, 1)
                dve.wait_ge(max_hi_done, u + 1)
                dve.tensor_tensor(part(1), by_pair(neg_max), part(0).bitcast(F32), ALU.subtract).then_inc(max_done, 1)

            def low_values(g, b):
                dve.wait_ge(v_hi_done, BATCH * g + b + 1)
                dve.tensor_tensor(v_now[:, batch_tiles(b), v_at + QUAD:v_at + QUAD + HD1],
                                  v_tok[:, batch_tiles(b), bass.ds(g * HD1, HD1)],
                                  v_now[:, batch_tiles(b), v_at:v_at + HD1].bitcast(F32),
                                  ALU.subtract).then_inc(v_lo_done, 1)

            def finish(u, g, b, pair):
                turned = ps_turn[:, :].rearrange("p (t h d) -> p t h d", t=SEQ_TILES, h=2)
                at = g * GQ + pair * 2 * HD1
                dve.wait_ge(turn_ready, output_at(u, pair) + 1)
                dve.reciprocal(inv_sum[:, :, :], turned[:, :, :, HD1]).then_inc(inv_done, 1)
                dve.tensor_copy(o_sum[:, :, :, :], turned[:, :, :, QUAD:QUAD + HD1]).then_inc(summed, 1)
                dve.wait_ge(summed, 2 * (2 * u + pair) + 1)
                dve.tensor_tensor(o_sum[:, :, :, :], turned[:, :, :, 0:HD1], o_sum[:, :, :, :],
                                  ALU.add).then_inc(summed, 1)
                dve.wait_ge(inv_done, 2 * u + pair + 1)
                dve.wait_ge(summed, 2 * (2 * u + pair) + 2)
                dve.tensor_tensor(
                    o_tok[:, batch_tiles(b), bass.ds(at, 2 * HD1)].rearrange("p t (h d) -> p t h d", d=HD1),
                    o_sum[:, :, :, :],
                    inv_sum[:, :, :].rearrange("p t (h a) -> p t h a", a=1).broadcast_to([P, SEQ_TILES, 2, HD1]),
                    ALU.mult).then_inc(turn_read, 1)

            dve.wait_ge(pads_set, PADS)
            for tile in range(TILES):
                rotate(tile)
                if tile == 5:
                    low_parts(0, 0)
                if tile == 6:
                    stacks(0, 0)
            maxima(0, range(12))
            low_parts(0, 1)
            low_values(0, 0)
            low_values(0, 1)
            split_maxima(0)
            stacks(1, 1)
            maxima(1, range(0, 4))
            split_low(dve, 0, 0, probs_lo_done)
            with dve.Fori(0, KV1) as g:
                for b in range(BATCH):
                    u = BATCH * g + b
                    maxima(u + 1, range(4, 8))
                    split_low(dve, u, 1, probs_lo_done)
                    maxima(u + 1, range(8, 12))
                    split_maxima(u + 1)
                    low_parts(g + 1, b)
                    split_low(dve, u, 2, probs_lo_done)
                    stacks(u + 2, b)
                    finish(u, g, b, 0)
                    split_low(dve, u + 1, 0, probs_lo_done)
                    maxima(u + 2, range(0, 4))
                    low_values(g + 1, b)
                    finish(u, g, b, 1)
            for tile in range(TILES):
                at = slice(tile * P, (tile + 1) * P)
                dve.wait_ge(out_hi, tile + 1)
                dve.tensor_tensor(xT_lo[:, :, at], norm.bank(tile), xT_hi[:, :, at].bitcast(F32),
                                  ALU.subtract).then_inc(out_lo, 1)
            for tile in range(TILES):
                dve.wait_ge(y_ready, tile + 1)
                dve.tensor_tensor(rows[:, tile, :], ps_y[tile % 2][:, :], rows[:, tile, :], ALU.add).then_inc(y_added, 1)
                dve.wait_ge(y_added, tile + 1)
                next_norm.take(dve, tile)

        @block.tensor
        def _(pe):
            def first_unit(u):
                return isinstance(u, int) and u == 0

            def stack(u, n, at):
                bank = ps_s[n] if n < STACK_BLOCKS else ps_turn
                if n < STACK_BLOCKS:
                    if not first_unit(u):
                        pe.wait_ge(score_read, PER_UNIT * u + n - 2)
                elif not first_unit(u):
                    pe.wait_ge(turn_read, at)
                for j in range(SEQ_TILES):
                    if n < 2:
                        source = q_parts[:, j, 2 * n:2 * n + 2, :, :].rearrange("p h n d -> p (h n d)")
                    else:
                        first = STACK if n == 2 else 0
                        source = k_parts[:, j, first:first + PAIR]
                    mm = pe.transpose(bank[0:PAIR, j * P:(j + 1) * P].bitcast(F32R), source, ident_r[:, :])
                mm.then_inc(scored if n < STACK_BLOCKS else turn_ready, 1)

            def stacks(u, at, blocks):
                if 0 in blocks:
                    pe.wait_ge(part_hi, 4 * (u + 1))
                    pe.wait_ge(part_lo, 2 * (u + 1))
                for n in blocks:
                    stack(u, n, at)

            def score(u, b, blocks):
                for n in blocks:
                    qt, first, heads_n = SCORE_BLOCKS[n]
                    width = max(qt + 1, 2) * P
                    row = b * SEQ + qt * P
                    bank = ps_s[(STACK_BLOCKS + n) % 3]
                    pe.wait_ge(score_read, PER_UNIT * u + STACK_BLOCKS + max(n - 2, 0))
                    for i in range(heads_n):
                        h = first + i
                        pe.matmul(bank[:, i * width:(i + 1) * width], q_stack[0:PAIR, h // 2, row:row + P],
                                  k_stack[0:PAIR, h % 2, b * SEQ:b * SEQ + width], start=True, stop=False)
                        own = i * width + qt * P
                        mm = pe.matmul(bank[:, own:own + P], ident_half[:, :], mask_half[:, 0:P], start=False, stop=True)
                    mm.then_inc(scored, 1)

            def score_turned(u, b, h):
                for kb, (bank, at, qt) in TURNED_SCORES.items():
                    if at == 0 and not (first_unit(u) and h == 0):
                        pe.wait_ge(exp_done, 3 * (GROUP1 * u + h - 1) + bank + 1)
                    width = SEQ - qt * P
                    own = at + (kb - qt) * P
                    pe.matmul(ps_exp[bank][:, at:at + width], k_stack[:, h % 2, b * SEQ + kb * P:b * SEQ + (kb + 1) * P],
                              q_stack[:, h // 2, b * SEQ + qt * P:(b + 1) * SEQ], start=True, stop=False)
                    mm = pe.matmul(ps_exp[bank][:, own:own + P], ident_half[:, :], mask_half[:, P:2 * P],
                                   start=False, stop=True)
                    if kb != 3:
                        mm.then_inc(exp_ready, 1)

            def apply(u, b, h):
                if h == 0:
                    pe.wait_ge(v_lo_done, u + 1)
                if h == 2:
                    pe.wait_ge(o_read, 2 * u + 1)
                for kb in (0, 1, 3, 2):
                    if kb in (0, 3):
                        lo_done, blocks = (last_lo_done, u) if h == LOW_HEAD else (probs_lo_done, LOW_HEAD * u + h)
                        pe.wait_ge(lo_done, 2 * blocks + (1 if kb == 0 else 2))
                    qt = TURNED_SCORES[kb][2]
                    window = v_at - (h % 2) * HALF
                    for part in (probs_hi, probs_lo):
                        mm = pe.matmul(ps_o[:, qt * P:SEQ], v_now[:, b * SEQ_TILES + kb, window:window + P],
                                       part[:, h, PROBS_AT[kb]:PROBS_AT[kb] + SEQ - qt * P],
                                       start=(kb == 0 and h % 2 == 0 and part is probs_hi),
                                       stop=(kb == 2 and h % 2 == 1 and part is probs_lo))
                if h % 2 == 1:
                    mm.then_inc(o_ready, 1)

            def turn_maxima(u, at):
                pe.wait_ge(max_done, u + 1)
                pe.wait_ge(turn_read, at)
                for j in range(SEQ_TILES):
                    mm = pe.transpose(ps_turn[:, j * P:(j + 1) * P].bitcast(F32R),
                                      max_parts[:, j, :, :].rearrange("p a c -> p (a c)"), ident_r[:, :])
                mm.then_inc(turn_ready, 1)

            def turn_output(u, pair):
                pe.wait_ge(o_read, 2 * u + pair + 1)
                pe.wait_ge(turn_read, output_at(u, pair))
                for j in range(SEQ_TILES):
                    mm = pe.transpose(ps_turn[:, j * P:(j + 1) * P], oT_now[:, j * P:(j + 1) * P], ident[:, :])
                mm.then_inc(turn_ready, 1)

            norm.on_tensor(pe, range(0, 4))
            pe.wait_ge(w_lo_done, KC)
            for tile in range(TILES):
                at = slice(tile * P, (tile + 1) * P)
                if tile == TILES - 1:
                    pe.wait_ge(ident_done, 4)
                    pe.wait_ge(pads_set, PADS)
                    stacks(0, 0, range(4))
                pe.wait_ge(norm.lo_done, tile + 1)
                if tile >= 2:
                    pe.wait_ge(v_done, tile - 1)
                three(pe, ps_q[tile % 2][:, :], [(xT_hi[:, k, at], xT_lo[:, k, at], w_hi[:, k, 0:D], w_lo[:, k, 0:D])
                                                 for k in range(KC)], qkv_ready)
                three(pe, ps_kv[tile % 2][:, 0:KVW], [(xT_hi[:, k, at], xT_lo[:, k, at], w_hi[:, k, D:], w_lo[:, k, D:])
                                                      for k in range(KC)], qkv_ready)
                if tile < 2:
                    norm.on_tensor(pe, range(4 + 2 * tile, 6 + 2 * tile))
            pe.wait_ge(turn_read, 1)
            score(0, 0, range(12))
            turn_maxima(0, 1)
            stacks(1, 2, range(4))
            score_turned(0, 0, 0)
            score_turned(0, 0, 1)
            pe.wait_ge(turn_read, 3)
            score(1, 1, range(0, 4))
            pe.wait_ge(gaps_set, 2)
            with pe.Fori(0, KV1) as g:
                for b in range(BATCH):
                    u = BATCH * g + b
                    score_turned(u, b, 2)
                    score(u + 1, 1 - b, range(4, 7))
                    apply(u, b, 0)
                    score(u + 1, 1 - b, range(7, 8))
                    score_turned(u, b, 3)
                    score(u + 1, 1 - b, range(8, 12))
                    apply(u, b, 1)
                    turn_maxima(u + 1, next_maxima_at(u))
                    stacks(u + 2, 0, range(0, 3))
                    apply(u, b, 2)
                    turn_output(u, 0)
                    score_turned(u + 1, 1 - b, 0)
                    stacks(u + 2, later_keys_at(u), range(3, 4))
                    score_turned(u + 1, 1 - b, 1)
                    apply(u, b, 3)
                    pe.wait_ge(turn_read, later_keys_at(u) + 1)
                    score(u + 2, b, range(0, 4))
                    turn_output(u, 1)
            pe.wait_ge(turn_read, 4 * UNITS1 + FIRST_TURNED)
            pe.wait_ge(score_read, PER_UNIT * (UNITS1 + 1) + STACK_BLOCKS + 4)
            for tile in range(TILES):
                if tile >= 2:
                    pe.wait_ge(out_lo, tile - 1)
                for k in range(KC):
                    mm = pe.transpose(norm.banks[tile % 2][:, k * P:(k + 1) * P], o_tok[:, tile, k * P:(k + 1) * P],
                                      ident[:, :])
                mm.then_inc(out_turned, 1)
            pe.wait_ge(w_lo_done, 2 * KC)
            pe.wait_ge(out_lo, TILES)
            pe.wait_ge(exp_done, 3 * (GROUP1 * UNITS1 + 2))
            for tile in range(TILES):
                if tile >= 2:
                    pe.wait_ge(y_added, tile - 1)
                at = slice(tile * P, (tile + 1) * P)
                three(pe, ps_y[tile % 2][:, :], [(xT_hi[:, k, at], xT_lo[:, k, at], wo_hi[:, k, :], wo_lo[:, k, :])
                                                 for k in range(KC)], y_ready)


def layout1(inputs):
    qkv = np.concatenate([inputs["L1_attn_Wq"], inputs["L1_attn_Wk"], inputs["L1_attn_Wv"]], 1)
    return {"weights_qkv1": qkv.reshape(KC, P, D + 2 * KV1 * HD1), "weights_o1": inputs["L1_attn_Wo"].reshape(KC, P, D)}


def tables1():
    inv = (1.0 / 500000.0 ** (np.arange(0, HD1, 2, dtype=np.float32) / HD1)).astype(np.float32)
    ang = np.arange(SEQ, dtype=np.float32)[:, None] * inv[None, :]
    tile = lambda a: np.ascontiguousarray(a.astype(np.float32).reshape(SEQ_TILES, P, HD1).transpose(1, 0, 2))
    q, k = np.arange(P)[:, None], np.arange(P)[None, :]
    mask = np.where(k <= q, 0, MASKED).astype(np.float32)
    ones = np.zeros((QUAD, 2, TOK), np.float32)
    ones[0:2, 0] = ones[2:4, 1] = 1
    return {"cos1": tile(np.concatenate([np.cos(ang), np.cos(ang)], 1)),
            "sin1": tile(np.concatenate([-np.sin(ang), np.sin(ang)], 1)),
            "mask1": np.concatenate([mask, mask.T], 1), "ones1": ones}



EXPERTS, RANK, GATE_H = 8, 16, 32
LORA = EXPERTS * RANK
CAPACITY = int(3.0 * TOK / EXPERTS)
ALPHA = 1.0 / RANK
SIDE = 256
SMALL = {"gb1": GATE_H, "gamma": GATE_H, "beta": GATE_H, "gw2": EXPERTS * GATE_H, "gb2": EXPERTS, "index": EXPERTS}
AHEAD = 6


def feed_forward1(nc, t, w_in, lora_b_in, small_in, out, psum):
    ctx = ExitStack()
    with ctx:
        def sb(name, shape, dt=F32):
            return ctx.enter_context(nc.sbuf_tensor("f1_" + name, shape, dt))

        sem = lambda name: ctx.enter_context(nc.semaphore("f1_" + name))
        rows, ident = t["rows"], t["ident"]
        xT_hi, xT_lo = (sb(f"xT_{n}", [P, KC, TOK], F32R) for n in ("hi", "lo"))
        w_hi, w_lo = (sb(f"w_{n}", [P, KC, D + SIDE], F32R) for n in ("hi", "lo"))
        b_hi, b_lo = (sb(f"b_{n}", [P, D], F32R) for n in ("hi", "lo"))
        staged = sb("staged", [P, KC, D + SIDE])
        b_staged = sb("b_staged", [P, D])
        small = sb("small", [P, sum(SMALL.values())])
        low = sb("low", [P, TILES, LORA])
        h = sb("h", [P, TILES, GATE_H])
        squares = sb("squares", [P, TILES, GATE_H])
        mean = sb("mean", [P, TILES])
        var = sb("var", [P, TILES])
        dev = sb("dev", [P, TILES])
        products = sb("products", [P, TILES, EXPERTS, GATE_H])
        gates = sb("gates", [P, TILES, EXPERTS])
        top = sb("top", [P, TILES, 8])
        top_index = sb("top_index", [P, TILES, 8], mybir.dt.uint32)
        top_at = sb("top_at", [P, TILES, 8])
        gap = sb("gap", [P, TILES])
        share = sb("share", [P, 2, TILES])
        total = sb("total", [P, TILES])
        chosen = sb("chosen", [P, 2, TILES, EXPERTS])
        count = sb("count", [P, 2, EXPERTS])
        allowed = sb("allowed", [P, 2, EXPERTS])
        weight = sb("weight", [P, 2, TILES, EXPERTS])
        ones = sb("ones", [P, P])
        low_T_hi, low_T_lo = (sb(f"low_T_{n}", [P, TOK], F32R) for n in ("hi", "lo"))

        names, at = {}, 0
        for name, width in SMALL.items():
            names[name] = small[:, at:at + width]
            at += width

        norm = t["norms"][2].attach(psum[6:8], xT_hi, xT_lo)
        last = t["norms"][3]
        ps_side, ps_y, ps_count, ps_low = psum[0:2], psum[0:6], psum[6], psum[6:8]
        weight_in, small_in_done, b_in = [sem(f"weight_in{k}") for k in range(KC)], sem("small_in"), sem("b_in")
        w_hi_done, w_lo_done = sem("w_hi_done"), sem("w_lo_done")
        side_ready, low_copied, h_copied = sem("side_ready"), sem("low_copied"), sem("h_copied")
        step_done, var_ready, dev_done, gap_ready, exp_done = (sem("step_done"), sem("var_ready"), sem("dev_done"),
                                                               sem("gap_ready"), sem("exp_done"))
        ones_set, count_ready, counted, weighted = sem("ones_set"), sem("count_ready"), sem("counted"), sem("weighted")
        low_turned, low_hi_done, low_lo_done = sem("low_turned"), sem("low_hi_done"), sem("low_lo_done")
        y_ready, y_added, stored = sem("y_ready"), sem("y_added"), sem("stored")

        block = ctx.enter_context(nc.Block())

        @block.sync
        def _(sp):
            for k in range(KC):
                sp.dma_start(staged[:, k, :], w_in[k]).then_inc(weight_in[k], 16)
            sp.dma_start(small[:, :], small_in).then_inc(small_in_done, 16)
            sp.dma_start(b_staged[:, :], lora_b_in).then_inc(b_in, 16)
            for tile in range(TILES):
                sp.wait_ge(last.normed, tile + 1)
                sp.dma_start(out[tile * P:(tile + 1) * P, :], rows[:, tile, :]).then_inc(stored, 16)
            sp.wait_ge(stored, 16 * TILES)

        @block.scalar
        def _(act):
            for k in range(KC):
                act.wait_ge(weight_in[k], 16)
                act.activation(w_hi[:, k, :], staged[:, k, :], ACT.Copy).then_inc(w_hi_done, 1)
            act.wait_ge(b_in, 16)
            act.activation(b_hi[:, :], b_staged[:, :], ACT.Copy).then_inc(w_hi_done, 1)
            norm.on_scalar(act)
            for tile in range(TILES):
                act.wait_ge(h_copied, tile + 1)
                act.activation(low[:, tile, :], ps_side[tile % 2][:, GATE_H:GATE_H + LORA],
                               ACT.Copy).then_inc(low_copied, 1)
            act.wait_ge(var_ready, 1)
            act.activation(dev[:, :], var[:, :], ACT.Sqrt, bias=norm.eps[:, 0:1],
                           scale=1.0 / GATE_H).then_inc(dev_done, 1)
            act.wait_ge(gap_ready, 1)
            act.activation(share[:, 1, :], gap[:, :], ACT.Exp).then_inc(exp_done, 1)
            for half in range(2):
                act.wait_ge(low_turned, half + 1)
                act.activation(low_T_hi[:, half * 512:(half + 1) * 512], ps_low[half][:, :], ACT.Copy).then_inc(low_hi_done, 1)
            act.wait_ge(y_added, TILES)
            last.on_scalar(act, transposed=False)

        @block.gpsimd
        def _(pool):
            pool.memset(ones[:, :], 1.0).then_inc(ones_set, 1)
            for k in range(KC):
                pool.wait_ge(w_hi_done, k + 1)
                pool.tensor_tensor(w_lo[:, k, :], staged[:, k, :], w_hi[:, k, :].bitcast(F32),
                                   ALU.subtract).then_inc(w_lo_done, 1)
            pool.wait_ge(w_hi_done, KC + 1)
            pool.tensor_tensor(b_lo[:, :], b_staged[:, :], b_hi[:, :].bitcast(F32), ALU.subtract).then_inc(w_lo_done, 1)

        @block.vector
        def _(dve):
            steps = [0]

            def step(instruction):
                steps[0] += 1
                instruction.then_inc(step_done, 1)
                dve.wait_ge(step_done, steps[0])

            def each_tile(name):
                return names[name].rearrange("p (a c) -> p a c", a=1).broadcast_to([P, TILES, SMALL[name]])

            def each_column(ap, n):
                return ap.rearrange("p (t a) -> p t a", a=1).broadcast_to([P, TILES, n])

            norm.on_vector(dve)
            for tile in range(TILES):
                dve.wait_ge(side_ready, tile + 1)
                dve.tensor_copy(h[:, tile, :], ps_side[tile % 2][:, 0:GATE_H]).then_inc(h_copied, 1)
            dve.wait_ge(small_in_done, 16)
            dve.wait_ge(h_copied, TILES)
            step(dve.tensor_tensor(h[:, :, :], h[:, :, :], each_tile("gb1"), ALU.add))
            step(dve.tensor_reduce(mean[:, :], h[:, :, :], mybir.AxisListType.X, ALU.add))
            step(dve.tensor_scalar(mean[:, :], mean[:, :], 1.0 / GATE_H, None, ALU.mult))
            step(dve.tensor_tensor(h[:, :, :], h[:, :, :], each_column(mean[:, :], GATE_H), ALU.subtract))
            step(dve.tensor_tensor(squares[:, :, :], h[:, :, :], h[:, :, :], ALU.mult))
            dve.tensor_reduce(var[:, :], squares[:, :, :], mybir.AxisListType.X, ALU.add).then_inc(var_ready, 1)
            dve.wait_ge(dev_done, 1)
            step(dve.reciprocal(dev[:, :], dev[:, :]))
            step(dve.tensor_tensor(h[:, :, :], h[:, :, :], each_column(dev[:, :], GATE_H), ALU.mult))
            step(dve.tensor_tensor(h[:, :, :], h[:, :, :], each_tile("gamma"), ALU.mult))
            step(dve.tensor_tensor(h[:, :, :], h[:, :, :], each_tile("beta"), ALU.add))
            step(dve.tensor_scalar(h[:, :, :], h[:, :, :], 0.0, None, ALU.max))
            for e in range(EXPERTS):
                row = names["gw2"][:, e * GATE_H:(e + 1) * GATE_H].rearrange("p (a c) -> p a c", a=1)
                mult = dve.tensor_tensor(products[:, :, e, :], h[:, :, :], row.broadcast_to([P, TILES, GATE_H]), ALU.mult)
            step(mult)
            step(dve.tensor_reduce(gates[:, :, :].rearrange("p t e -> p (t e)"),
                                   products[:, :, :, :].rearrange("p t e c -> p (t e) c"),
                                   mybir.AxisListType.X, ALU.add))
            step(dve.tensor_tensor(gates[:, :, :], gates[:, :, :], each_tile("gb2"), ALU.add))
            for tile in range(TILES):
                found = dve.max(top[:, tile, :], gates[:, tile, :])
            step(found)
            for tile in range(TILES):
                found = dve.max_index(top_index[:, tile, :], top[:, tile, :], gates[:, tile, :])
            step(found)
            step(dve.tensor_copy(top_at[:, :, :], top_index[:, :, :]))
            dve.tensor_tensor(gap[:, :], top[:, :, 1], top[:, :, 0], ALU.subtract).then_inc(gap_ready, 1)
            for n in range(2):
                found = dve.tensor_tensor(chosen[:, n, :, :], each_column(top_at[:, :, n], EXPERTS), each_tile("index"),
                                          ALU.is_equal)
            step(found)
            dve.tensor_reduce(count[:, :, :].rearrange("p n e -> p (n e)"),
                              chosen[:, :, :, :].rearrange("p n t e -> p n e t"), mybir.AxisListType.X,
                              ALU.add).then_inc(count_ready, 1)
            dve.wait_ge(exp_done, 1)
            step(dve.tensor_scalar(total[:, :], share[:, 1, :], 1.0, None, ALU.add))
            step(dve.reciprocal(share[:, 0, :], total[:, :]))
            step(dve.tensor_tensor(share[:, 1, :], share[:, 1, :], share[:, 0, :], ALU.mult))
            dve.wait_ge(counted, 1)
            step(dve.tensor_scalar(allowed[:, :, :].rearrange("p n e -> p (n e)"), ps_count[:, 0:2 * EXPERTS],
                                   float(CAPACITY), ALPHA, ALU.is_le, ALU.mult))
            for n in range(2):
                found = dve.tensor_tensor(weight[:, n, :, :], chosen[:, n, :, :], each_column(share[:, n, :], EXPERTS),
                                          ALU.mult)
            step(found)
            for n in range(2):
                found = dve.tensor_tensor(weight[:, n, :, :], weight[:, n, :, :],
                                          allowed[:, n, :].rearrange("p (a e) -> p a e", a=1).broadcast_to(
                                              [P, TILES, EXPERTS]), ALU.mult)
            step(found)
            step(dve.tensor_tensor(weight[:, 0, :, :], weight[:, 0, :, :], weight[:, 1, :, :], ALU.add))
            dve.wait_ge(low_copied, TILES)
            by_expert = low[:, :, :].rearrange("p t (e r) -> p (t e) r", r=RANK)
            dve.tensor_tensor(by_expert, by_expert,
                              weight[:, 0, :, :].rearrange("p t (e a) -> p (t e) a", a=1).broadcast_to(
                                  [P, TILES * EXPERTS, RANK]), ALU.mult).then_inc(weighted, 1)
            for half in range(2):
                dve.wait_ge(low_hi_done, half + 1)
                cols = slice(half * 512, (half + 1) * 512)
                dve.tensor_tensor(low_T_lo[:, cols], ps_low[half][:, :], low_T_hi[:, cols].bitcast(F32),
                                  ALU.subtract).then_inc(low_lo_done, 1)
            for tile in range(TILES):
                dve.wait_ge(y_ready, tile + 1)
                dve.tensor_tensor(rows[:, tile, :], ps_y[tile % AHEAD][:, :], rows[:, tile, :], ALU.add).then_inc(y_added, 1)
                dve.wait_ge(y_added, tile + 1)
                last.take(dve, tile)
            last.on_vector(dve, transposed=False)

        @block.tensor
        def _(pe):
            norm.on_tensor(pe, range(0, 4))
            pe.wait_ge(w_lo_done, KC)
            for tile in range(TILES):
                pe.wait_ge(norm.lo_done, tile + 1)
                if tile >= 2:
                    pe.wait_ge(low_copied, tile - 1)
                at = slice(tile * P, (tile + 1) * P)
                three(pe, ps_side[tile % 2][:, 0:SIDE], [(xT_hi[:, k, at], xT_lo[:, k, at], w_hi[:, k, D:], w_lo[:, k, D:])
                                                         for k in range(KC)], side_ready)
                if tile < 2:
                    norm.on_tensor(pe, range(4 + 2 * tile, 6 + 2 * tile))

            def dense(tile):
                at = slice(tile * P, (tile + 1) * P)
                for k in range(KC):
                    for a, b in ((xT_hi, w_hi), (xT_hi, w_lo), (xT_lo, w_hi)):
                        pe.matmul(ps_y[tile % AHEAD][:, :], a[:, k, at], b[:, k, 0:D],
                                  start=(k == 0 and a is xT_hi and b is w_hi), stop=False)

            def low_rank(tile):
                at = slice(tile * P, (tile + 1) * P)
                for a, b in ((low_T_hi, b_hi), (low_T_hi, b_lo), (low_T_lo, b_hi)):
                    mm = pe.matmul(ps_y[tile % AHEAD][:, :], a[:, at], b[:, :], start=False, stop=(a is low_T_lo))
                mm.then_inc(y_ready, 1)

            pe.wait_ge(low_copied, TILES)
            for tile in range(AHEAD):
                dense(tile)
            pe.wait_ge(ones_set, 1)
            pe.wait_ge(count_ready, 1)
            pe.matmul(ps_count[:, 0:2 * EXPERTS], ones[:, :], count[:, :, :].rearrange("p n e -> p (n e)"),
                      start=True, stop=True).then_inc(counted, 1)
            pe.wait_ge(weighted, 1)
            for half in range(2):
                for j in range(4):
                    mm = pe.transpose(ps_low[half][:, j * P:(j + 1) * P], low[:, 4 * half + j, :], ident[:, :])
                mm.then_inc(low_turned, 1)
            pe.wait_ge(w_lo_done, KC + 1)
            pe.wait_ge(low_lo_done, 2)
            for tile in range(AHEAD):
                low_rank(tile)
            for tile in range(AHEAD, TILES):
                pe.wait_ge(y_added, tile - AHEAD + 1)
                dense(tile)
                low_rank(tile)


def layout_ffn1(inputs):
    low = inputs["L1_ffn_lora_A"].transpose(1, 0, 2).reshape(D, LORA)
    pad = np.zeros((D, SIDE - GATE_H - LORA), np.float32)
    w = np.concatenate([inputs["L1_ffn_weight"].T, inputs["L1_ffn_gw1"].T, low, pad], 1)
    small = np.concatenate([inputs["L1_ffn_gb1"], inputs["L1_ffn_ln_gamma"], inputs["L1_ffn_ln_beta"],
                            inputs["L1_ffn_gw2"].reshape(-1), inputs["L1_ffn_gb2"],
                            np.arange(EXPERTS, dtype=np.float32)])
    return {"weights_f1": w.reshape(KC, P, D + SIDE), "lora_b": inputs["L1_ffn_lora_B"].reshape(LORA, D),
            "small_f1": np.ascontiguousarray(np.broadcast_to(small, (P, small.size)))}


def program(nc, a, out):
    with ExitStack() as ctx:
        rows = ctx.enter_context(nc.sbuf_tensor("rows", [P, TILES, D], F32))
        ident = ctx.enter_context(nc.sbuf_tensor("identity", [P, P], F32))
        psum = [ctx.enter_context(nc.psum_tensor(f"bank{n}", [P, 512], F32)) for n in range(8)]
        x_stage = rows[:, :, :].rearrange("p t d -> p (t d)").rearrange("p (k c) -> p k c", k=KC)
        norms = [Norm(ctx, nc, f"n{n}", rows, ident, transposed=n < 3) for n in range(4)]
        t = {"rows": rows, "ident": ident, "x_stage": x_stage, "norms": norms}
        attention0(nc, t, a["x_T"], a["weights0"], a["x_rows"], a["cos0"], a["sin0"], a["mask0"], a["ident"], psum)
        feed_forward0(nc, t, a["weights_f0"], psum)
        attention1(nc, t, a["weights_qkv1"], a["weights_o1"], a["cos1"], a["sin1"], a["mask1"], a["ones1"], psum)
        feed_forward1(nc, t, a["weights_f1"], a["lora_b"], a["small_f1"], out, psum)


def kernel(**inputs):
    from concourse import bacc
    from concourse.bass_utils import run_bass_kernel_spmd

    inputs = {k: np.asarray(v) for k, v in inputs.items()}
    arrays = {**layout0(inputs), **tables0(), **layout_ffn0(inputs), **layout1(inputs), **tables1(), **layout_ffn1(inputs)}
    arrays = {k: np.ascontiguousarray(v) for k, v in arrays.items()}
    nc = bacc.Bacc("TRN2", target_bir_lowering=False, num_devices=1)
    args = {k: nc.dram_tensor(k, v.shape, F32, kind="ExternalInput").ap() for k, v in arrays.items()}
    out = nc.dram_tensor("out", (TOK, D), F32, kind="ExternalOutput").ap()
    program(nc, args, out)
    result = run_bass_kernel_spmd(nc, [arrays], core_ids=[0])
    return result.results[0]["out"].reshape(BATCH, SEQ, D)
```
